# Optimizing a Trainium2 kernel written in Bass

```python
import numpy as np
import jax
import jax.numpy as jnp

def _softmax(x, axis=-1):
    return jax.nn.softmax(x, axis=axis)

def _gelu(x):
    return jax.nn.gelu(x, approximate=True)

def _silu(x):
    return jax.nn.silu(x)

def _sigmoid(x):
    return jax.nn.sigmoid(x)

def _layernorm(x, axis=-1, eps=1e-05):
    m = jnp.mean(x, axis=axis, keepdims=True)
    v = jnp.var(x, axis=axis, keepdims=True)
    return (x - m) / jnp.sqrt(v + eps)

def _scatter_add(tgt, idx, src, axis=0):
    return tgt.at[idx].add(src)

def _segment_sum(src, seg, n):
    return jax.ops.segment_sum(src, seg, n)
kernel_name = 'mk_vit_tower_d4_tok_img768_r4_b3973d'

def setup_inputs(seed: int=0):
    np.random.seed(seed)
    _w = jnp.asarray

    def _rec_inputs():
        import jax
        import jax.numpy as jnp
        _rk = jax.random.key(seed)
        x = -0.000348323 + 0.999952 * jax.random.normal(jax.random.fold_in(_rk, 1), (16, 3, 96, 96), jnp.float32)
        return x
    x = _rec_inputs()

    def _L0_tok_setup():
        import jax, jax.numpy as jnp
        import numpy as np
        PATCH = 16
        EMBED = 192
        IMG = 96
        CH = 3
        NP_ = (IMG // PATCH) ** 2
        key = jax.random.key(seed)
        k1, k2, k3 = jax.random.split(key, 3)
        x = jax.random.normal(k1, (32, CH, IMG, IMG), dtype=jnp.float32)
        in_feat = PATCH * PATCH * CH
        lim = 1.0 / np.sqrt(in_feat)
        W = jax.random.uniform(k2, (EMBED, in_feat), dtype=jnp.float32, minval=-lim, maxval=lim)
        b = jax.random.uniform(k3, (EMBED,), dtype=jnp.float32, minval=-lim, maxval=lim)
        pos = jnp.zeros((1, NP_, EMBED), dtype=jnp.float32)
        return {'x': x, 'W': W, 'b': b, 'pos': pos}
    _L0_tok_all = _L0_tok_setup()
    _L0_tok_in = {k: v for k, v in _L0_tok_all.items() if k in ('W', 'b', 'pos')}
    del _L0_tok_all

    def _L0_attn_setup():
        import jax, jax.numpy as jnp
        import numpy as np
        N_HEAD = 12

        def _rotate_half(x):
            x_even = x[..., ::2]
            x_odd = x[..., 1::2]
            return jnp.stack((-x_odd, x_even), axis=-1).reshape(x.shape)

        def _rope_tables(T, D, dtype):
            inv_freq = 1.0 / 10000.0 ** (jnp.arange(0, D, 2, dtype=jnp.float32) / D)
            freqs = jnp.arange(T, dtype=jnp.float32)[:, None] * inv_freq[None, :]
            cos = jnp.repeat(jnp.cos(freqs), 2, axis=-1).astype(dtype)
            sin = jnp.repeat(jnp.sin(freqs), 2, axis=-1).astype(dtype)
            return (cos, sin)
        key = jax.random.key(seed)
        ks = jax.random.split(key, 5)
        B, T, C = (8, 256, 192)
        return {'x': jax.random.normal(ks[0], (B, T, C), dtype=jnp.float32), 'W_attn': jax.random.normal(ks[1], (C, 3 * C), dtype=jnp.float32) * C ** (-0.5), 'b_attn': jax.random.normal(ks[2], (3 * C,), dtype=jnp.float32) * 0.02, 'W_proj': jax.random.normal(ks[3], (C, C), dtype=jnp.float32) * C ** (-0.5), 'b_proj': jax.random.normal(ks[4], (C,), dtype=jnp.float32) * 0.02}
    _L0_attn_all = _L0_attn_setup()
    _L0_attn_in = {k: v for k, v in _L0_attn_all.items() if k in ('W_attn', 'b_attn', 'W_proj', 'b_proj')}
    del _L0_attn_all

    def _L0_ffn_setup():
        import jax, jax.numpy as jnp
        import numpy as np
        S, B, DIM = (256, 4, 192)
        N_EXPERTS = 8
        HID = 512
        key = jax.random.key(seed)
        ks = jax.random.split(key, 6)
        scale = 0.02
        return {'hidden_states': jax.random.normal(ks[0], (S, B, DIM), dtype=jnp.float32), 'router_w': jax.random.normal(ks[1], (DIM, N_EXPERTS), dtype=jnp.float32) * scale, 'router_b': jnp.zeros((N_EXPERTS,), dtype=jnp.float32), 'w1': jax.random.normal(ks[2], (N_EXPERTS, DIM, HID), dtype=jnp.float32) * scale, 'w2': jax.random.normal(ks[3], (N_EXPERTS, DIM, HID), dtype=jnp.float32) * scale, 'w3': jax.random.normal(ks[4], (N_EXPERTS, HID, DIM), dtype=jnp.float32) * scale}
    _L0_ffn_all = _L0_ffn_setup()
    _L0_ffn_in = {k: v for k, v in _L0_ffn_all.items() if k in ('router_w', 'router_b', 'w1', 'w2', 'w3')}
    del _L0_ffn_all

    def _L1_attn_setup():
        import jax, jax.numpy as jnp
        import numpy as np
        B, N, C = (8, 768, 192)
        NUM_HEADS, NUM_DIL, KS = (12, 3, 3)
        key = jax.random.key(seed)
        k1, k2, k3 = jax.random.split(key, 3)
        x = jax.random.normal(k1, (B, N, C), dtype=jnp.float32)
        qkv_w = jax.random.normal(k2, (3 * C, C), dtype=jnp.float32) * 0.02
        proj_w = jax.random.normal(k3, (C, C), dtype=jnp.float32) * 0.02
        proj_b = jnp.zeros((C,), dtype=jnp.float32)
        return {'x': x, 'qkv_w': qkv_w, 'proj_w': proj_w, 'proj_b': proj_b}
    _L1_attn_all = _L1_attn_setup()
    _L1_attn_in = {k: v for k, v in _L1_attn_all.items() if k in ('qkv_w', 'proj_w', 'proj_b')}
    del _L1_attn_all

    def _L1_ffn_setup():
        import jax, jax.numpy as jnp
        import numpy as np
        DIM = 192
        H = 12
        HD = 64
        SHARED = 2
        ROUTED = 2
        E_ROUTED = H - SHARED
        LN_EPS = 1e-05

        def _layernorm(x, w, b):
            m = x.mean(-1, keepdims=True)
            v = ((x - m) ** 2).mean(-1, keepdims=True)
            return (x - m) * jax.lax.rsqrt(v + LN_EPS) * w + b
        key = jax.random.key(seed)
        ks = jax.random.split(key, 12)
        B, N = (4, 512)
        s = 0.02
        return {'x': jax.random.normal(ks[0], (B, N, DIM), jnp.float32), 'qkv_w': jax.random.normal(ks[1], (DIM, 3 * H * HD), jnp.float32) * s, 'qkv_b': jnp.zeros((3 * H * HD,), jnp.float32), 'q_norm_w': jnp.ones((HD,), jnp.float32), 'q_norm_b': jnp.zeros((HD,), jnp.float32), 'k_norm_w': jnp.ones((HD,), jnp.float32), 'k_norm_b': jnp.zeros((HD,), jnp.float32), 'wg_w': jax.random.normal(ks[2], (DIM, E_ROUTED), jnp.float32) * s, 'wg0_w': jax.random.normal(ks[3], (DIM, 2), jnp.float32) * s, 'wg1_w': jax.random.normal(ks[4], (DIM, SHARED), jnp.float32) * s, 'proj_w': jax.random.normal(ks[5], (H * HD, DIM), jnp.float32) * s, 'proj_b': jnp.zeros((DIM,), jnp.float32)}
    _L1_ffn_all = _L1_ffn_setup()
    _L1_ffn_in = {k: v for k, v in _L1_ffn_all.items() if k in ('qkv_w', 'qkv_b', 'q_norm_w', 'q_norm_b', 'k_norm_w', 'k_norm_b', 'wg_w', 'wg0_w', 'wg1_w', 'proj_w', 'proj_b')}
    del _L1_ffn_all

    def _L2_attn_setup():
        import jax, jax.numpy as jnp
        import numpy as np
        NPATCH = 64
        NWINDOW = 32
        HEADS = 12
        DIM_HEAD = 64
        LN_EPS = 1e-05
        key = jax.random.key(seed)
        k1, k2, k3 = jax.random.split(key, 3)
        b, n, dim = (2, NPATCH * NWINDOW, 192)
        inner = HEADS * DIM_HEAD
        return {'x': jax.random.normal(k1, (b, n, dim), dtype=jnp.float32), 'gamma': jnp.ones((dim,), jnp.float32), 'beta': jnp.zeros((dim,), jnp.float32), 'w_qkv': jax.random.normal(k2, (dim, 3 * inner), dtype=jnp.float32) * dim ** (-0.5), 'w_out': jax.random.normal(k3, (inner, dim), dtype=jnp.float32) * inner ** (-0.5), 'b_out': jnp.zeros((dim,), jnp.float32)}
    _L2_attn_all = _L2_attn_setup()
    _L2_attn_in = {k: v for k, v in _L2_attn_all.items() if k in ('gamma', 'beta', 'w_qkv', 'w_out', 'b_out')}
    del _L2_attn_all

    def _L2_ffn_setup():
        import jax, jax.numpy as jnp
        import numpy as np
        B, S, D = (2, 512, 192)
        E, K, F = (8, 2, 384)

        def _swiglu(xf, wg, wu, wd):
            return jax.nn.silu(xf @ wg.T) * (xf @ wu.T) @ wd.T
        key = jax.random.key(seed)
        ks = jax.random.split(key, 9)
        scale = 0.02
        x = jax.random.normal(ks[0], (B, S, D), dtype=jnp.float32)
        w_router = jax.random.normal(ks[1], (E, D), dtype=jnp.float32) * scale
        expert_bias = jnp.zeros((E,), dtype=jnp.float32)
        Wg = jax.random.normal(ks[2], (E, F, D), dtype=jnp.float32) * scale
        Wu = jax.random.normal(ks[3], (E, F, D), dtype=jnp.float32) * scale
        Wd = jax.random.normal(ks[4], (E, D, F), dtype=jnp.float32) * scale
        sg = jax.random.normal(ks[5], (F, D), dtype=jnp.float32) * scale
        su = jax.random.normal(ks[6], (F, D), dtype=jnp.float32) * scale
        sd = jax.random.normal(ks[7], (D, F), dtype=jnp.float32) * scale
        return {'x': x, 'w_router': w_router, 'expert_bias': expert_bias, 'Wg': Wg, 'Wu': Wu, 'Wd': Wd, 'sg': sg, 'su': su, 'sd': sd}
    _L2_ffn_all = _L2_ffn_setup()
    _L2_ffn_in = {k: v for k, v in _L2_ffn_all.items() if k in ('w_router', 'expert_bias', 'Wg', 'Wu', 'Wd', 'sg', 'su', 'sd')}
    del _L2_ffn_all

    def _L3_attn_setup():
        import jax, jax.numpy as jnp
        import numpy as np
        H = 192
        NH = 12
        HD = H // NH
        WINDOW = 64

        def _attn(hidden_states, Wq, bq, Wk, bk, Wv, bv, Wo, bo):
            B, S, _ = hidden_states.shape
            q = (hidden_states @ Wq + bq).reshape(B, S, NH, HD).transpose(0, 2, 1, 3)
            k = (hidden_states @ Wk + bk).reshape(B, S, NH, HD).transpose(0, 2, 1, 3)
            v = (hidden_states @ Wv + bv).reshape(B, S, NH, HD).transpose(0, 2, 1, 3)
            scores = jnp.einsum('bhqd,bhkd->bhqk', q, k) / jnp.sqrt(jnp.float32(HD))
            i = jnp.arange(S)[:, None]
            j = jnp.arange(S)[None, :]
            band = jnp.abs(i - j) <= WINDOW // 2
            scores = jnp.where(band[None, None, :, :], scores, jnp.float32(-1000000000.0))
            probs = jax.nn.softmax(scores, axis=-1)
            ctx = jnp.einsum('bhqk,bhkd->bhqd', probs, v)
            ctx = ctx.transpose(0, 2, 1, 3).reshape(B, S, H)
            return ctx @ Wo + bo
        key = jax.random.key(seed)
        ks = jax.random.split(key, 9)
        s = 0.02
        return {'hidden_states': jax.random.normal(ks[0], (4, 512, H), dtype=jnp.float32), 'Wq': jax.random.normal(ks[1], (H, H), dtype=jnp.float32) * s, 'bq': jnp.zeros((H,), dtype=jnp.float32), 'Wk': jax.random.normal(ks[2], (H, H), dtype=jnp.float32) * s, 'bk': jnp.zeros((H,), dtype=jnp.float32), 'Wv': jax.random.normal(ks[3], (H, H), dtype=jnp.float32) * s, 'bv': jnp.zeros((H,), dtype=jnp.float32), 'Wo': jax.random.normal(ks[4], (H, H), dtype=jnp.float32) * s, 'bo': jnp.zeros((H,), dtype=jnp.float32)}
    _L3_attn_all = _L3_attn_setup()
    _L3_attn_in = {k: v for k, v in _L3_attn_all.items() if k in ('Wq', 'bq', 'Wk', 'bk', 'Wv', 'bv', 'Wo', 'bo')}
    del _L3_attn_all

    def _L3_ffn_setup():
        import jax, jax.numpy as jnp
        import numpy as np
        N_EMBD = 192
        EXPERT_SIZES = [(8, 128), (8, 256)]
        TOP_K = 8
        NORM_TOPK_PROB = True
        EXPERT_WIDTHS = []
        for cnt, w in EXPERT_SIZES:
            EXPERT_WIDTHS += [w] * cnt
        EXPERT_OFFSETS = np.concatenate([[0], np.cumsum(EXPERT_WIDTHS)]).astype(np.int64)
        NUM_EXPERTS = len(EXPERT_WIDTHS)
        TOTAL_WIDTH = int(EXPERT_OFFSETS[-1])
        key = jax.random.key(seed)
        k1, k2, k3, k4 = jax.random.split(key, 4)
        x = jax.random.normal(k1, (1, 512, N_EMBD), dtype=jnp.float32)
        router_w = jax.random.normal(k2, (NUM_EXPERTS, N_EMBD), dtype=jnp.float32) * 0.02
        w1 = jnp.clip(jax.random.normal(k3, (N_EMBD, TOTAL_WIDTH), dtype=jnp.float32) * 0.02, -0.06, 0.06)
        w2 = jnp.clip(jax.random.normal(k4, (TOTAL_WIDTH, N_EMBD), dtype=jnp.float32) * 0.02, -0.06, 0.06)
        return {'x': x, 'router_w': router_w, 'w1': w1, 'w2': w2}
    _L3_ffn_all = _L3_ffn_setup()
    _L3_ffn_in = {k: v for k, v in _L3_ffn_all.items() if k in ('router_w', 'w1', 'w2')}
    del _L3_ffn_all
    return {'x': x, 'L0_tok_W': _L0_tok_in['W'], 'L0_tok_b': _L0_tok_in['b'], 'L0_tok_pos': _L0_tok_in['pos'], 'L0_attn_W_attn': _L0_attn_in['W_attn'], 'L0_attn_b_attn': _L0_attn_in['b_attn'], 'L0_attn_W_proj': _L0_attn_in['W_proj'], 'L0_attn_b_proj': _L0_attn_in['b_proj'], 'L0_ffn_router_w': _L0_ffn_in['router_w'], 'L0_ffn_router_b': _L0_ffn_in['router_b'], 'L0_ffn_w1': _L0_ffn_in['w1'], 'L0_ffn_w2': _L0_ffn_in['w2'], 'L0_ffn_w3': _L0_ffn_in['w3'], 'L1_attn_qkv_w': _L1_attn_in['qkv_w'], 'L1_attn_proj_w': _L1_attn_in['proj_w'], 'L1_attn_proj_b': _L1_attn_in['proj_b'], 'L1_ffn_qkv_w': _L1_ffn_in['qkv_w'], 'L1_ffn_qkv_b': _L1_ffn_in['qkv_b'], 'L1_ffn_q_norm_w': _L1_ffn_in['q_norm_w'], 'L1_ffn_q_norm_b': _L1_ffn_in['q_norm_b'], 'L1_ffn_k_norm_w': _L1_ffn_in['k_norm_w'], 'L1_ffn_k_norm_b': _L1_ffn_in['k_norm_b'], 'L1_ffn_wg_w': _L1_ffn_in['wg_w'], 'L1_ffn_wg0_w': _L1_ffn_in['wg0_w'], 'L1_ffn_wg1_w': _L1_ffn_in['wg1_w'], 'L1_ffn_proj_w': _L1_ffn_in['proj_w'], 'L1_ffn_proj_b': _L1_ffn_in['proj_b'], 'L2_attn_gamma': _L2_attn_in['gamma'], 'L2_attn_beta': _L2_attn_in['beta'], 'L2_attn_w_qkv': _L2_attn_in['w_qkv'], 'L2_attn_w_out': _L2_attn_in['w_out'], 'L2_attn_b_out': _L2_attn_in['b_out'], 'L2_ffn_w_router': _L2_ffn_in['w_router'], 'L2_ffn_expert_bias': _L2_ffn_in['expert_bias'], 'L2_ffn_Wg': _L2_ffn_in['Wg'], 'L2_ffn_Wu': _L2_ffn_in['Wu'], 'L2_ffn_Wd': _L2_ffn_in['Wd'], 'L2_ffn_sg': _L2_ffn_in['sg'], 'L2_ffn_su': _L2_ffn_in['su'], 'L2_ffn_sd': _L2_ffn_in['sd'], 'L3_attn_Wq': _L3_attn_in['Wq'], 'L3_attn_bq': _L3_attn_in['bq'], 'L3_attn_Wk': _L3_attn_in['Wk'], 'L3_attn_bk': _L3_attn_in['bk'], 'L3_attn_Wv': _L3_attn_in['Wv'], 'L3_attn_bv': _L3_attn_in['bv'], 'L3_attn_Wo': _L3_attn_in['Wo'], 'L3_attn_bo': _L3_attn_in['bo'], 'L3_ffn_router_w': _L3_ffn_in['router_w'], 'L3_ffn_w1': _L3_ffn_in['w1'], 'L3_ffn_w2': _L3_ffn_in['w2']}

def reference(x, L0_tok_W, L0_tok_b, L0_tok_pos, L0_attn_W_attn, L0_attn_b_attn, L0_attn_W_proj, L0_attn_b_proj, L0_ffn_router_w, L0_ffn_router_b, L0_ffn_w1, L0_ffn_w2, L0_ffn_w3, L1_attn_qkv_w, L1_attn_proj_w, L1_attn_proj_b, L1_ffn_qkv_w, L1_ffn_qkv_b, L1_ffn_q_norm_w, L1_ffn_q_norm_b, L1_ffn_k_norm_w, L1_ffn_k_norm_b, L1_ffn_wg_w, L1_ffn_wg0_w, L1_ffn_wg1_w, L1_ffn_proj_w, L1_ffn_proj_b, L2_attn_gamma, L2_attn_beta, L2_attn_w_qkv, L2_attn_w_out, L2_attn_b_out, L2_ffn_w_router, L2_ffn_expert_bias, L2_ffn_Wg, L2_ffn_Wu, L2_ffn_Wd, L2_ffn_sg, L2_ffn_su, L2_ffn_sd, L3_attn_Wq, L3_attn_bq, L3_attn_Wk, L3_attn_bk, L3_attn_Wv, L3_attn_bv, L3_attn_Wo, L3_attn_bo, L3_ffn_router_w, L3_ffn_w1, L3_ffn_w2):
    import jax
    import jax.numpy as jnp

    def _L0_tok_ref(x, W, b, pos):
        import jax, jax.numpy as jnp
        import numpy as np
        PATCH = 16
        EMBED = 192
        IMG = 96
        CH = 3
        NP_ = (IMG // PATCH) ** 2
        B, C, H, Wd = x.shape
        hp, wp = (H // PATCH, Wd // PATCH)
        patches = x.reshape(B, C, hp, PATCH, wp, PATCH)
        patches = patches.transpose(0, 2, 4, 1, 3, 5).reshape(B, hp * wp, C * PATCH * PATCH)
        out = jnp.einsum('bnf,ef->bne', patches, W) + b + pos
        return out

    def _L0_attn_ref(x, W_attn, b_attn, W_proj, b_proj):
        import jax, jax.numpy as jnp
        import numpy as np
        N_HEAD = 12

        def _rotate_half(x):
            x_even = x[..., ::2]
            x_odd = x[..., 1::2]
            return jnp.stack((-x_odd, x_even), axis=-1).reshape(x.shape)

        def _rope_tables(T, D, dtype):
            inv_freq = 1.0 / 10000.0 ** (jnp.arange(0, D, 2, dtype=jnp.float32) / D)
            freqs = jnp.arange(T, dtype=jnp.float32)[:, None] * inv_freq[None, :]
            cos = jnp.repeat(jnp.cos(freqs), 2, axis=-1).astype(dtype)
            sin = jnp.repeat(jnp.sin(freqs), 2, axis=-1).astype(dtype)
            return (cos, sin)
        B, T, C = x.shape
        H = N_HEAD
        D = C // H
        qkv = x @ W_attn + b_attn
        q, k, v = jnp.split(qkv, 3, axis=-1)
        q = q.reshape(B, T, H, D).transpose(0, 2, 1, 3)
        k = k.reshape(B, T, H, D).transpose(0, 2, 1, 3)
        v = v.reshape(B, T, H, D).transpose(0, 2, 1, 3)
        cos, sin = _rope_tables(T, D, x.dtype)
        q = q * cos + _rotate_half(q) * sin
        k = k * cos + _rotate_half(k) * sin
        att = jnp.einsum('bhqd,bhkd->bhqk', q, k) * D ** (-0.5)
        causal = jnp.tril(jnp.ones((T, T), dtype=bool))
        att = jnp.where(causal, att, -jnp.inf)
        att = jax.nn.softmax(att, axis=-1)
        y = jnp.einsum('bhqk,bhkd->bhqd', att, v)
        y = y.transpose(0, 2, 1, 3).reshape(B, T, C)
        return y @ W_proj + b_proj

    def _L0_ffn_ref(hidden_states, router_w, router_b, w1, w2, w3):
        import jax, jax.numpy as jnp
        import numpy as np
        S, B, DIM = (256, 4, 192)
        N_EXPERTS = 8
        HID = 512
        s, b, h = hidden_states.shape
        route = jax.nn.softmax(hidden_states @ router_w + router_b, axis=2)
        max_prob = jnp.max(route, axis=2).reshape(-1, 1)
        max_ind = jnp.argmax(route, axis=2).reshape(-1)
        x = hidden_states.reshape(-1, h)
        out = jnp.zeros_like(x)
        for e in range(N_EXPERTS):
            mask = (max_ind == e)[:, None]
            xe = jnp.where(mask, x, 0.0)
            oe = jax.nn.silu(xe @ w1[e]) * (xe @ w2[e]) @ w3[e]
            out = out + jnp.where(mask, oe, 0.0)
        out = out.astype(jnp.bfloat16) * max_prob
        return out.reshape(s, b, h)

    def _L1_attn_ref(x, qkv_w, proj_w, proj_b):
        import jax, jax.numpy as jnp
        import numpy as np
        B, N, C = (8, 768, 192)
        NUM_HEADS, NUM_DIL, KS = (12, 3, 3)
        Bx, Nx, Cx = x.shape
        nd, ks, heads = (NUM_DIL, KS, NUM_HEADS)
        hd = Cx // heads
        d = Cx // nd
        h = heads // nd
        nb = Nx // ks
        scale = hd ** (-0.5)
        qkv = (x @ qkv_w.T).reshape(Bx, Nx, 3, nd, d)
        qkv = jnp.transpose(qkv, (3, 2, 0, 4, 1))
        q, k, v = (qkv[:, 0], qkv[:, 1], qkv[:, 2])

        def split_heads(t):
            t = t.reshape(nd, Bx, h, hd, ks, nb)
            return jnp.transpose(t, (0, 1, 2, 5, 4, 3))
        qh = split_heads(q)
        kh = split_heads(k)
        vh = split_heads(v)
        attn = jnp.einsum('nbhwqd,nbhwkd->nbhwqk', qh, kh) * scale
        attn = jax.nn.softmax(attn, axis=-1)
        out = jnp.einsum('nbhwqk,nbhwkd->nbhwqd', attn, vh)
        out = jnp.transpose(out, (0, 1, 3, 2, 4, 5)).reshape(nd, Bx, Nx, d)
        out = jnp.transpose(out, (1, 2, 0, 3)).reshape(Bx, Nx, Cx)
        return out @ proj_w.T + proj_b

    def _L1_ffn_ref(x, qkv_w, qkv_b, q_norm_w, q_norm_b, k_norm_w, k_norm_b, wg_w, wg0_w, wg1_w, proj_w, proj_b):
        import jax, jax.numpy as jnp
        import numpy as np
        DIM = 192
        H = 12
        HD = 64
        SHARED = 2
        ROUTED = 2
        E_ROUTED = H - SHARED
        LN_EPS = 1e-05

        def _layernorm(x, w, b):
            m = x.mean(-1, keepdims=True)
            v = ((x - m) ** 2).mean(-1, keepdims=True)
            return (x - m) * jax.lax.rsqrt(v + LN_EPS) * w + b
        B, N, C = x.shape
        scale = HD ** (-0.5)
        gates = jax.nn.softmax(x @ wg_w, axis=-1)
        _, idx = jax.lax.top_k(gates, ROUTED)
        mask = jax.nn.one_hot(idx, E_ROUTED, dtype=gates.dtype).sum(-2)
        rg = gates * mask
        denom = jnp.clip(rg.sum(-1, keepdims=True), jnp.finfo(rg.dtype).eps, None)
        routed_gates = rg / denom * ROUTED
        qkv = (x @ qkv_w + qkv_b).reshape(B, N, 3, H, HD)
        qkv = jnp.transpose(qkv, (2, 0, 3, 1, 4))
        q, k, v = (qkv[0], qkv[1], qkv[2])
        q = _layernorm(q, q_norm_w, q_norm_b)
        k = _layernorm(k, k_norm_w, k_norm_b)
        attn = jax.nn.softmax(jnp.einsum('bhqd,bhkd->bhqk', q * scale, k), axis=-1)
        o = jnp.einsum('bhqk,bhkd->bhqd', attn, v)
        o = jnp.transpose(o, (0, 2, 1, 3))
        shared_gates = jax.nn.softmax(x @ wg1_w, axis=-1) * SHARED
        w0 = jax.nn.softmax(x @ wg0_w, axis=-1) * 2.0
        shared_gates = w0[..., 0:1] * shared_gates
        routed_gates = w0[..., 1:2] * routed_gates
        masked_gates = jnp.concatenate([shared_gates, routed_gates], axis=-1)
        o = (masked_gates[..., None] * o).reshape(B, N, H * HD)
        return o @ proj_w + proj_b

    def _L2_attn_ref(x, gamma, beta, w_qkv, w_out, b_out):
        import jax, jax.numpy as jnp
        import numpy as np
        NPATCH = 64
        NWINDOW = 32
        HEADS = 12
        DIM_HEAD = 64
        LN_EPS = 1e-05
        b, n, dim = x.shape
        mu = jnp.mean(x, axis=-1, keepdims=True)
        var = jnp.mean(jnp.square(x - mu), axis=-1, keepdims=True)
        xn = (x - mu) * jax.lax.rsqrt(var + LN_EPS) * gamma + beta
        qkv = xn @ w_qkv
        q, k, v = jnp.split(qkv, 3, axis=-1)

        def to_heads(t):
            return t.reshape(b, n, HEADS, DIM_HEAD).transpose(0, 2, 1, 3)
        q, k, v = (to_heads(q), to_heads(k), to_heads(v))
        scale = DIM_HEAD ** (-0.5)
        dots = jnp.einsum('bhid,bhjd->bhij', q, k) * scale
        blk = jnp.arange(n) // NPATCH
        mask = blk[:, None] >= blk[None, :]
        dots = jnp.where(mask[None, None], dots, -jnp.inf)
        attn = jax.nn.softmax(dots, axis=-1)
        out = jnp.einsum('bhij,bhjd->bhid', attn, v)
        out = out.transpose(0, 2, 1, 3).reshape(b, n, HEADS * DIM_HEAD)
        return out @ w_out + b_out

    def _L2_ffn_ref(x, w_router, expert_bias, Wg, Wu, Wd, sg, su, sd):
        import jax, jax.numpy as jnp
        import numpy as np
        B, S, D = (2, 512, 192)
        E, K, F = (8, 2, 384)

        def _swiglu(xf, wg, wu, wd):
            return jax.nn.silu(xf @ wg.T) * (xf @ wu.T) @ wd.T
        b, s, d = x.shape
        xf = x.reshape(-1, d)
        T = xf.shape[0]
        e = w_router.shape[0]
        logits = xf @ w_router.T
        scores = jax.nn.softmax(logits, axis=-1)
        selection = scores + expert_bias[None, :]
        _, top_idx = jax.lax.top_k(selection, K)
        top_s = jnp.take_along_axis(scores, top_idx, axis=-1)
        top_s = top_s / (jnp.sum(top_s, axis=-1, keepdims=True) + 1e-09)
        comb = jnp.zeros((T, e), dtype=x.dtype).at[jnp.arange(T)[:, None], top_idx].add(top_s)

        def body(acc, p):
            wg, wu, wd, c = p
            return (acc + c[:, None] * _swiglu(xf, wg, wu, wd), None)
        routed, _ = jax.lax.scan(body, jnp.zeros_like(xf), (Wg, Wu, Wd, comb.T))
        out = routed + _swiglu(xf, sg, su, sd)
        return out.reshape(b, s, d)

    def _L3_attn_ref(hidden_states, Wq, bq, Wk, bk, Wv, bv, Wo, bo):
        import jax, jax.numpy as jnp
        import numpy as np
        H = 192
        NH = 12
        HD = H // NH
        WINDOW = 64

        def _attn(hidden_states, Wq, bq, Wk, bk, Wv, bv, Wo, bo):
            B, S, _ = hidden_states.shape
            q = (hidden_states @ Wq + bq).reshape(B, S, NH, HD).transpose(0, 2, 1, 3)
            k = (hidden_states @ Wk + bk).reshape(B, S, NH, HD).transpose(0, 2, 1, 3)
            v = (hidden_states @ Wv + bv).reshape(B, S, NH, HD).transpose(0, 2, 1, 3)
            scores = jnp.einsum('bhqd,bhkd->bhqk', q, k) / jnp.sqrt(jnp.float32(HD))
            i = jnp.arange(S)[:, None]
            j = jnp.arange(S)[None, :]
            band = jnp.abs(i - j) <= WINDOW // 2
            scores = jnp.where(band[None, None, :, :], scores, jnp.float32(-1000000000.0))
            probs = jax.nn.softmax(scores, axis=-1)
            ctx = jnp.einsum('bhqk,bhkd->bhqd', probs, v)
            ctx = ctx.transpose(0, 2, 1, 3).reshape(B, S, H)
            return ctx @ Wo + bo
        return _attn(hidden_states, Wq, bq, Wk, bk, Wv, bv, Wo, bo)

    def _L3_ffn_ref(x, router_w, w1, w2):
        import jax, jax.numpy as jnp
        import numpy as np
        N_EMBD = 192
        EXPERT_SIZES = [(8, 128), (8, 256)]
        TOP_K = 8
        NORM_TOPK_PROB = True
        EXPERT_WIDTHS = []
        for cnt, w in EXPERT_SIZES:
            EXPERT_WIDTHS += [w] * cnt
        EXPERT_OFFSETS = np.concatenate([[0], np.cumsum(EXPERT_WIDTHS)]).astype(np.int64)
        NUM_EXPERTS = len(EXPERT_WIDTHS)
        TOTAL_WIDTH = int(EXPERT_OFFSETS[-1])
        B, S, D = x.shape
        xt = x.reshape(-1, D)
        T = xt.shape[0]
        logits = jnp.einsum('td,ed->te', xt, router_w)
        probs = jax.nn.softmax(logits, axis=-1)
        topk_w, topk_idx = jax.lax.top_k(probs, TOP_K)
        if NORM_TOPK_PROB:
            topk_w = topk_w / jnp.sum(topk_w, axis=-1, keepdims=True)
        comb = jnp.zeros((T, NUM_EXPERTS), dtype=xt.dtype)
        comb = comb.at[jnp.arange(T)[:, None], topk_idx].add(topk_w)
        out = jnp.zeros_like(xt)
        for e in range(NUM_EXPERTS):
            off = int(EXPERT_OFFSETS[e])
            wd = EXPERT_WIDTHS[e]
            h = jax.nn.gelu(xt @ w1[:, off:off + wd])
            out = out + comb[:, e:e + 1] * (h @ w2[off:off + wd, :])
        return out.reshape(B, S, D)
    h = _L0_tok_ref(x, L0_tok_W, L0_tok_b, L0_tok_pos)
    h = h + _L0_attn_ref(_layernorm(h, axis=-1), L0_attn_W_attn, L0_attn_b_attn, L0_attn_W_proj, L0_attn_b_proj)
    h = h + _L0_ffn_ref(_layernorm(h, axis=-1), L0_ffn_router_w, L0_ffn_router_b, L0_ffn_w1, L0_ffn_w2, L0_ffn_w3)
    h = h + _L1_attn_ref(_layernorm(h, axis=-1), L1_attn_qkv_w, L1_attn_proj_w, L1_attn_proj_b)
    h = h + _L1_ffn_ref(_layernorm(h, axis=-1), L1_ffn_qkv_w, L1_ffn_qkv_b, L1_ffn_q_norm_w, L1_ffn_q_norm_b, L1_ffn_k_norm_w, L1_ffn_k_norm_b, L1_ffn_wg_w, L1_ffn_wg0_w, L1_ffn_wg1_w, L1_ffn_proj_w, L1_ffn_proj_b)
    h = h + _L2_attn_ref(_layernorm(h, axis=-1), L2_attn_gamma, L2_attn_beta, L2_attn_w_qkv, L2_attn_w_out, L2_attn_b_out)
    h = h + _L2_ffn_ref(_layernorm(h, axis=-1), L2_ffn_w_router, L2_ffn_expert_bias, L2_ffn_Wg, L2_ffn_Wu, L2_ffn_Wd, L2_ffn_sg, L2_ffn_su, L2_ffn_sd)
    h = h + _L3_attn_ref(_layernorm(h, axis=-1), L3_attn_Wq, L3_attn_bq, L3_attn_Wk, L3_attn_bk, L3_attn_Wv, L3_attn_bv, L3_attn_Wo, L3_attn_bo)
    h = h + _L3_ffn_ref(_layernorm(h, axis=-1), L3_ffn_router_w, L3_ffn_w1, L3_ffn_w2)
    return h

_drawn_inputs = setup_inputs


def setup_inputs(seed=0):
    import zlib

    import numpy as np

    out = dict(_drawn_inputs(seed))
    spreads = {'L0_tok_pos': (0.0, 0.1),
     'L0_ffn_router_b': (0.0, 0.8),
     'L1_attn_proj_b': (0.0, 0.414),
     'L1_ffn_qkv_b': (0.0, 0.451),
     'L1_ffn_q_norm_w': (1.0, 0.6),
     'L1_ffn_q_norm_b': (0.0, 2.0),
     'L1_ffn_k_norm_w': (1.0, 0.6),
     'L1_ffn_k_norm_b': (0.0, 2.0),
     'L1_ffn_proj_b': (0.0, 0.365),
     'L2_attn_gamma': (1.0, 0.6),
     'L2_attn_beta': (0.0, 0.305),
     'L2_attn_b_out': (0.0, 0.298),
     'L2_ffn_expert_bias': (0.0, 0.709),
     'L3_attn_bq': (0.0, 2.0),
     'L3_attn_bk': (0.0, 2.0),
     'L3_attn_bv': (0.0, 0.8),
     'L3_attn_bo': (0.0, 0.658)}
    factors = {'L0_ffn_router_w': 8.0,
     'L0_ffn_w1': 8.0,
     'L0_ffn_w2': 8.0,
     'L0_ffn_w3': 8.0,
     'L1_ffn_wg0_w': 18.035,
     'L1_ffn_wg1_w': 22.822,
     'L2_ffn_w_router': 6.247,
     'L2_ffn_Wg': 4.555,
     'L2_ffn_Wu': 4.514,
     'L2_ffn_Wd': 4.487,
     'L2_ffn_sg': 3.274,
     'L2_ffn_su': 3.231,
     'L2_ffn_sd': 3.208,
     'L3_attn_Wq': 63.059,
     'L3_attn_Wk': 61.436,
     'L3_ffn_router_w': 5.02,
     'L3_ffn_w1': 3.542,
     'L3_ffn_w2': 3.481,
     'L1_attn_qkv_w': 5.198,
     'L1_attn_proj_w': 7.987,
     'L1_ffn_qkv_w': 4.212,
     'L1_ffn_wg_w': 3.914,
     'L3_attn_Wv': 7.523,
     'L3_attn_Wo': 6.887}
    for name, (base, spread) in spreads.items():
        noise = np.random.default_rng([zlib.crc32(name.encode()), seed]).standard_normal(out[name].shape)
        drawn = base * np.exp(spread * noise) if base else spread * noise
        out[name] = jnp.asarray(drawn.astype(out[name].dtype))
    for name, factor in factors.items():
        out[name] = (out[name] * factor).astype(out[name].dtype)
    return out
```

```python
from contextlib import ExitStack

import numpy as np
import concourse.bass as bass
from concourse import mybir

ALU = mybir.AluOpType
ACT = mybir.ActivationFunctionType
F32 = mybir.dt.float32
BF16 = mybir.dt.bfloat16
X = mybir.AxisListType.X

B, N, C = 16, 36, 192
NC_ = 2
CR = (128, C - 128)
CB = (CR[0], CR[1] + 1)
TP = 96
NG = B * N // TP
TAU = 3
HB = 8
HN = HB * N
NB = N // TAU
TOKF = 768 // 128
VW = 64
EPS = 1e-5
FEPS = float(np.finfo(np.float32).eps)


class Attn:

    def __init__(self, name, heads_of_group, dim, slot, stride, token_major, rope=False, qk_norm=False,
                 mask=None, gated=False, double_ln=False):
        self.name, self.hg, self.dim, self.slot, self.stride = name, heads_of_group, dim, slot, stride
        self.ng = 12 // heads_of_group
        self.fq = heads_of_group * dim
        self.fv = heads_of_group * slot
        self.rows = heads_of_group * stride
        self.tm, self.rope, self.qk_norm = token_major, rope, qk_norm
        self.mask, self.gated, self.double_ln = mask, gated, double_ln
        self.width = 2 * self.fq + self.fv
        self.units = 2 * self.ng
        self.scale = float(dim) ** -0.5


class Moe:

    def __init__(self, name, slots, chunks, up, act, experts, topk, owner):
        self.name, self.slots, self.chunks, self.up, self.act = name, slots, chunks, up, act
        self.experts, self.topk, self.owner = experts, topk, owner
        self.units = slots * chunks * 2
        self.width = chunks * 128 * (2 if up else 1)

    def expert(self, s, m):
        return self.owner[s * self.chunks + m]

    def first(self, s, m):
        n = s * self.chunks + m
        return n == 0 or self.owner[n - 1] != self.owner[n]

    def last(self, s, m):
        n = s * self.chunks + m
        return n == len(self.owner) - 1 or self.owner[n + 1] != self.owner[n]


A0 = Attn("l0a", 3, 16, 32, N, True, rope=True, mask="causal")
A1 = Attn("l1f", 2, 64, 64, VW, True, qk_norm=True, gated=True)
A2 = Attn("l2a", 2, 64, 64, N, False, double_ln=True)
A3 = Attn("l3a", 3, 16, 32, N, False, mask="band")
ATTNS = [A0, A1, A2, A3]
M0 = Moe("l0f", 8, 4, True, ACT.Silu, 8, 1, [s for s in range(8) for _ in range(4)])
M2 = Moe("l2f", 9, 3, True, ACT.Silu, 8, 2, [s for s in range(9) for _ in range(3)])
M3 = Moe("l3f", 6, 4, False, ACT.Gelu_apprx_tanh, 16, 8,
         list(range(8)) + [8 + e for e in range(8) for _ in range(2)])
MOES = [M0, M2, M3]
UNIT0 = {a.name: sum(x.units for x in ATTNS[:i]) for i, a in enumerate(ATTNS)}
TM0 = {A0.name: 0, A1.name: A0.units}
MU0 = {m.name: sum(x.units for x in MOES[:i]) for i, m in enumerate(MOES)}
MS0 = {m.name: sum(x.slots for x in MOES[:i]) for i, m in enumerate(MOES)}
SG0 = {M0.name: 0, M2.name: M0.units}
MD0 = {}
_d = 0
for _m in MOES:
    MD0[_m.name] = _d
    _d += 2 * len(set(_m.owner))
PT_LAG = 3
RING = 2
WG_ = 1024
GRP = 14
STAGES = [("attn", A0), ("moe", M0), ("grid", None), ("attn", A1), ("attn", A2), ("moe", M2), ("attn", A3), ("moe", M3)]
LN_PASS = [0, 1, 2, 3, 5, 6, 7, 8]
ROUTER = {"l0f": (0, 8), "l2f": (2, 8), "l3f": (3, 16)}
XV_N = {"l0a": 0, "l1f": 1, "l2a": 2, "l3a": 3}
CONSTS = ["ident", "mh", "rope", "masks", "posb", "bias", "gb", "qn", "ebias", "wr0", "wr1", "wr2", "wr3"]
STOP = 99


def owner_index(m, s, ch):
    return m.owner[s * m.chunks + ch]


def units_before(slot):
    n = 0
    for m in MOES:
        k = min(slot, m.slots)
        n += k * m.chunks * 2
        slot -= k
    return n


def bass_vit_tower(nc, t, out):
    with ExitStack() as ctx:
        def sb(name, shape, dt=F32):
            return ctx.enter_context(nc.sbuf_tensor(name, shape, dt))

        def sem(name):
            return ctx.enter_context(nc.semaphore(name))

        PS = ctx.enter_context(nc.psum_tensor("PS", [128, 8, 512], F32))
        PSF = PS[:, :, :].rearrange("p b n -> p (b n)")

        OB = PS[:, 6:8, 0:HN // 2]

        def YB(g):
            return PS[0:TP, (5, 5, 6, 7, 7, 4)[g], (g % TAU % 2) * C:(g % TAU % 2 + 1) * C]

        H = sb("H", [TP, NG, C])
        XN = sb("XN", [TP, NG, 256])
        XT = sb("XT", [128, NC_, B * N])
        ACC = sb("ACC", [TP, NG, C])
        BIG = sb("BIG", [128, TOKF * B * N])
        OT = sb("OT", [128, 6 * B * N])
        WTOK = OT[:, 0:TOKF * C].rearrange("p (k f) -> p k f", k=TOKF)
        MIX = sb("MIX", [128, NC_ * B * VW])
        XV = MIX[:, :].rearrange("k (c n) -> k c n", c=NC_)
        st = sb("st", [TP, NG, 6])
        mv = sb("mv", [TP, NG, 2])
        var = sb("var", [TP, NG])
        rstd = sb("rstd", [TP, NG])
        cst = sb("cst", [128, 128])
        mh = sb("mh", [128, 6])
        nhalf = sb("nhalf", [128, 16])
        tri = sb("tri", [128, 16, 16])
        rope = sb("rope", [TP, 2, TAU, 96])
        masks = sb("masks", [108, 2, N])
        posb = sb("posb", [TP, TAU, C])
        bias = sb("bias", [TP, 6, C])
        gb = sb("gb", [128, 4])
        qn = sb("qn", [128, 4])
        qs = sb("qs", [128, 4])
        ebias = sb("ebias", [TP, 8])
        wr = [sb(f"wr{i}", [128, NC_, e]) for i, e in enumerate((8, GRP, 8, 16))]
        wqkv = {a.name: sb("wqkv_" + a.name, [128, NC_, a.ng * a.width]) for a in (A0, A1)}
        wp = {a.name: sb("wp_" + a.name, [a.fv, a.ng, C]) for a in (A0, A1, A2)}
        wqkv["l3a"], wp["l3a"] = wqkv["l0a"], wp["l0a"]
        wqkv["l2a"] = wqkv["l1f"]
        wg = sb("wg", [128, NC_, 3 * C])
        wgp = sb("wgp", [64, 3, C])
        RG = [sb(f"RG{r}", [128, NC_, WG_]) for r in range(RING)]
        RD = [sb(f"RD{r}", [128, 4 * C]) for r in range(RING)]
        ACCB = MIX[0:TP, 4 * HN:4 * HN + NG * C // 2].bitcast(BF16).rearrange("p (g f) -> p g f", g=NG)
        SG = [MIX[:, r * HN:(r + 1) * HN] for r in range(2)]
        AF = [MIX[:, r * HN:(r + 1) * HN] for r in range(2, 4)]
        T2 = ACC[:, 0:4, :].rearrange("p g f -> p (g f)")
        sm = sb("sm", [128, 4, HB])
        ssq = sb("ssq", [TP, 3, 12])
        cw = sb("cw", [128, NC_ * 24])
        R1, R2 = BIG[:, 0:1600], BIG[:, 1600:3200]
        rl = sb("rl", [128, 4, 16 * 16])
        rs = sb("rs", [128, 8, 16])
        GH = sb("GH", [128, 6, 16])
        comb = [sb(f"comb{i}", [TP, NG, e]) for i, e in enumerate((8, 9, 16))]
        maxp = sb("maxp", [TP, NG])
        sg1 = sb("sg1", [TP, 3, 216])

        with ExitStack() as place:
            def sb1(name, shape, dt=F32):
                return place.enter_context(nc.sbuf_tensor(name, shape, dt))
            QB = [sb1(f"QB{r}", [128, HB, 128]) for r in range(2)]
            KS = [sb1(f"KS{r}", [128, HN]) for r in range(2)]
            VS = [sb1(f"VS{r}", [128, 512]) for r in range(5)]
            ES = [sb1(f"ES{r}", [128, HN]) for r in range(2)]
            PN = [sb1(f"PN{r}", [128, HB, VW]) for r in range(2)]
            PT = [sb1(f"PT{r}", [128, 512]) for r in range(2)]
            TX = [sb1(f"TX{r}", [TP, TAU * 256]) for r in range(2)]
        F32R = mybir.dt.float32r
        XH = sb("XH", [128, B * N], F32R)
        XL = sb("XL", [128, B * N], F32R)
        X1 = sb("X1", [128, B * N], F32R)
        X1F = sb("X1F", [128, B * N])
        X1T = sb("X1T", [128, B * N], F32R)
        WH = [sb(f"WH{r}", [128, NC_, WG_], F32R) for r in range(RING)]
        WL = [sb(f"WL{r}", [128, NC_, WG_], F32R) for r in range(RING)]
        DH = [sb(f"DH{r}", [128, 4 * C], F32R) for r in range(RING)]
        DL = [sb(f"DL{r}", [128, 4 * C], F32R) for r in range(RING)]
        AH = [sb(f"AH{r}", [128, HN], F32R) for r in range(3)]
        AL = [sb(f"AL{r}", [128, HN], F32R) for r in range(3)]

        S = {n: sem(n) for n in (
            "in_patch", "in_const", "wslot0", "wslot1", "out_written",
            "setup_pool", "setup_dve", "patch_summed", "h_ready",
            "ln_stats", "ln_rstd", "ln_normed", "ln_turned", "xt0_ready", "xt1_ready", "xv_ready", "x_split",
            "tm_ready", "tm_square", "tm_sum", "tm_rstd", "tm_done", "qk_ready", "q_sb", "k_sb", "v_ready", "v_sb",
            "s_ready", "s_taken", "e_ready", "p_sb", "pt_ready", "pt_sb", "o_ready", "o_sb", "y_ready",
            "bias_added",
            "logits", "r_shift", "r_exp", "r_done",
            "g_ready", "sg_ready", "a_ready", "ah_hi", "ah_lo", "w3_done", "drained", "w_hi", "w_lo", "w_lo1", "ring_pads",
            "grid_ready", "grid_sb", "grid_s", "grid_e", "grid_o", "grid_turned", "grid_osb",
            "dve_step", "pool_step", "act_step",
        )}
        in_att = {n: sem("in_att_" + n) for n in ("l0a", "grid", "l1f", "l2a", "l3a")}
        wslot = [S["wslot0"], S["wslot1"]]

        GQ = BIG[0:TP, :]
        GO = XN[:, :, :].rearrange("p g f -> p (g f)")[:, 0:2 * 3 * C]
        GT = OT[0:64, 9 * C:18 * C]
        consts = [(dst[tuple(slice(None) for _ in dst.shape)], t[n]) for dst, n in zip(
            [cst, mh, rope, masks, posb, bias, gb, qn, ebias, *wr], CONSTS)]

        def xt_copy(copy, c, j, double, grid, moe):
            k, cols = CR[c], slice(HN * j, HN * (j + 1))
            if grid:
                for tau in range(TAU):
                    o = XT[0:k, c, cols].rearrange("k (s b m t) -> k t b s m", s=3, b=HB, t=TAU)[:, tau]
                    i = PS[0:k, 4 + 2 * j + c, tau * TP:(tau + 1) * TP].rearrange("k (b s m) -> k b s m", b=HB, s=3)
                    last = copy(o, i, None)
                return last
            o = XT[:, c, cols].rearrange("k (p t) -> k t p", t=TAU)
            i = PS[:, 4 + 2 * j + c, 0:HN].rearrange("k (t p) -> k t p", t=TAU)
            if moe and c == 1:
                copy(X1F[k:2 * k, cols].rearrange("k (p t) -> k t p", t=TAU), i[k:2 * k], None)
            return copy(o[0:k], i[0:k], c if double else None)

        block = ctx.enter_context(nc.Block())

        def tile(ap2, j, tau, width=TP):
            return ap2[:, HN * j + tau:HN * (j + 1):TAU]

        @block.sync
        def _(sp):
            sp.dma_start(WTOK[:, :, :], t["wtok"]).then_inc(S["in_patch"], 16)
            for k in range(TOKF):
                sp.dma_start(BIG[:, k * B * N:(k + 1) * B * N], t["patch"][:, k, :]).then_inc(S["in_patch"], 16)
            for dst, src in consts:
                sp.dma_start(dst, src).then_inc(S["in_const"], 16)

            def qkv(a):
                for c in range(NC_):
                    sp.dma_start(wqkv[a.name][0:CB[c], c, :], t[f"wqkv_{a.name}_{c}"]).then_inc(in_att[a.name], 16)

            def proj(a):
                sp.dma_start(wp[a.name][:, :, :], t["wp_" + a.name]).then_inc(in_att[a.name], 16)

            def slots(m, lo, hi):
                w = m.width
                for s in range(lo, hi):
                    n = MS0[m.name] + s
                    if n >= RING:
                        sp.wait_ge(S["w_hi"], n - 1)
                        sp.wait_ge(S["w_lo"], n - 1)
                        sp.wait_ge(S["w_lo1"], n - 1)
                    r, arrived = n % RING, wslot[n % RING]
                    sp.dma_start(RG[r][:, 0, 0:w], t["gu_" + m.name][s, 0:128]).then_inc(arrived, 16)
                    for half in (0, 64):
                        sp.dma_start(RG[r][half:half + 64, 1, 0:w], t["gu_" + m.name][s, 128:C]).then_inc(arrived, 16)
                    sp.dma_start(RD[r][:, 0:m.chunks * C], t["wd_" + m.name][s]).then_inc(arrived, 16)

            qkv(A0)
            proj(A0)
            slots(M0, 0, RING)
            for c in range(NC_):
                sp.dma_start(wg[0:CR[c], c, :], t[f"wg_{c}"]).then_inc(in_att["grid"], 16)
            sp.dma_start(wgp[:, :, :], t["wgp"]).then_inc(in_att["grid"], 16)
            qkv(A1)
            proj(A1)
            proj(A2)
            slots(M0, RING, M0.slots)
            slots(M2, 0, RING)
            sp.wait_ge(S["y_ready"], 1)
            qkv(A3)
            proj(A3)
            sp.wait_ge(S["v_ready"], UNIT0["l2a"])
            qkv(A2)
            slots(M2, RING, M2.slots)
            slots(M3, 0, M3.slots)
            sp.wait_ge(S["h_ready"], 1)
            for j in range(2):
                sp.dma_start(out.rearrange("b n f -> (b n) f").rearrange("(j p t) f -> j p (t f)", j=2, t=TAU)[j],
                             H[:, TAU * j:TAU * (j + 1), :].rearrange("p t f -> p (t f)")).then_inc(S["out_written"], 16)
            sp.wait_ge(S["out_written"], 32)



        @block.tensor
        def _(pe):
            mm, tr = nc.tensor.matmul, nc.tensor.transpose

            def ln_turn(k, moe):
                for j in range(2):
                    pe.wait_ge(S["ln_normed"], 2 * LN_PASS[k] + j + 1)
                    for tau in range(TAU):
                        for c in range(NC_):
                            k_ = 128 if moe else CR[c]
                            last = tr(PS[0:k_, 4 + 2 * j + c, tau * TP:(tau + 1) * TP],
                                      XN[:, TAU * j + tau, c * 128:c * 128 + k_], cst[0:TP, 0:TP])
                    last.then_inc(S["ln_turned"], 1)
                pe.wait_ge(S["xt0_ready"], 2 * k + 2)
                pe.wait_ge(S["xt1_ready"], 2 * k + 2)

            def router(i, e):
                for g in range(NG):
                    for c in range(NC_):
                        last = mm(PS[0:TP, 4, g * e:(g + 1) * e], tile(XT[0:CB[c], c, 0:B * N], g // TAU, g % TAU),
                                  wr[i][0:CB[c], c, :], start=(c == 0), stop=(c == NC_ - 1))
                last.then_inc(S["logits"], 1)

            def moe(m):
                u0 = MU0[m.name]

                def hidden(u):
                    s, ch, j = u // (2 * m.chunks), u // 2 % m.chunks, u % 2
                    n, U = MS0[m.name] + s, u0 + u
                    r, cols = n % RING, slice(HN * j, HN * (j + 1))
                    if ch == 0 and j == 0:
                        pe.wait_ge(S["w_lo"], n + 1)
                        pe.wait_ge(S["w_lo1"], n + 1)
                    if u < 2:
                        pe.wait_ge(S["x_split"], 2 * MOES.index(m) + j + 1)
                    if U >= 2:
                        pe.wait_ge(S["a_ready"], U - 1)
                    for k in range(2 if m.up else 1):
                        o = PS[:, 2 * k + u % 2, 0:HN]
                        w = slice((k * m.chunks + ch) * 128, (k * m.chunks + ch + 1) * 128)
                        mm(o, WH[r][:, 0, w], XH[:, cols], start=True, stop=False)
                        mm(o, WH[r][:, 0, w], XL[:, cols], start=False, stop=False)
                        mm(o, WL[r][:, 0, w], XH[:, cols], start=False, stop=False)
                        mm(o, WH[r][:, 1, w], X1[:, cols], start=False, stop=False)
                        last = mm(o, WL[r][0:64, 1, w], X1[0:64, cols], start=False, stop=True)
                    last.then_inc(S["g_ready"], 1)

                def down(u):
                    s, ch, j = u // (2 * m.chunks), u // 2 % m.chunks, u % 2
                    n, U = MS0[m.name] + s, u0 + u
                    pe.wait_ge(S["ah_lo"], U + 1)
                    if u == 1:
                        pe.wait_ge(S["r_shift"], ROUTER[m.name][0] + 1)
                    if m.first(s, ch):
                        d = MD0[m.name] + 2 * owner_index(m, s, ch) - 2 + j
                        if d >= 0:
                            pe.wait_ge(S["drained"], d + 1)
                    for tau in range(TAU):
                        g = TAU * j + tau
                        w = slice(ch * C, (ch + 1) * C)
                        first = m.first(s, ch) and tau != 1
                        hi, lo = AH[U % 3][:, tau:HN:TAU], AL[U % 3][:, tau:HN:TAU]
                        mm(YB(g), hi, DH[n % RING][:, w], start=first, stop=False, skip_group_check=True)
                        mm(YB(g), hi, DL[n % RING][:, w], start=False, stop=False, skip_group_check=True)
                        last = mm(YB(g), lo, DH[n % RING][:, w], start=False, stop=m.last(s, ch), skip_group_check=True)
                    last.then_inc(S["w3_done"], 1)

                for u in range(m.units + 2):
                    if u < m.units:
                        hidden(u)
                    if u >= 2:
                        down(u - 2)

            def attention(a):
                u0 = UNIT0[a.name]
                W, P2 = wqkv[a.name], wp[a.name]
                pe.wait_ge(in_att[a.name], 48)
                if a.gated:
                    pe.wait_ge(S["setup_dve"], 1)
                    pe.wait_ge(S["xv_ready"], 2 * XV_N[a.name] + 2)
                    for b in range(B):
                        for r in (0, VW):
                            for c in range(NC_):
                                last = mm(PS[r:r + VW, 7, b * GRP:(b + 1) * GRP], XV[0:CB[c], c, b * VW:(b + 1) * VW],
                                          wr[1][0:CB[c], c, :], start=(c == 0), stop=(c == NC_ - 1))
                    last.then_inc(S["logits"], 1)

                def token_major(u):
                    g, j = u // 2, u % 2
                    if u >= 1:
                        pe.wait_ge(S["tm_done"], TM0[a.name] + u)
                    for tau in range(TAU):
                        for c in range(NC_):
                            last = mm(PSF[0:TP, 1024 + tau * 2 * a.fq:1024 + (tau + 1) * 2 * a.fq],
                                      tile(XT[0:CB[c], c, 0:B * N], j, tau),
                                      W[0:CB[c], c, g * a.width:g * a.width + 2 * a.fq],
                                      start=(c == 0), stop=(c == NC_ - 1))
                    last.then_inc(S["tm_ready"], 1)

                def qk(u):
                    g, j = u // 2, u % 2
                    U = u0 + u
                    if a.tm:
                        pe.wait_ge(S["tm_done"], TM0[a.name] + u + 1)
                    if u >= 1:
                        pe.wait_ge(S["q_sb"], U)
                        pe.wait_ge(S["k_sb"], U)
                    for k in range(2):
                        if a.tm:
                            for tau in range(TAU):
                                last = tr(PS[0:a.fq, k, tau * TP:(tau + 1) * TP],
                                          TX[u % 2][:, (2 * tau + k) * a.fq:(2 * tau + k + 1) * a.fq],
                                          cst[0:TP, 0:TP])
                        else:
                            for c in range(NC_):
                                off = g * a.width + k * a.fq
                                last = mm(PS[0:a.fq, k, 0:HN], W[0:CB[c], c, off:off + a.fq],
                                          XT[0:CB[c], c, HN * j:HN * (j + 1)], start=(c == 0), stop=(c == NC_ - 1))
                    last.then_inc(S["qk_ready"], 1)

                def values(u):
                    g, j = u // 2, u % 2
                    if u >= PT_LAG + 1:
                        pe.wait_ge(S["pt_sb"], u0 + u - PT_LAG)
                    elif u >= 1:
                        pe.wait_ge(S["v_sb"], u0 + u)
                    if g == 0:
                        pe.wait_ge(S["xv_ready"], 2 * XV_N[a.name] + j + 1)
                    off = g * a.width + 2 * a.fq
                    for i in range(HB // 2):
                        for c in range(NC_):
                            last = mm(PS[:, 4, i * a.fv:(i + 1) * a.fv], XV[0:CB[c], c, (HB * j + 2 * i) * VW:(HB * j + 2 * i + 2) * VW],
                                      W[0:CB[c], c, off:off + a.fv], start=(c == 0), stop=(c == NC_ - 1))
                    last.then_inc(S["v_ready"], 1)

                def scores(u):
                    U = u0 + u
                    pe.wait_ge(S["q_sb"], U + 1)
                    pe.wait_ge(S["k_sb"], U + 1)
                    if u >= 1:
                        pe.wait_ge(S["s_taken"], U)
                    for b in range(HB):
                        last = mm(PS[0:a.rows, 5, b * N:(b + 1) * N], QB[u % 2][0:a.fq, b, 0:a.rows],
                                  KS[u % 2][0:a.fq, b * N:(b + 1) * N], start=True, stop=True)
                    last.then_inc(S["s_ready"], 1)

                def turn_probs(u):
                    U = u0 + u
                    pe.wait_ge(S["p_sb"], U + 1)
                    pe.wait_ge(S["v_sb"], u0 + min(u + PT_LAG, a.units - 1) + 1)
                    if u >= 1:
                        pe.wait_ge(S["pt_sb"], U)
                    for i in range(HB // 2):
                        last = tr(PS[:, 4, i * 128:i * 128 + a.rows], PN[u % 2][0:a.rows, 2 * i:2 * i + 2, :],
                                  cst[0:a.rows, 0:a.rows])
                    last.then_inc(S["pt_ready"], 1)

                def mix(u):
                    U = u0 + u
                    pe.wait_ge(S["pt_sb"], U + 1)
                    pe.wait_ge(S["v_sb"], U + 1)
                    if u >= 1:
                        pe.wait_ge(S["o_sb"], U)
                    for b in range(HB):
                        i, r = b // 2, VW * (b % 2)
                        for h in range(a.hg):
                            last = mm(OB[a.slot * h:a.slot * (h + 1), b % 2, i * N:(i + 1) * N],
                                      VS[u % 5][r:r + N, i * a.fv + h * a.slot:i * a.fv + (h + 1) * a.slot],
                                      PT[u % 2][r:r + N, i * 128 + h * a.stride:i * 128 + h * a.stride + N],
                                      start=True, stop=True)
                    last.then_inc(S["o_ready"], 1)

                lag = 1 if a.tm else 0
                for i in range(a.units + lag + 4):
                    if a.tm and i < a.units:
                        token_major(i)
                    if 0 <= i - lag < a.units:
                        values(i - lag)
                        qk(i - lag)
                    if 0 <= i - lag - 1 < a.units:
                        scores(i - lag - 1)
                    if 0 <= i - lag - 3 < a.units:
                        turn_probs(i - lag - 3)
                    if 0 <= i - lag - 4 < a.units:
                        mix(i - lag - 4)

                pe.wait_ge(S["o_sb"], u0 + a.units)
                for g6 in range(NG):
                    for g in range(a.ng):
                        last = mm(PS[0:TP, g6 // 2, (g6 % 2) * C:(g6 % 2 + 1) * C],
                                  tile(OT[0:a.fv, g * B * N:(g + 1) * B * N], g6 // TAU, g6 % TAU), P2[:, g, :],
                                  start=(g == 0), stop=(g == a.ng - 1))
                last.then_inc(S["y_ready"], 1)

            def grid_attention():
                pe.wait_ge(in_att["grid"], 48)
                for i in range(NG):
                    j, ks = i // TAU, i % TAU
                    if i >= 2:
                        pe.wait_ge(S["grid_sb"], i - 1)
                    for n in range(2):
                        for c in range(NC_):
                            last = mm(PS[0:TP, 2 * (i % 2) + n, 0:288], XT[0:CR[c], c, i * TP:(i + 1) * TP], wg[0:CR[c], c, 288 * n:288 * (n + 1)],
                                      start=(c == 0), stop=(c == NC_ - 1))
                    last.then_inc(S["grid_ready"], 1)
                for g in range(NG):
                    j, tau = g // TAU, g % TAU
                    if tau == 0:
                        pe.wait_ge(S["grid_o"], j + 1)
                    if g >= 2:
                        pe.wait_ge(S["grid_osb"], g - 1)
                    for nd in range(3):
                        last = tr(PS[0:64, 4 + g % 2, nd * TP:(nd + 1) * TP],
                                  GO[:, j * 576 + nd * C + 64 * tau:j * 576 + nd * C + 64 * (tau + 1)], cst[0:TP, 0:TP])
                    last.then_inc(S["grid_turned"], 1)
                for g in range(NG):
                    pe.wait_ge(S["grid_osb"], g + 1)
                    for nd in range(3):
                        last = mm(PS[0:TP, g // 2, (g % 2) * C:(g % 2 + 1) * C],
                                  GT[:, (3 * g + nd) * TP:(3 * g + nd + 1) * TP], wgp[:, nd, :],
                                  start=(nd == 0), stop=(nd == 2))
                last.then_inc(S["y_ready"], 1)

            pe.wait_ge(S["in_patch"], 16 * (TOKF + 1))
            for g in range(NG):
                for k in range(TOKF):
                    last = mm(PS[0:TP, g // 2, (g % 2) * C:(g % 2 + 1) * C],
                              tile(BIG[:, k * B * N:(k + 1) * B * N], g // TAU, g % TAU), WTOK[:, k, :],
                              start=(k == 0), stop=(k == TOKF - 1))
            last.then_inc(S["patch_summed"], 1)
            pe.wait_ge(S["in_const"], 16 * len(consts))
            pe.wait_ge(S["setup_pool"], 1)
            for i, (kind, arg) in enumerate(STAGES[:STOP]):
                ln_turn(i, kind == "moe")
                if kind == "moe":
                    router(*ROUTER[arg.name])
                    moe(arg)
                elif kind == "attn":
                    attention(arg)
                else:
                    grid_attention()

        @block.scalar
        def _(act):
            activation = nc.scalar.activation

            def evac_xt(k, double, grid, moe):
                for j in range(2):
                    act.wait_ge(S["ln_turned"], 2 * k + j + 1)
                    xt_copy(lambda o, i, c: activation(o, i, ACT.Copy) if c is None else
                            activation(o, i, ACT.Identity, bias=gb[:, 2:3], scale=gb[:, 0:1]),
                            0, j, double, grid, moe).then_inc(S["xt0_ready"], 1)

            def split_high(m, s):
                n = MS0[m.name] + s
                r = n % RING
                act.wait_ge(wslot[r], 64 * (n // RING + 1))
                if s >= RING:
                    act.wait_ge(S["w3_done"], units_before(n - RING + 1))
                activation(WH[r][:, :, 0:m.width], RG[r][:, :, 0:m.width], ACT.Copy)
                activation(DH[r][:, 0:m.chunks * C], RD[r][:, 0:m.chunks * C], ACT.Copy).then_inc(S["w_hi"], 1)

            def moe(m):
                for u in range(m.units):
                    U = MU0[m.name] + u
                    act.wait_ge(S["g_ready"], U + 1)
                    if m.up:
                        if SG0[m.name] + u >= 2:
                            act.wait_ge(S["a_ready"], U - 1)
                        activation(SG[u % 2][:, :], PS[:, u % 2, 0:HN], m.act).then_inc(S["sg_ready"], 1)
                    else:
                        act.wait_ge(S["ah_lo"], U - 1)
                        activation(AF[U % 2][:, :], PS[:, u % 2, 0:HN], m.act).then_inc(S["a_ready"], 1)
                    if u == 1:
                        router_exp(ROUTER[m.name][0], NG * m.experts, TP)
                    s = u // (2 * m.chunks)
                    if u % (2 * m.chunks) == 3 and s + 1 < m.slots:
                        split_high(m, s + 1)

            def router_exp(i, w, rows):
                act.wait_ge(S["r_shift"], i + 1)
                activation(rl[0:rows, 1, 0:w], rl[0:rows, 0, 0:w], ACT.Exp).then_inc(S["r_exp"], 1)

            def attention(a):
                u0 = UNIT0[a.name]

                def keys(u):
                    U = u0 + u
                    act.wait_ge(S["qk_ready"], U + 1)
                    if U >= 2:
                        act.wait_ge(S["s_ready"], U - 1)
                    if a.tm:
                        o = KS[u % 2][0:a.fq, :].rearrange("f (p t) -> f t p", t=TAU)
                        i = PS[0:a.fq, 1, 0:HN].rearrange("f (t p) -> f t p", t=TAU)
                    else:
                        o, i = KS[u % 2][0:a.fq, :], PS[0:a.fq, 1, 0:HN]
                    if a.qk_norm:
                        activation(o, i, ACT.Identity, bias=qn[:, 3:4], scale=qn[:, 2:3]).then_inc(S["k_sb"], 1)
                    else:
                        activation(o, i, ACT.Copy).then_inc(S["k_sb"], 1)

                def vals(u):
                    U = u0 + u
                    act.wait_ge(S["v_ready"], U + 1)
                    if U >= 5:
                        act.wait_ge(S["o_ready"], U - 4)
                    activation(VS[u % 5][:, 0:4 * a.fv], PS[:, 4, 0:4 * a.fv], ACT.Copy).then_inc(S["v_sb"], 1)

                def exps(u):
                    U = u0 + u
                    act.wait_ge(S["s_taken"], U + 1)
                    e = ES[u % 2][0:a.rows, :]
                    activation(e, e, ACT.Exp).then_inc(S["e_ready"], 1)

                def probs_turned(u):
                    U = u0 + u
                    act.wait_ge(S["pt_ready"], U + 1)
                    if U >= 2:
                        act.wait_ge(S["o_ready"], U - 1)
                    view = lambda x: x.rearrange("p (i r) -> p i r", i=4)[:, :, 0:a.rows]
                    activation(view(PT[u % 2][:, :]), view(PS[:, 4, :]), ACT.Copy).then_inc(S["pt_sb"], 1)

                def outs(u):
                    U = u0 + u
                    act.wait_ge(S["o_ready"], U + 1)
                    o = (u // 2) * B * N + HN * (u % 2)
                    activation(OT[0:a.fv, o:o + HN].rearrange("f (i r n) -> f r i n", i=4, r=2),
                               OB[0:a.fv, :, :].rearrange("f r (i n) -> f r i n", i=4), ACT.Copy).then_inc(S["o_sb"], 1)

                def square(u):
                    n = u + 1
                    act.wait_ge(S["tm_ready"], TM0[a.name] + n)
                    if u >= 1:
                        act.wait_ge(S["tm_sum"], u)
                    activation(T2[:, :], PSF[0:TP, 1024:1024 + TAU * 256], ACT.Square).then_inc(S["tm_square"], 1)

                lag = 1 if a.tm else 0
                for i in range(a.units + lag + 4):
                    if a.qk_norm and i < a.units:
                        square(i)
                    if 0 <= i - lag < a.units:
                        vals(i - lag)
                        keys(i - lag)
                    if 0 <= i - lag - 1 < a.units:
                        exps(i - lag - 1)
                    if a.gated and i == lag + 2:
                        router_exp(1, B * GRP, 128)
                    if 0 <= i - lag - 3 < a.units:
                        probs_turned(i - lag - 3)
                    if 0 <= i - lag - 4 < a.units:
                        outs(i - lag - 4)

            def grid_attention():
                for i in range(0, NG):
                    act.wait_ge(S["grid_ready"], i + 1)
                    activation(GQ[:, i * 576:(i + 1) * 576].rearrange("p (n w) -> p n w", n=2),
                               PS[0:TP, 2 * (i % 2):2 * (i % 2) + 2, 0:288], ACT.Copy).then_inc(S["grid_sb"], 1)
                for j in range(2):
                    act.wait_ge(S["grid_s"], j + 1)
                    e = sg1[:, 1, 0:108]
                    activation(e, e, ACT.Exp, scale=0.25).then_inc(S["grid_e"], 1)
                for g in range(NG):
                    act.wait_ge(S["grid_turned"], g + 1)
                    activation(GT[:, 3 * g * TP:3 * (g + 1) * TP], PS[0:64, 4 + g % 2, 0:3 * TP],
                               ACT.Copy).then_inc(S["grid_osb"], 1)

            act.wait_ge(S["in_const"], 16 * len(consts))
            y = 0
            for i, (kind, arg) in enumerate(STAGES[:STOP]):
                if kind == "moe":
                    act.wait_ge(S["y_ready"], y)
                    split_high(arg, 0)
                else:
                    y += 1
                evac_xt(i, kind == "attn" and arg.double_ln, kind == "grid", kind == "moe")
                if kind == "moe":
                    moe(arg)
                elif kind == "attn":
                    attention(arg)
                else:
                    grid_attention()

        @block.vector
        def _(dve):
            V = nc.vector
            count = [0]

            def link(ins):
                count[0] += 1
                ins.then_inc(S["dve_step"], 1)
                dve.wait_ge(S["dve_step"], count[0])

            def layer_norm(p, src, moe=False):
                for j in range(2):
                    for g in range(TAU * j, TAU * (j + 1)):
                        last = V.bn_stats(st[:, g, :], src[:, g, 0:C])
                    link(last)
                    for g in range(TAU * j, TAU * (j + 1)):
                        last = V.bn_aggr(mv[:, g, :], st[:, g, :])
                    link(last)
                    V.tensor_scalar(var[:, TAU * j:TAU * (j + 1)], mv[:, TAU * j:TAU * (j + 1), 1], EPS, None,
                                    ALU.add).then_inc(S["ln_stats"], 1)
                for j in range(2):
                    dve.wait_ge(S["ln_rstd"], 2 * p + j + 1)
                    for tau in range(TAU):
                        g = TAU * j + tau
                        last = V.tensor_scalar(XN[:, g, 0:C], src[:, g, 0:C], mv[:, g, 0:1], rstd[:, g:g + 1],
                                               ALU.subtract, ALU.mult)
                        if moe:
                            last = V.tensor_scalar(XN[:, g, C:], src[:, g, 128:C], mv[:, g, 0:1], rstd[:, g:g + 1],
                                                   ALU.subtract, ALU.mult)
                    last.then_inc(S["ln_normed"], 1)
                dve.wait_ge(S["ln_normed"], 2 * p + 2)

            def evac_xt(k, double, grid, moe):
                for j in range(2):
                    dve.wait_ge(S["ln_turned"], 2 * k + j + 1)
                    xt_copy(lambda o, i, c: V.tensor_copy(o, i) if c is None else
                            V.tensor_scalar(o, i, gb[0:64, 1:2], gb[0:64, 3:4], ALU.mult, ALU.add),
                            1, j, double, grid, moe).then_inc(S["xt1_ready"], 1)

            def split_low1(m, s):
                n = MS0[m.name] + s
                r = n % RING
                dve.wait_ge(S["w_hi"], n + 1)
                V.tensor_tensor(WL[r][0:64, 1, 0:m.width], RG[r][0:64, 1, 0:m.width],
                                WH[r][0:64, 1, 0:m.width].bitcast(F32), ALU.subtract).then_inc(S["w_lo1"], 1)

            def split_stream(k):
                for j in range(2):
                    cols = slice(HN * j, HN * (j + 1))
                    dve.wait_ge(S["xt0_ready"], 2 * k + j + 1)
                    dve.wait_ge(S["xt1_ready"], 2 * k + j + 1)
                    V.tensor_copy(XH[:, cols], XT[:, 0, cols])
                    V.tensor_copy(X1[0:64, cols], XT[0:64, 1, cols])
                    link(V.tensor_copy(X1T[64:128, cols], X1F[64:128, cols]))
                    V.tensor_tensor(XL[:, cols], XT[:, 0, cols], XH[:, cols].bitcast(F32), ALU.subtract)
                    V.tensor_tensor(X1[64:128, cols], X1F[64:128, cols], X1T[64:128, cols].bitcast(F32),
                                    ALU.subtract).then_inc(S["x_split"], 1)

            def softmax(rows, w, parts, logits, add=None):
                G = w[0]
                view = lambda k, o, n: rl[0:rows, k, 0:G * w[1]].rearrange("p (g e) -> p g e", g=G)[:, :, o:o + n]
                for n_, (o, n) in enumerate(parts):
                    link(V.tensor_reduce(rs[0:rows, n_, 0:G], logits[:, :, o:o + n], X, ALU.max))
                    last = V.tensor_tensor(view(0, o, n), logits[:, :, o:o + n],
                                           rs[0:rows, n_, 0:G].unsqueeze(2).to_broadcast([rows, G, n]), ALU.subtract)
                return last, view

            def normalise(rows, w, parts, view, r):
                dve.wait_ge(S["r_exp"], r + 1)
                G = w[0]
                for n_, (o, n) in enumerate(parts):
                    link(V.tensor_reduce(rs[0:rows, n_, 0:G], view(1, o, n), X, ALU.add))
                    link(V.reciprocal(rs[0:rows, n_, 0:G], rs[0:rows, n_, 0:G]))
                    link(V.tensor_tensor(view(2, o, n), view(1, o, n),
                                         rs[0:rows, n_, 0:G].unsqueeze(2).to_broadcast([rows, G, n]), ALU.mult))

            def top_mask(dst, sel, rows, G, E, k):
                cube = [rows, G, E, E]
                r1 = R1[0:rows, 0:G * E * E].rearrange("p (g e f) -> p g e f", g=G, e=E)
                r2 = R2[0:rows, 0:G * E * E].rearrange("p (g e f) -> p g e f", g=G, e=E)
                other = sel.unsqueeze(2).to_broadcast(cube)
                own = sel.unsqueeze(3).to_broadcast(cube)
                V.tensor_tensor(r1, other, own, ALU.is_gt)
                link(V.tensor_tensor(r2, other, own, ALU.is_equal))
                link(V.tensor_tensor(r2, r2, tri[0:rows, 0:E, 0:E].unsqueeze(1).to_broadcast(cube), ALU.mult))
                link(V.tensor_tensor(r1, r1, r2, ALU.add))
                link(V.tensor_reduce(dst, r1, X, ALU.add))
                link(V.tensor_scalar(dst, dst, float(k), None, ALU.is_lt))

            def router(m, i):
                r, e = ROUTER[m.name]
                w = (NG, e)
                dve.wait_ge(S["logits"], r + 1)
                logits = PS[0:TP, 4, 0:NG * e].rearrange("p (g e) -> p g e", g=NG)
                last, view = softmax(TP, w, [(0, e)], logits)
                last.then_inc(S["r_shift"], 1)
                normalise(TP, w, [(0, e)], view, r)
                probs = view(2, 0, e)
                mask = view(3, 0, e)
                sel = probs
                if m is M2:
                    sel = view(0, 0, e)
                    link(V.tensor_tensor(sel, probs, ebias[:, :].unsqueeze(1).to_broadcast([TP, NG, e]), ALU.add))
                top_mask(mask, sel, TP, NG, e, m.topk)
                if m is M0:
                    V.tensor_reduce(maxp[:, :], probs, X, ALU.max)
                    link(V.tensor_copy(comb[0][:, :, :], mask))
                    return
                link(V.tensor_tensor(mask, mask, probs, ALU.mult))
                link(V.tensor_reduce(rs[0:TP, 0, 0:NG], mask, X, ALU.add))
                if m is M2:
                    link(V.tensor_scalar(rs[0:TP, 0, 0:NG], rs[0:TP, 0, 0:NG], 1e-9, None, ALU.add))
                link(V.reciprocal(rs[0:TP, 0, 0:NG], rs[0:TP, 0, 0:NG]))
                link(V.tensor_tensor(comb[i][:, :, 0:e], mask,
                                     rs[0:TP, 0, 0:NG].unsqueeze(2).to_broadcast([TP, NG, e]), ALU.mult))

            def centre(n):
                c, g = n // A1.ng, n % A1.ng
                if n == 0:
                    dve.wait_ge(in_att["l1f"], 48)
                w = wqkv["l1f"][:, c, g * A1.width:g * A1.width + 256].rearrange("k (h d) -> k h d", d=64)
                w = w[0:CB[c]]
                m = cw[0:CB[c], 4 * n:4 * (n + 1)]
                link(V.tensor_reduce(m, w, X, ALU.add))
                link(V.tensor_scalar(m, m, -1.0 / 64, None, ALU.mult))
                last = V.tensor_tensor(w, w, m.unsqueeze(2).to_broadcast([CB[c], 4, 64]), ALU.add)
                if n == NC_ * A1.ng - 1:
                    last.then_inc(S["setup_dve"], 1)

            def moe(m, i):
                def drain(u):
                    s, ch, j = u // (2 * m.chunks), u // 2 % m.chunks, u % 2
                    if not m.last(s, ch):
                        return
                    e = m.expert(s, ch)
                    dve.wait_ge(S["w3_done"], MU0[m.name] + u + 1)
                    d = MD0[m.name] + 2 * owner_index(m, s, ch) + j
                    if d >= 2 and owner_index(m, s, ch):
                        dve.wait_ge(S["drained"], d - 1)
                    for tau in range(TAU):
                        g = TAU * j + tau
                        y = YB(g)
                        into = ACC if m is M0 else H
                        coef = comb[i][:, g, e:e + 1]
                        if m is M0 and e == 0:
                            last = V.tensor_scalar(ACC[:, g, :], y, coef, None, ALU.mult)
                        else:
                            last = V.scalar_tensor_tensor(into[:, g, :], y, coef, into[:, g, :], ALU.mult, ALU.add)
                    last.then_inc(S["drained"], 1)

                for u in range(m.units + 2):
                    if m is M0 and u >= 8 and u % 4 == 0 and u // 4 - 2 < NC_ * A1.ng:
                        centre(u // 4 - 2)
                    if u < m.units:
                        U = MU0[m.name] + u
                        if m.up:
                            dve.wait_ge(S["sg_ready"], SG0[m.name] + u + 1)
                            if U >= 2:
                                dve.wait_ge(S["ah_lo"], U - 1)
                            V.tensor_tensor(AF[U % 2][:, :], SG[u % 2][:, :], PS[:, 2 + u % 2, 0:HN],
                                            ALU.mult).then_inc(S["a_ready"], 1)
                        dve.wait_ge(S["a_ready"], U + 1)
                        if U >= 3:
                            dve.wait_ge(S["w3_done"], U - 2)
                        V.tensor_copy(AH[U % 3][:, :], AF[U % 2][:, :]).then_inc(S["ah_hi"], 1)
                        s = u // (2 * m.chunks)
                        if u % (2 * m.chunks) == 4 and s + 1 < m.slots:
                            split_low1(m, s + 1)
                    if u == 1:
                        router(m, i)
                    if u >= 2:
                        drain(u - 2)
                dve.wait_ge(S["drained"], MD0[m.name] + 2 * len(set(m.owner)))
                if m is M0:
                    link(V.tensor_copy(ACCB[:, :, :], ACC[:, :, :]))
                    for g in range(NG):
                        last = V.scalar_tensor_tensor(H[:, g, :], ACCB[:, g, :], maxp[:, g:g + 1], H[:, g, :],
                                                      ALU.mult, ALU.add)
                    link(last)

            def add_y(n):
                dve.wait_ge(S["y_ready"], n + 1)
                dve.wait_ge(S["bias_added"], n + 1)
                for i in range(3):
                    last = V.tensor_tensor(H[:, 2 * i:2 * i + 2, :].rearrange("p g f -> p (g f)"), PS[0:TP, i, 0:2 * C],
                                           H[:, 2 * i:2 * i + 2, :].rearrange("p g f -> p (g f)"), ALU.add)
                link(last)

            def gates(a):
                dve.wait_ge(S["logits"], 2)
                logits = PS[:, 7, 0:B * GRP].rearrange("p (g e) -> p g e", g=B)
                parts = [(0, 10), (10, 2), (12, 2)]
                last, view = softmax(128, (B, GRP), parts, logits)
                last.then_inc(S["r_shift"], 1)
                normalise(128, (B, GRP), parts, view, 1)
                p, m10 = view(2, 0, 10), view(3, 0, 10)
                top_mask(m10, p, 128, B, 10, 2)
                link(V.tensor_tensor(m10, m10, p, ALU.mult))
                tot = rs[:, 0, 0:B]
                link(V.tensor_reduce(tot, m10, X, ALU.add))
                link(V.tensor_scalar(tot, tot, FEPS, None, ALU.max))
                link(V.reciprocal(tot, tot))
                w0 = view(2, 10, 2)
                link(V.tensor_scalar(w0, w0, 4.0, None, ALU.mult))
                link(V.tensor_tensor(tot, tot, view(2, 10, 2)[:, :, 1], ALU.mult))
                link(V.tensor_tensor(m10, m10, tot.unsqueeze(2).to_broadcast([128, B, 10]), ALU.mult))
                sh = view(2, 12, 2)
                link(V.tensor_tensor(sh, sh, w0[:, :, 0:1].to_broadcast([128, B, 2]), ALU.mult))
                for hh in range(2):
                    r = slice(64 * hh, 64 * (hh + 1))
                    V.tensor_copy(GH[r, 0, :], sh[r, :, hh])
                    last = V.tensor_copy(GH[r, 1:6, :].rearrange("p g b -> p b g"), m10[r, :, hh:10:2])
                link(last)

            def attention(a):
                u0 = UNIT0[a.name]

                def token_major(u):
                    n = TM0[a.name] + u
                    f2 = TAU * 2 * a.fq
                    src = PSF[0:TP, 1024:1024 + f2]
                    tx, t2 = TX[u % 2][:, 0:f2], T2[:, 0:f2]
                    if u0 + u >= 2:
                        dve.wait_ge(S["qk_ready"], u0 + u - 1)
                    if a.rope:
                        dve.wait_ge(S["tm_ready"], n + 1)
                        co = rope[:, 0, :, :].rearrange("p t f -> p (t f)")
                        si = rope[:, 1, :, :].rearrange("p t f -> p (t f)")
                        V.tensor_tensor(tx, src, co, ALU.mult)
                        V.tensor_tensor(t2[:, 0:f2:2], src[:, 1:f2:2], si[:, 0:f2:2], ALU.mult)
                        link(V.tensor_tensor(t2[:, 1:f2:2], src[:, 0:f2:2], si[:, 1:f2:2], ALU.mult))
                        V.tensor_tensor(tx, tx, t2, ALU.add).then_inc(S["tm_done"], 1)
                    else:
                        dve.wait_ge(S["tm_rstd"], u + 1)
                        V.tensor_tensor(tx.rearrange("p (h d) -> p h d", d=64), src.rearrange("p (h d) -> p h d", d=64),
                                        ssq[:, 2, :].unsqueeze(2).to_broadcast([TP, 12, 64]),
                                        ALU.mult).then_inc(S["tm_done"], 1)

                def mean_square(u):
                    dve.wait_ge(S["tm_square"], u + 1)
                    link(V.tensor_reduce(ssq[:, 0, :], T2[:, :].rearrange("p (h d) -> p h d", d=64), X, ALU.add))
                    V.tensor_scalar(ssq[:, 1, :], ssq[:, 0, :], 1.0 / 64, EPS, ALU.mult, ALU.add).then_inc(S["tm_sum"], 1)

                def queries(u):
                    U = u0 + u
                    dve.wait_ge(S["qk_ready"], U + 1)
                    if U >= 2:
                        dve.wait_ge(S["s_ready"], U - 1)
                    for h in range(a.hg):
                        q = QB[u % 2][0:a.fq, :, h * a.stride:h * a.stride + N]
                        if a.tm:
                            last = q_scale(q.rearrange("f b (n t) -> f b n t", t=TAU),
                                           PS[0:a.fq, 0, 0:HN].rearrange("f (t b n) -> f b n t", t=TAU, b=HB), h)
                        else:
                            last = q_scale(q, PS[0:a.fq, 0, 0:HN].rearrange("f (b n) -> f b n", b=HB), h)
                    last.then_inc(S["q_sb"], 1)

                def q_scale(o, i, h):
                    if a.qk_norm:
                        return V.tensor_scalar(o, i, qs[:, 2 * h:2 * h + 1], qs[:, 2 * h + 1:2 * h + 2], ALU.mult, ALU.add)
                    k = h if a.dim == 16 else 3 + h
                    return V.tensor_scalar(o, i, mh[0:a.fq, k:k + 1], None, ALU.mult)

                def shift(u):
                    U = u0 + u
                    dve.wait_ge(S["s_ready"], U + 1)
                    if U >= 2:
                        dve.wait_ge(S["p_sb"], U - 1)
                    s = PS[0:a.rows, 5, 0:HN].rearrange("p (b k) -> p b k", b=HB)
                    e = ES[u % 2][0:a.rows, :].rearrange("p (b k) -> p b k", b=HB)
                    mx = sm[0:a.rows, 0, :]
                    if a.mask:
                        mk = masks[:, 0 if a.mask == "causal" else 1, :]
                        link(V.tensor_tensor(e, s, mk.unsqueeze(1).to_broadcast([a.rows, HB, N]), ALU.add))
                        s = e
                    link(V.tensor_reduce(mx, s, X, ALU.max))
                    V.tensor_tensor(e, s, mx.unsqueeze(2).to_broadcast([a.rows, HB, N]),
                                    ALU.subtract).then_inc(S["s_taken"], 1)

                def norm(u):
                    U = u0 + u
                    dve.wait_ge(S["e_ready"], U + 1)
                    e = ES[u % 2][0:a.rows, :].rearrange("p (b k) -> p b k", b=HB)
                    tot, inv = sm[0:a.rows, 1, :], sm[0:a.rows, 2, :]
                    link(V.tensor_reduce(tot, e, X, ALU.add))
                    link(V.reciprocal(inv, tot))
                    if a.gated:
                        link(V.tensor_tensor(inv, inv, GH[:, u // 2, HB * (u % 2):HB * (u % 2 + 1)], ALU.mult))
                    if U >= 2:
                        dve.wait_ge(S["pt_ready"], U - 1)
                    V.tensor_tensor(PN[u % 2][0:a.rows, :, 0:N], e, inv.unsqueeze(2).to_broadcast([a.rows, HB, N]),
                                    ALU.mult).then_inc(S["p_sb"], 1)

                for r in range(2):
                    if a is not A2:
                        V.memset(PN[r][:, :, N:], 0.0)
                    if a.stride != N:
                        V.memset(QB[r][:, :, :], 0.0)
                link(V.memset(sm[:, 3, :], 0.0))
                lag = 1 if a.tm else 0
                for i in range(a.units + lag + 4):
                    if a.qk_norm and i < a.units:
                        mean_square(i)
                    if a.rope and i < a.units:
                        token_major(i)
                    if 0 <= i - lag < a.units:
                        queries(i - lag)
                    if a.qk_norm and i < a.units:
                        token_major(i)
                    if 0 <= i - lag - 1 < a.units:
                        shift(i - lag - 1)
                    if a.gated and i == lag + 2:
                        gates(a)
                    if 0 <= i - lag - 2 < a.units:
                        norm(i - lag - 2)

            def grid_attention():
                qkv = GQ.rearrange("p (j k f) -> p j k f", j=2, k=3)
                for j in range(2):
                    dve.wait_ge(S["grid_sb"], 3 * j + 3)
                    prod = OT[0:TP, 0:9 * C].rearrange("p (q k f) -> p q k f", q=3, k=3)
                    q = qkv[:, j, :, 0:C].unsqueeze(2).to_broadcast([TP, 3, 3, C])
                    k = qkv[:, j, :, C:2 * C].unsqueeze(1).to_broadcast([TP, 3, 3, C])
                    link(V.tensor_tensor(prod, q, k, ALU.mult))
                    sc = sg1[:, 0, 0:108]
                    link(V.tensor_reduce(sc, OT[0:TP, 0:9 * C].rearrange("p (s d) -> p s d", d=16), X, ALU.add))
                    s3 = sc.rearrange("p (q k n) -> p q n k", q=3, k=3)
                    mx = sg1[:, 2, 0:36].rearrange("p (q n) -> p q n", q=3)
                    link(V.tensor_reduce(mx, s3, X, ALU.max))
                    e3 = sg1[:, 1, 0:108].rearrange("p (q k n) -> p q n k", q=3, k=3)
                    V.tensor_tensor(e3, s3, mx.unsqueeze(3).to_broadcast([TP, 3, 12, 3]),
                                    ALU.subtract).then_inc(S["grid_s"], 1)
                    dve.wait_ge(S["grid_e"], j + 1)
                    link(V.tensor_reduce(mx, e3, X, ALU.add))
                    link(V.reciprocal(mx, mx))
                    link(V.tensor_tensor(e3, e3, mx.unsqueeze(3).to_broadcast([TP, 3, 12, 3]), ALU.mult))
                    o = GO[:, j * 576:(j + 1) * 576].rearrange("p (n q d) -> p q n d", n=12, q=3)
                    p4 = sg1[:, 1, 0:108].rearrange("p (q k n) -> p q k n", q=3, k=3)
                    tmp = OT[0:TP, 0:576].rearrange("p (q n d) -> p q n d", q=3, n=12)
                    for ki in range(3):
                        v = qkv[:, j, ki, 2 * C:3 * C].rearrange("p (n d) -> p n d", n=12)
                        w = p4[:, :, ki, :].unsqueeze(3).to_broadcast([TP, 3, 12, 16])
                        vv = v.unsqueeze(1).to_broadcast([TP, 3, 12, 16])
                        link(V.tensor_tensor(o if ki == 0 else tmp, w, vv, ALU.mult))
                        if ki:
                            last = V.tensor_tensor(o, o, tmp, ALU.add)
                            if ki == 1:
                                link(last)
                    last.then_inc(S["grid_o"], 1)
                    dve.wait_ge(S["grid_o"], j + 1)

            V.memset(comb[1][:, :, 8:9], 1.0)
            V.memset(MIX[:, :], 0.0)
            link(V.memset(XT[64:65, 1, :], 1.0))
            dve.wait_ge(S["in_const"], 16 * len(consts))
            for h in range(2):
                V.tensor_scalar(qs[:, 2 * h:2 * h + 1], qn[:, 0:1], mh[:, 3 + h:4 + h], None, ALU.mult)
                last = V.tensor_scalar(qs[:, 2 * h + 1:2 * h + 2], qn[:, 1:2], mh[:, 3 + h:4 + h], None, ALU.mult)
            link(last)

            dve.wait_ge(S["patch_summed"], 1)
            for g in range(NG):
                last = V.tensor_tensor(H[:, g, :], PS[0:TP, g // 2, (g % 2) * C:(g % 2 + 1) * C], bias[:, 0, :], ALU.add)
            link(last)
            for j in range(2):
                last = V.tensor_tensor(H[:, TAU * j:TAU * (j + 1), :], H[:, TAU * j:TAU * (j + 1), :], posb[:, :, :], ALU.add)
            link(last)

            y = 0
            p = 0
            for i, (kind, arg) in enumerate(STAGES[:STOP]):
                layer_norm(p, H, kind == "moe")
                p += 1
                if kind == "attn" and arg.double_ln:
                    layer_norm(p, XN)
                    p += 1
                if kind == "moe":
                    split_low1(arg, 0)
                evac_xt(i, kind == "attn" and arg.double_ln, kind == "grid", kind == "moe")
                if kind == "moe":
                    split_stream(i)
                    moe(arg, MOES.index(arg))
                elif kind == "attn":
                    attention(arg)
                    add_y(y)
                    y += 1
                else:
                    grid_attention()
                    add_y(y)
                    y += 1
            V.memset(sg1[:, 0, 0:1], 0.0).then_inc(S["h_ready"], 1)

        @block.gpsimd
        def _(pool):
            G = nc.gpsimd
            count = [0]

            def link(ins):
                count[0] += 1
                ins.then_inc(S["pool_step"], 1)
                pool.wait_ge(S["pool_step"], count[0])

            link(G.memset(nhalf[:, :], -0.5))
            link(G.memset(tri[:, :, :], 1.0))
            link(G.affine_select(out=tri[:, :, :], in_=tri[:, :, :], compare_op=ALU.is_gt, fill=0.0, base=0,
                                 pattern=[[1, 16], [-1, 16]], channel_multiplier=0))
            G.memset(nhalf[:, 0:1], -0.5).then_inc(S["setup_pool"], 1)
            pool.wait_ge(S["setup_pool"], 1)
            pool.wait_ge(S["in_const"], 16 * len(consts))
            def split_low(m, s):
                n = MS0[m.name] + s
                r, w, d = n % RING, m.width, m.chunks * C
                pool.wait_ge(S["w_hi"], n + 1)
                G.tensor_tensor(WL[r][:, 0, 0:w], RG[r][:, 0, 0:w], WH[r][:, 0, 0:w].bitcast(F32), ALU.subtract)
                G.tensor_tensor(DL[r][:, 0:d], RD[r][:, 0:d], DH[r][:, 0:d].bitcast(F32),
                                ALU.subtract).then_inc(S["w_lo"], 1)

            def experts(m):
                split_low(m, 0)
                for u in range(m.units):
                    U = MU0[m.name] + u
                    pool.wait_ge(S["ah_hi"], U + 1)
                    G.tensor_tensor(AL[U % 3][:, :], AF[U % 2][:, :], AH[U % 3][:, :].bitcast(F32),
                                    ALU.subtract).then_inc(S["ah_lo"], 1)
                    s = u // (2 * m.chunks)
                    if u % (2 * m.chunks) == 4 and s + 1 < m.slots:
                        split_low(m, s + 1)

            y = p = 0
            for i, (kind, arg) in enumerate(STAGES[:STOP]):
                for _ in range(2 if kind == "attn" and arg.double_ln else 1):
                    for j in range(2):
                        pool.wait_ge(S["ln_stats"], 2 * p + j + 1)
                        r = rstd[:, TAU * j:TAU * (j + 1)]
                        G.tensor_tensor(r, var[:, TAU * j:TAU * (j + 1)], nhalf[0:TP, 0:TAU], ALU.pow).then_inc(S["ln_rstd"], 1)
                    p += 1
                if kind != "moe":
                    pool.wait_ge(S["ln_normed"], 2 * p)
                    G.tensor_tensor(H[:, :, :], H[:, :, :], bias[:, 1 + y, :].unsqueeze(1).to_broadcast([TP, NG, C]),
                                    ALU.add).then_inc(S["bias_added"], 1)
                    y += 1
                if kind == "moe":
                    experts(arg)
                if kind == "attn":
                    for j in range(2):
                        pool.wait_ge(S["xt0_ready"], 2 * i + 2)
                        pool.wait_ge(S["xt1_ready"], 2 * i + 2)
                        for c in range(NC_):
                            o = XV[0:CB[c], c, :].rearrange("k (b n) -> k b n", b=B)[:, HB * j:HB * (j + 1), 0:N]
                            last = G.tensor_copy(o, XT[0:CB[c], c, HN * j:HN * (j + 1)].rearrange("k (b n) -> k b n", b=HB))
                        last.then_inc(S["xv_ready"], 1)
                if kind == "attn" and arg.qk_norm:
                    for u in range(arg.units):
                        pool.wait_ge(S["tm_sum"], u + 1)
                        G.tensor_tensor(ssq[:, 2, :], ssq[:, 1, :], nhalf[0:TP, 0:12], ALU.pow).then_inc(S["tm_rstd"], 1)


def layouts(a):
    f = np.float32
    z = lambda *shape: np.zeros(shape, f)
    t = {}
    t["patch"] = a["x"].reshape(B, 3, 6, 16, 6, 16).transpose(1, 3, 5, 0, 2, 4).reshape(TOKF, 128, B * N).transpose(1, 0, 2)
    t["wtok"] = a["L0_tok_W"].T.reshape(TOKF, 128, C).transpose(1, 0, 2)

    def chunks(w, b=None):
        o = z(128, NC_, w.shape[1])
        for c in range(NC_):
            o[0:CR[c], c] = w[128 * c:128 * c + CR[c]]
        if b is not None:
            o[CR[1], 1] = b
        return o

    def attn(at, wq, wk, wv, wo, bq, bk, bv):
        parts = []
        for w, b, slot in ((wq, bq, at.dim), (wk, bk, at.dim), (wv, bv, at.slot)):
            w = chunks(w, b).reshape(128, NC_, at.ng, at.hg, at.dim)
            o = z(128, NC_, at.ng, at.hg, slot)
            o[..., 0:at.dim] = w
            parts.append(o.reshape(128, NC_, at.ng, at.hg * slot))
        w = np.concatenate(parts, axis=3).reshape(128, NC_, at.ng * at.width)
        for c in range(NC_):
            t[f"wqkv_{at.name}_{c}"] = w[0:CB[c], c]
        o = z(at.ng, at.hg, at.slot, C)
        o[:, :, 0:at.dim] = wo.reshape(at.ng, at.hg, at.dim, C)
        t["wp_" + at.name] = o.reshape(at.ng, at.fv, C).transpose(1, 0, 2)

    def thirds(w):
        n = w.shape[-1] // 3
        return w[..., 0:n], w[..., n:2 * n], w[..., 2 * n:]

    q, k, v = thirds(a["L0_attn_W_attn"])
    bq, bk, bv = thirds(a["L0_attn_b_attn"])
    attn(A0, q, k, v, a["L0_attn_W_proj"], bq, bk, bv)
    q, k, v = thirds(a["L1_ffn_qkv_w"])
    bq, bk, bv = thirds(a["L1_ffn_qkv_b"])
    attn(A1, q, k, v, a["L1_ffn_proj_w"], bq, bk, bv)
    q, k, v = thirds(a["L2_attn_w_qkv"])
    attn(A2, q, k, v, a["L2_attn_w_out"], None, None, None)
    attn(A3, a["L3_attn_Wq"], a["L3_attn_Wk"], a["L3_attn_Wv"], a["L3_attn_Wo"],
         a["L3_attn_bq"], a["L3_attn_bk"], a["L3_attn_bv"])
    t["wg_0"], t["wg_1"] = a["L1_attn_qkv_w"].T[0:128], a["L1_attn_qkv_w"].T[128:]
    t["wgp"] = a["L1_attn_proj_w"].T.reshape(3, 64, C).transpose(1, 0, 2)

    def moe(m, gate, up, down):
        t["gu_" + m.name] = np.concatenate([w for w in (gate, up) if w is not None], axis=2)
        t["wd_" + m.name] = down.reshape(m.slots, m.chunks, 128, C).transpose(0, 2, 1, 3)

    moe(M0, a["L0_ffn_w1"], a["L0_ffn_w2"], a["L0_ffn_w3"])
    cat = lambda w, s: np.concatenate([w, s[None]]).transpose(0, 2, 1)
    moe(M2, cat(a["L2_ffn_Wg"], a["L2_ffn_sg"]), cat(a["L2_ffn_Wu"], a["L2_ffn_su"]), cat(a["L2_ffn_Wd"], a["L2_ffn_sd"]))
    moe(M3, a["L3_ffn_w1"].reshape(C, M3.slots, 512).transpose(1, 0, 2), None,
        a["L3_ffn_w2"].reshape(M3.slots, 512, C))

    t["wr0"] = chunks(a["L0_ffn_router_w"], a["L0_ffn_router_b"])
    t["wr1"] = chunks(np.concatenate([a["L1_ffn_wg_w"], a["L1_ffn_wg0_w"], a["L1_ffn_wg1_w"]], axis=1))
    t["wr2"] = chunks(a["L2_ffn_w_router"].T)
    t["wr3"] = chunks(a["L3_ffn_router_w"].T)
    t["bias"] = np.broadcast_to(np.stack([a[n] for n in (
        "L0_tok_b", "L0_attn_b_proj", "L1_attn_proj_b", "L1_ffn_proj_b", "L2_attn_b_out", "L3_attn_bo")]), (TP, 6, C))
    t["posb"] = np.broadcast_to(a["L0_tok_pos"].reshape(1, NB, TAU, C), (HB, NB, TAU, C)).reshape(TP, TAU, C)
    t["gb"] = np.concatenate([chunks(a[n][:, None])[:, :, 0] for n in ("L2_attn_gamma", "L2_attn_beta")], axis=1)
    t["qn"] = np.stack([np.concatenate([a["L1_ffn_" + n]] * 2) for n in
                        ("q_norm_w", "q_norm_b", "k_norm_w", "k_norm_b")], axis=1)
    t["ebias"] = np.broadcast_to(a["L2_ffn_expert_bias"], (TP, 8))

    t["ident"] = np.eye(128, dtype=f)
    mh = z(128, 6)
    for h in range(3):
        mh[16 * h:16 * (h + 1), h] = 16 ** -0.5
    for h in range(2):
        mh[64 * h:64 * (h + 1), 3 + h] = 64 ** -0.5
    t["mh"] = mh
    inv = (1.0 / 10000.0 ** (np.arange(0, 16, 2, dtype=f) / f(16))).astype(f)
    ang = (np.arange(N, dtype=f)[:, None] * inv[None]).astype(f)
    cos, sin = np.repeat(np.cos(ang), 2, axis=1).astype(f), np.repeat(np.sin(ang), 2, axis=1).astype(f)
    sin[:, 0::2] *= -1
    tok = (TAU * (np.arange(TP) % NB))[:, None] + np.arange(TAU)[None]
    t["rope"] = np.stack([np.tile(w[tok], (1, 1, 6)) for w in (cos, sin)], axis=1)
    i, j = np.arange(N)[:, None], np.arange(N)[None]
    causal = np.where(j <= i, 0, -1e30).astype(f)
    band = np.where(abs(i - j) <= 32, 0, -1e9).astype(f)
    t["masks"] = np.stack([np.tile(w, (3, 1)) for w in (causal, band)], axis=1)
    return {n: np.ascontiguousarray(w) for n, w in t.items()}


def kernel(**inputs):
    import concourse.bacc as _bacc
    from concourse.bass_utils import run_bass_kernel_spmd as _run

    nc = _bacc.Bacc("TRN2", target_bir_lowering=False, num_devices=1)
    arrays, aps = {}, {}
    for name, w in layouts({n: np.asarray(v) for n, v in inputs.items()}).items():
        arrays[f"in_{name}_dram"] = w
        aps[name] = nc.dram_tensor(f"in_{name}_dram", w.shape, mybir.dt.from_np(w.dtype), kind="ExternalInput").ap()
    out = nc.dram_tensor("out_0_dram", (B, N, C), F32, kind="ExternalOutput").ap()
    bass_vit_tower(nc, aps, out)
    r = _run(nc, [arrays], core_ids=[0])
    return r.results[0]["out_0_dram"]
```

```python
from contextlib import ExitStack

import numpy as np
import concourse.bass as bass
from concourse import mybir

ALU = mybir.AluOpType
ACT = mybir.ActivationFunctionType
F32 = mybir.dt.float32
BF16 = mybir.dt.bfloat16
X = mybir.AxisListType.X

B, N, C = 16, 36, 192
NC_ = 2
CR = (128, C - 128)
CB = (CR[0], CR[1] + 1)
TP = 96
NG = B * N // TP
TAU = 3
HB = 8
HN = HB * N
NB = N // TAU
TOKF = 768 // 128
VW = 64
EPS = 1e-5
FEPS = float(np.finfo(np.float32).eps)


class Attn:

    def __init__(self, name, heads_of_group, dim, slot, stride, token_major, rope=False, qk_norm=False,
                 mask=None, gated=False, double_ln=False):
        self.name, self.hg, self.dim, self.slot, self.stride = name, heads_of_group, dim, slot, stride
        self.ng = 12 // heads_of_group
        self.fq = heads_of_group * dim
        self.fv = heads_of_group * slot
        self.rows = heads_of_group * stride
        self.tm, self.rope, self.qk_norm = token_major, rope, qk_norm
        self.mask, self.gated, self.double_ln = mask, gated, double_ln
        self.v0 = self.ng * 2 * self.fq
        self.width = self.v0 + self.ng * self.fv
        self.vparts = self.ng * self.fv // 384
        self.vpieces = 4 * self.vparts
        self.units = 2 * self.ng
        self.scale = float(dim) ** -0.5


class Moe:

    def __init__(self, name, slots, chunks, up, act, experts, topk, owner):
        self.name, self.slots, self.chunks, self.up, self.act = name, slots, chunks, up, act
        self.experts, self.topk, self.owner = experts, topk, owner
        self.units = slots * chunks * 2
        self.width = chunks * 128 * (2 if up else 1)

    def expert(self, s, m):
        return self.owner[s * self.chunks + m]

    def first(self, s, m):
        n = s * self.chunks + m
        return n == 0 or self.owner[n - 1] != self.owner[n]

    def last(self, s, m):
        n = s * self.chunks + m
        return n == len(self.owner) - 1 or self.owner[n + 1] != self.owner[n]


A0 = Attn("l0a", 3, 16, 32, N, True, rope=True, mask="causal")
A1 = Attn("l1f", 2, 64, 64, VW, True, qk_norm=True, gated=True)
A2 = Attn("l2a", 2, 64, 64, N, False, double_ln=True)
A3 = Attn("l3a", 3, 16, 32, N, False, mask="band")
ATTNS = [A0, A1, A2, A3]
M0 = Moe("l0f", 8, 4, True, ACT.Silu, 8, 1, [s for s in range(8) for _ in range(4)])
M2 = Moe("l2f", 9, 3, True, ACT.Silu, 8, 2, [s for s in range(9) for _ in range(3)])
M3 = Moe("l3f", 6, 4, False, ACT.Gelu_apprx_tanh, 16, 8,
         list(range(8)) + [8 + e for e in range(8) for _ in range(2)])
MOES = [M0, M2, M3]
UNIT0 = {a.name: sum(x.units for x in ATTNS[:i]) for i, a in enumerate(ATTNS)}
TM0 = {A0.name: 0, A1.name: A0.units}
V0 = {a.name: sum(2 * x.vpieces for x in ATTNS[:i]) for i, a in enumerate(ATTNS)}
MU0 = {m.name: sum(x.units for x in MOES[:i]) for i, m in enumerate(MOES)}
MS0 = {m.name: sum(x.slots for x in MOES[:i]) for i, m in enumerate(MOES)}
SG0 = {M0.name: 0, M2.name: M0.units}
MD0 = {}
_d = 0
for _m in MOES:
    MD0[_m.name] = _d
    _d += 2 * len(set(_m.owner))
RING = 2
WG_ = 1024
GRP = 14
STAGES = [("attn", A0), ("moe", M0), ("grid", None), ("attn", A1), ("attn", A2), ("moe", M2), ("attn", A3), ("moe", M3)]
XT0_N = [2 * sum(1 for k, a in STAGES[:i] if k != "attn" or a.tm) for i in range(len(STAGES))]
PADDED = [A0, A1, A3]
ROUTER = {"l0f": (0, 8), "l2f": (2, 8), "l3f": (3, 16)}
XV_N = {"l0a": 0, "l1f": 1, "l2a": 2, "l3a": 3}
CONSTS = ["ident", "mh", "rope", "masks", "posb", "bias", "gb", "qn", "ebias", "wr0", "wr1", "wr2", "wr3"]


def pieces(a, i):
    n = 4 if a.tm else 3
    return range(a.vpieces * (i - 1) // n, a.vpieces * i // n) if 1 <= i <= n else ()


def owner_index(m, s, ch):
    return m.owner[s * m.chunks + ch]


def units_before(slot):
    n = 0
    for m in MOES:
        k = min(slot, m.slots)
        n += k * m.chunks * 2
        slot -= k
    return n


def bass_vit_tower(nc, t, out):
    with ExitStack() as ctx:
        def sb(name, shape, dt=F32):
            return ctx.enter_context(nc.sbuf_tensor(name, shape, dt))

        def sem(name):
            return ctx.enter_context(nc.semaphore(name))

        PS = ctx.enter_context(nc.psum_tensor("PS", [128, 8, 512], F32))
        PSF = PS[:, :, :].rearrange("p b n -> p (b n)")

        OB = PS[:, 6:8, 0:HN // 2]

        def YB(g):
            return PS[0:TP, (4, 4, 5, 6, 6, 7)[g], (g % TAU % 2) * C:(g % TAU % 2 + 1) * C]

        def PB(g):
            return PS[0:TP, (0, 0, 1, 2, 2, 3)[g], (g % TAU % 2) * C:(g % TAU % 2 + 1) * C]

        H = sb("H", [TP, NG, C])
        XN = sb("XN", [TP, NG, 256])
        XT = sb("XT", [128, NC_, B * N])
        ACC = sb("ACC", [TP, NG, C])
        BIG = sb("BIG", [128, TOKF * B * N])
        OT = sb("OT", [128, 6 * B * N])
        WTOK = OT[:, 0:TOKF * C].rearrange("p (k f) -> p k f", k=TOKF)
        MIX = sb("MIX", [128, NC_ * B * VW])
        XV = MIX[:, :].rearrange("k (c n) -> k c n", c=NC_)
        st = sb("st", [TP, NG, 6])
        mv = sb("mv", [TP, NG, 2])
        var = sb("var", [TP, NG])
        rstd = sb("rstd", [TP, NG])
        cst = sb("cst", [128, 128])
        mh = sb("mh", [128, 6])
        nhalf = sb("nhalf", [128, 16])
        tri = sb("tri", [128, 16, 16])
        rope = sb("rope", [TP, 2, TAU, 96])
        masks = sb("masks", [108, 2, N])
        posb = sb("posb", [TP, TAU, C])
        bias = sb("bias", [TP, 6, C])
        gb = sb("gb", [128, 4])
        qn = sb("qn", [128, 4])
        qs = sb("qs", [128, 4])
        ebias = sb("ebias", [TP, 8])
        wr = [sb(f"wr{i}", [128, NC_, e]) for i, e in enumerate((8, GRP, 8, 16))]
        wqkv = {a.name: sb("wqkv_" + a.name, [128, NC_, a.width]) for a in (A0, A1)}
        wp = {a.name: sb("wp_" + a.name, [a.fv, a.ng, C]) for a in (A0, A1, A2)}
        wqkv["l3a"], wp["l3a"] = wqkv["l0a"], wp["l0a"]
        wqkv["l2a"] = wqkv["l1f"]
        wg = sb("wg", [128, NC_, 3 * C])
        wgp = sb("wgp", [64, 3, C])
        RG = [sb(f"RG{r}", [128, NC_, WG_]) for r in range(RING)]
        RD = [sb(f"RD{r}", [128, 4 * C]) for r in range(RING)]
        ACCB = MIX[0:TP, 4 * HN:4 * HN + NG * C // 2].bitcast(BF16).rearrange("p (g f) -> p g f", g=NG)
        SG = [MIX[:, r * HN:(r + 1) * HN] for r in range(2)]
        AF = [MIX[:, r * HN:(r + 1) * HN] for r in range(2, 4)]
        T2 = ACC[:, 0:4, :].rearrange("p g f -> p (g f)")
        sm = sb("sm", [128, 4, HB])
        ssq = sb("ssq", [TP, 3, 12])
        cw = sb("cw", [128, NC_ * 24])
        R1, R2 = BIG[:, 0:1600], BIG[:, 1600:3200]
        rl = sb("rl", [128, 4, 16 * 16])
        rs = sb("rs", [128, 8, 16])
        GH = sb("GH", [128, 6, 16])
        comb = [sb(f"comb{i}", [TP, NG, e]) for i, e in enumerate((8, 9, 16))]
        maxp = sb("maxp", [TP, NG])
        top8 = sb("top8", [TP, NG, 8])
        sg1 = sb("sg1", [TP, 3, 216])

        with ExitStack() as place:
            def sb1(name, shape, dt=F32):
                return place.enter_context(nc.sbuf_tensor(name, shape, dt))
            QB = [sb1(f"QB{r}", [128, HB, 128]) for r in range(2)]
            KS = [sb1(f"KS{r}", [128, HN]) for r in range(2)]
            VS = sb1("VS", [128, HB, 768])
            ES = [sb1(f"ES{r}", [128, HN]) for r in range(2)]
            PN = [sb1(f"PN{r}", [128, HB, VW]) for r in range(2)]
            PT = [sb1(f"PT{r}", [128, 512]) for r in range(2)]
            TX = [sb1(f"TX{r}", [TP, TAU * 256]) for r in range(2)]
        F32R = mybir.dt.float32r
        XH = sb("XH", [128, B * N], F32R)
        XL = sb("XL", [128, B * N], F32R)
        X1 = sb("X1", [128, B * N], F32R)
        X1T = sb("X1T", [128, B * N], F32R)
        WH = [sb(f"WH{r}", [128, NC_, WG_], F32R) for r in range(RING)]
        WL = [sb(f"WL{r}", [128, NC_, WG_], F32R) for r in range(RING)]
        DH = [sb(f"DH{r}", [128, 4 * C], F32R) for r in range(RING)]
        DL = [sb(f"DL{r}", [128, 4 * C], F32R) for r in range(RING)]
        AH = [sb(f"AH{r}", [128, HN], F32R) for r in range(3)]
        AL = [sb(f"AL{r}", [128, HN], F32R) for r in range(3)]

        S = {n: sem(n) for n in (
            "in_const", "wslot0", "wslot1", "out_written",
            "setup_pool", "setup_dve", "patch_summed", "pads",
            "ln_stats", "ln_rstd", "ln_normed", "ln_third", "ln_turned", "xt0_ready", "xt1_ready", "xv0_ready", "xv1_ready",
            "x_high", "x_split",
            "tm_ready", "tm_square", "tm_sum", "tm_rstd", "tm_done", "qk_ready", "q_sb", "k_sb", "v_ready", "v_sb",
            "s_ready", "s_taken", "e_ready", "p_sb", "pt_ready", "pt_sb", "o_ready", "o_sb", "y_ready",
            "bias_added",
            "logits", "r_shift", "r_exp", "r_done",
            "g_ready", "sg_ready", "a_ready", "ah_hi", "ah_lo", "w3_done", "drained", "w_hi", "w_lo", "w_lo1",
            "grid_ready", "grid_sb", "grid_s", "grid_e", "grid_o", "grid_turned", "grid_osb",
            "dve_step", "pool_step", "act_step",
        )}
        in_att = {n: sem("in_att_" + n) for n in ("l0a", "grid", "l1f", "l2a", "l3a")}
        in_patch = [sem(f"in_patch{k}") for k in range(TOKF)]
        wslot = [S["wslot0"], S["wslot1"]]

        GQ = BIG[0:TP, :]
        GO = XN[:, :, :].rearrange("p g f -> p (g f)")
        GT = OT[0:64, 9 * C:18 * C]
        consts = [(dst[tuple(slice(None) for _ in dst.shape)], t[n]) for dst, n in zip(
            [cst, mh, rope, masks, posb, bias, gb, qn, ebias, *wr], CONSTS)]

        def xt_copy(copy, c, j, grid):
            k, cols = CR[c], slice(HN * j, HN * (j + 1))
            if grid:
                for tau in range(TAU):
                    o = XT[0:k, c, cols].rearrange("k (s b m t) -> k t b s m", s=3, b=HB, t=TAU)[:, tau]
                    i = PS[0:k, 4 + 2 * j + c, tau * TP:(tau + 1) * TP].rearrange("k (b s m) -> k b s m", b=HB, s=3)
                    last = copy(o, i)
                return last
            return copy(by_token(XT[0:k, c, cols]), turned(j, c, 0, k))

        def by_token(ap):
            return ap.rearrange("k (p t) -> k t p", t=TAU)

        def turned(j, c, lo, hi):
            return PS[lo:hi, 4 + 2 * j + c, 0:HN].rearrange("k (t p) -> k t p", t=TAU)

        def xv_half(c, j, rows):
            return XV[0:rows, c, :].rearrange("k (b n) -> k b n", b=B)[:, HB * j:HB * (j + 1), 0:N]

        block = ctx.enter_context(nc.Block())

        def tile(ap2, j, tau, width=TP):
            return ap2[:, HN * j + tau:HN * (j + 1):TAU]

        @block.sync
        def _(sp):
            for k in range(TOKF):
                sp.dma_start(WTOK[:, k, :], t["wtok"][:, k, :]).then_inc(in_patch[k], 16)
                sp.dma_start(BIG[:, k * B * N:(k + 1) * B * N], t["patch"][:, k, :]).then_inc(in_patch[k], 16)

            def qkv(a):
                for c in range(NC_):
                    sp.dma_start(wqkv[a.name][0:CB[c], c, :], t[f"wqkv_{a.name}_{c}"]).then_inc(in_att[a.name], 16)

            def proj(a):
                sp.dma_start(wp[a.name][:, :, :], t["wp_" + a.name]).then_inc(in_att[a.name], 16)

            def slots(m, lo, hi):
                w = m.width
                for s in range(lo, hi):
                    n = MS0[m.name] + s
                    if n >= RING:
                        sp.wait_ge(S["w_hi"], 3 * (n - 1))
                        sp.wait_ge(S["w_lo"], 2 * (n - 1))
                        sp.wait_ge(S["w_lo1"], n - 1)
                    r, arrived = n % RING, wslot[n % RING]
                    sp.dma_start(RG[r][:, 0, 0:w], t["gu_" + m.name][s, 0:128]).then_inc(arrived, 16)
                    for half in (0, 64):
                        sp.dma_start(RG[r][half:half + 64, 1, 0:w], t["gu_" + m.name][s, 128:C]).then_inc(arrived, 16)
                    sp.dma_start(RD[r][:, 0:m.chunks * C], t["wd_" + m.name][s]).then_inc(arrived, 16)

            qkv(A0)
            proj(A0)
            slots(M0, 0, RING)
            for c in range(NC_):
                sp.dma_start(wg[0:CR[c], c, :], t[f"wg_{c}"]).then_inc(in_att["grid"], 16)
            sp.dma_start(wgp[:, :, :], t["wgp"]).then_inc(in_att["grid"], 16)
            qkv(A1)
            proj(A1)
            proj(A2)
            slots(M0, RING, M0.slots)
            slots(M2, 0, RING)
            sp.wait_ge(S["y_ready"], 2)
            qkv(A3)
            proj(A3)
            sp.wait_ge(S["v_ready"], V0["l2a"])
            sp.wait_ge(S["tm_ready"], TM0["l1f"] + A1.units)
            qkv(A2)
            slots(M2, RING, M2.slots)
            slots(M3, 0, M3.slots)
            for j in range(2):
                sp.wait_ge(S["drained"], MD0[M3.name] + 2 * M3.experts - 1 + j)
                sp.dma_start(out.rearrange("b n f -> (b n) f").rearrange("(j p t) f -> j p (t f)", j=2, t=TAU)[j],
                             H[:, TAU * j:TAU * (j + 1), :].rearrange("p t f -> p (t f)")).then_inc(S["out_written"], 16)
            sp.wait_ge(S["out_written"], 32)



        @block.tensor
        def _(pe):
            mm, tr = nc.tensor.matmul, nc.tensor.transpose

            def turn(k, j, moe=False):
                for tau in range(TAU):
                    if tau == 0:
                        pe.wait_ge(S["ln_normed"], 2 * k + j + 1)
                    if tau == TAU - 1:
                        pe.wait_ge(S["ln_third"], 2 * k + j + 1)
                    for c in range(NC_):
                        k_ = 128 if moe else CR[c]
                        last = tr(PS[0:k_, 4 + 2 * j + c, tau * TP:(tau + 1) * TP],
                                  XN[:, TAU * j + tau, c * 128:c * 128 + k_], cst[0:TP, 0:TP])
                last.then_inc(S["ln_turned"], 1)

            def wait_xt(k, j):
                pe.wait_ge(S["xt0_ready"], XT0_N[k] + j + 1)
                pe.wait_ge(S["xt1_ready"], 2 * k + j + 1)

            def wait_xv(a, j):
                pe.wait_ge(S["xv0_ready"], 2 * XV_N[a.name] + j + 1)
                pe.wait_ge(S["xv1_ready"], 2 * XV_N[a.name] + j + 1)

            def router(i, e, stage):
                wait_xt(stage, 1)
                for g in range(NG):
                    for c in range(NC_):
                        last = mm(PS[0:TP, 7, g * e:(g + 1) * e], tile(XT[0:CB[c], c, 0:B * N], g // TAU, g % TAU),
                                  wr[i][0:CB[c], c, :], start=(c == 0), stop=(c == NC_ - 1))
                last.then_inc(S["logits"], 1)

            def moe(m, stage):
                u0 = MU0[m.name]

                def hidden(u):
                    s, ch, j = u // (2 * m.chunks), u // 2 % m.chunks, u % 2
                    n, U = MS0[m.name] + s, u0 + u
                    r, cols = n % RING, slice(HN * j, HN * (j + 1))
                    if ch == 0 and j == 0:
                        pe.wait_ge(S["w_lo"], 2 * n + 1)
                        pe.wait_ge(S["w_lo1"], n + 1)
                    if u < 2:
                        pe.wait_ge(S["x_split"], 2 * MOES.index(m) + j + 1)
                    if U >= 2:
                        pe.wait_ge(S["a_ready"], U - 1)
                    for k in range(2 if m.up else 1):
                        o = PS[:, 2 * k + u % 2, 0:HN]
                        w = slice((k * m.chunks + ch) * 128, (k * m.chunks + ch + 1) * 128)
                        mm(o, WH[r][:, 0, w], XH[:, cols], start=True, stop=False)
                        mm(o, WH[r][:, 0, w], XL[:, cols], start=False, stop=False)
                        mm(o, WL[r][:, 0, w], XH[:, cols], start=False, stop=False)
                        mm(o, WH[r][:, 1, w], X1[:, cols], start=False, stop=False)
                        last = mm(o, WL[r][0:64, 1, w], X1[0:64, cols], start=False, stop=True)
                    last.then_inc(S["g_ready"], 1)

                def down(u):
                    s, ch, j = u // (2 * m.chunks), u // 2 % m.chunks, u % 2
                    n, U = MS0[m.name] + s, u0 + u
                    pe.wait_ge(S["ah_lo"], U + 1)
                    if ch == 0 and j == 0:
                        pe.wait_ge(S["w_lo"], 2 * n + 2)
                    if u == 1:
                        pe.wait_ge(S["r_shift"], ROUTER[m.name][0] + 1)
                    if m.first(s, ch):
                        d = MD0[m.name] + 2 * owner_index(m, s, ch) - 2 + j
                        if d >= 0:
                            pe.wait_ge(S["drained"], d + 1)
                    for tau in range(TAU):
                        g = TAU * j + tau
                        w = slice(ch * C, (ch + 1) * C)
                        first = m.first(s, ch) and tau != 1
                        hi, lo = AH[U % 3][:, tau:HN:TAU], AL[U % 3][:, tau:HN:TAU]
                        mm(YB(g), hi, DH[n % RING][:, w], start=first, stop=False, skip_group_check=True)
                        mm(YB(g), hi, DL[n % RING][:, w], start=False, stop=False, skip_group_check=True)
                        last = mm(YB(g), lo, DH[n % RING][:, w], start=False, stop=m.last(s, ch), skip_group_check=True)
                    last.then_inc(S["w3_done"], 1)

                turn(stage, 0, True)
                for u in range(m.units + 2):
                    if u == 1:
                        turn(stage, 1, True)
                    if u < m.units:
                        hidden(u)
                    if u == 1:
                        router(*ROUTER[m.name], stage)
                    if u >= 2:
                        down(u - 2)

            def attention(a, stage):
                u0 = UNIT0[a.name]
                W, P2 = wqkv[a.name], wp[a.name]
                def gate_logits():
                    wait_xv(a, 1)
                    pe.wait_ge(S["v_sb"], V0[a.name] + a.vpieces)
                    for i in range(HB):
                        for c in range(NC_):
                            last = mm(PS[:, 4, i * GRP:(i + 1) * GRP], XV[0:CB[c], c, 2 * i * VW:2 * (i + 1) * VW],
                                      wr[1][0:CB[c], c, :], start=(c == 0), stop=(c == NC_ - 1))
                    last.then_inc(S["logits"], 1)

                def token_major(u):
                    g, j = u // 2, u % 2
                    if u >= 1:
                        pe.wait_ge(S["tm_done"], TM0[a.name] + u)
                    if g == 0:
                        wait_xt(stage, j)
                    for tau in range(TAU):
                        for c in range(NC_):
                            last = mm(PSF[0:TP, 1024 + tau * 2 * a.fq:1024 + (tau + 1) * 2 * a.fq],
                                      tile(XT[0:CB[c], c, 0:B * N], j, tau),
                                      W[0:CB[c], c, g * 2 * a.fq:(g + 1) * 2 * a.fq],
                                      start=(c == 0), stop=(c == NC_ - 1))
                    last.then_inc(S["tm_ready"], 1)

                def qk(u):
                    g, j = u // 2, u % 2
                    U = u0 + u
                    if a.tm:
                        pe.wait_ge(S["tm_done"], TM0[a.name] + u + 1)
                    if u >= 1:
                        pe.wait_ge(S["q_sb"], U)
                        pe.wait_ge(S["k_sb"], U)
                    for k in range(2):
                        if a.tm:
                            for tau in range(TAU):
                                last = tr(PS[0:a.fq, k, tau * TP:(tau + 1) * TP],
                                          TX[u % 2][:, (2 * tau + k) * a.fq:(2 * tau + k + 1) * a.fq],
                                          cst[0:TP, 0:TP])
                        else:
                            for c in range(NC_):
                                off = (2 * g + k) * a.fq
                                last = mm(PS[0:a.fq, k, 0:HN].rearrange("f (b n) -> f b n", b=HB), W[0:CB[c], c, off:off + a.fq],
                                          xv_half(c, j, CB[c]), start=(c == 0), stop=(c == NC_ - 1))
                    last.then_inc(S["qk_ready"], 1)

                def values(j, p):
                    pair, part = 4 * j + p // a.vparts, p % a.vparts
                    wait_xv(a, j)
                    if p >= 2:
                        pe.wait_ge(S["v_sb"], V0[a.name] + j * a.vpieces + p - 1)
                    for c in range(NC_):
                        last = mm(PS[:, 4 + 2 * j + p % 2, 0:384], XV[0:CB[c], c, 2 * pair * VW:2 * (pair + 1) * VW],
                                  W[0:CB[c], c, a.v0 + 384 * part:a.v0 + 384 * (part + 1)],
                                  start=(c == 0), stop=(c == NC_ - 1))
                    last.then_inc(S["v_ready"], 1)

                def scores(u):
                    U = u0 + u
                    pe.wait_ge(S["q_sb"], U + 1)
                    pe.wait_ge(S["k_sb"], U + 1)
                    if u == 0:
                        pe.wait_ge(S["v_sb"], V0[a.name] + a.vpieces)
                    if u >= 1:
                        pe.wait_ge(S["s_taken"], U)
                    for b in range(HB):
                        last = mm(PS[0:a.rows, 5, b * N:(b + 1) * N], QB[u % 2][0:a.fq, b, 0:a.rows],
                                  KS[u % 2][0:a.fq, b * N:(b + 1) * N], start=True, stop=True)
                    last.then_inc(S["s_ready"], 1)

                def turn_probs(u):
                    U = u0 + u
                    pe.wait_ge(S["p_sb"], U + 1)
                    if u >= 1:
                        pe.wait_ge(S["pt_sb"], U)
                    for i in range(HB // 2):
                        last = tr(PS[:, 4, i * 128:i * 128 + a.rows], PN[u % 2][0:a.rows, 2 * i:2 * i + 2, :],
                                  cst[0:a.rows, 0:a.rows])
                    last.then_inc(S["pt_ready"], 1)

                def mix(u):
                    U = u0 + u
                    pe.wait_ge(S["pt_sb"], U + 1)
                    if u == 0:
                        pe.wait_ge(S["v_sb"], V0[a.name] + 2 * a.vpieces)
                    if u >= 1:
                        pe.wait_ge(S["o_sb"], U)
                    for b in range(HB):
                        i, r = b // 2, VW * (b % 2)
                        for h in range(a.hg):
                            last = mm(OB[a.slot * h:a.slot * (h + 1), b % 2, i * N:(i + 1) * N],
                                      VS[r:r + N, 4 * (u % 2) + i, (u // 2) * a.fv + h * a.slot:(u // 2) * a.fv + (h + 1) * a.slot],
                                      PT[u % 2][r:r + N, i * 128 + h * a.stride:i * 128 + h * a.stride + N],
                                      start=True, stop=True)
                    last.then_inc(S["o_ready"], 1)

                def output(tiles, groups):
                    for t6 in tiles:
                        for g in groups:
                            last = mm(PB(t6), tile(OT[0:a.fv, g * B * N:(g + 1) * B * N], t6 // TAU, t6 % TAU), P2[:, g, :],
                                      start=(g == 0 and t6 % TAU != 1), stop=(g == a.ng - 1), skip_group_check=True)
                    return last

                lag = 1 if a.tm else 0
                turn(stage, 0)
                pe.wait_ge(in_att[a.name], 48)
                if a.gated:
                    pe.wait_ge(S["setup_dve"], 1)
                for i in range(a.units + lag + 4):
                    if a.tm and i < a.units:
                        token_major(i)
                    if i == 0:
                        for p in range(a.vpieces):
                            if p == 2:
                                turn(stage, 1)
                            values(0, p)
                    for p in pieces(a, i):
                        values(1, p)
                    if 0 <= i - lag < a.units:
                        qk(i - lag)
                    if a.gated and i == 1:
                        gate_logits()
                    if 0 <= i - lag - 1 < a.units:
                        scores(i - lag - 1)
                    if 0 <= i - lag - 3 < a.units:
                        turn_probs(i - lag - 3)
                    late = i - lag - a.units
                    if 0 <= late < 3:
                        pe.wait_ge(S["o_sb"], u0 + a.units - 4)
                        output(range(2 * late, 2 * late + 2), range(a.ng - 2))
                    if late == 3:
                        pe.wait_ge(S["o_sb"], u0 + a.units - 1)
                        output(range(TAU), range(a.ng - 2, a.ng)).then_inc(S["y_ready"], 1)
                    if 0 <= i - lag - 4 < a.units:
                        mix(i - lag - 4)
                pe.wait_ge(S["o_sb"], u0 + a.units)
                output(range(TAU, NG), range(a.ng - 2, a.ng)).then_inc(S["y_ready"], 1)

            def grid_attention(stage):
                turn(stage, 0)
                pe.wait_ge(in_att["grid"], 48)
                for i in range(NG):
                    j, ks = i // TAU, i % TAU
                    if i == 1:
                        turn(stage, 1)
                    if ks == 0:
                        wait_xt(stage, j)
                    if i >= 2:
                        pe.wait_ge(S["grid_sb"], i - 1)
                    for n in range(2):
                        for c in range(NC_):
                            last = mm(PS[0:TP, 2 * (i % 2) + n, 0:288], XT[0:CR[c], c, i * TP:(i + 1) * TP], wg[0:CR[c], c, 288 * n:288 * (n + 1)],
                                      start=(c == 0), stop=(c == NC_ - 1))
                    last.then_inc(S["grid_ready"], 1)
                pe.wait_ge(S["grid_sb"], NG)
                for j in range(2):
                    pe.wait_ge(S["grid_o"], j + 1)
                    for g in range(TAU * j, TAU * (j + 1)):
                        if g >= 2:
                            pe.wait_ge(S["grid_osb"], g - 1)
                        for nd in range(3):
                            o = 4 * C * j + nd * C + 64 * (g % TAU)
                            last = tr(PS[0:64, 4 + g % 2, nd * TP:(nd + 1) * TP], GO[:, o:o + 64], cst[0:TP, 0:TP])
                        last.then_inc(S["grid_turned"], 1)
                    for g in range(TAU * j, TAU * (j + 1)):
                        pe.wait_ge(S["grid_osb"], g + 1)
                        for nd in range(3):
                            last = mm(PB(g), GT[:, (3 * g + nd) * TP:(3 * g + nd + 1) * TP], wgp[:, nd, :],
                                      start=(nd == 0), stop=(nd == 2))
                    last.then_inc(S["y_ready"], 1)

            for k in range(TOKF):
                pe.wait_ge(in_patch[k], 32)
                for g in range(NG):
                    last = mm(PB(g), tile(BIG[:, k * B * N:(k + 1) * B * N], g // TAU, g % TAU), WTOK[:, k, :],
                              start=(k == 0 and g % TAU != 1), stop=(k == TOKF - 1), skip_group_check=True)
                    if k == TOKF - 1 and g % TAU == TAU - 1:
                        last.then_inc(S["patch_summed"], 1)
            pe.wait_ge(S["in_const"], 16 * len(consts))
            pe.wait_ge(S["setup_pool"], 1)
            for i, (kind, arg) in enumerate(STAGES):
                if kind == "moe":
                    moe(arg, i)
                elif kind == "attn":
                    attention(arg, i)
                else:
                    grid_attention(i)

        @block.scalar
        def _(act):
            activation = nc.scalar.activation

            def evac_xt(k, kind, a, j):
                def copy(o, i):
                    if kind == "attn" and a.double_ln:
                        return activation(o, i, ACT.Identity, bias=gb[:, 2:3], scale=gb[:, 0:1])
                    return activation(o, i, ACT.Copy)

                act.wait_ge(S["ln_turned"], 2 * k + j + 1)
                if kind != "attn" or a.tm:
                    xt_copy(copy, 0, j, kind == "grid").then_inc(S["xt0_ready"], 1)
                if kind == "attn":
                    copy(xv_half(0, j, 128).rearrange("k b (m t) -> k t b m", t=TAU),
                         PS[:, 4 + 2 * j, 0:HN].rearrange("k (t b m) -> k t b m", t=TAU, b=HB)).then_inc(S["xv0_ready"], 1)
                if kind == "moe":
                    copy(by_token(XH[:, HN * j:HN * (j + 1)]), turned(j, 0, 0, 128)).then_inc(S["x_high"], 1)

            def split_high(m, s, part):
                n = MS0[m.name] + s
                r = n % RING
                if part == 0:
                    act.wait_ge(wslot[r], 64 * (n // RING + 1))
                    if s >= RING:
                        act.wait_ge(S["w3_done"], units_before(n - RING + 1))
                if part < 2:
                    o, i = WH[r][:, part, 0:m.width], RG[r][:, part, 0:m.width]
                else:
                    o, i = DH[r][:, 0:m.chunks * C], RD[r][:, 0:m.chunks * C]
                activation(o, i, ACT.Copy).then_inc(S["w_hi"], 1)

            def moe(m):
                for u in range(m.units):
                    U = MU0[m.name] + u
                    act.wait_ge(S["g_ready"], U + 1)
                    if m.up:
                        if SG0[m.name] + u >= 2:
                            act.wait_ge(S["a_ready"], U - 1)
                        activation(SG[u % 2][:, :], PS[:, u % 2, 0:HN], m.act).then_inc(S["sg_ready"], 1)
                    else:
                        act.wait_ge(S["ah_lo"], U - 1)
                        activation(AF[U % 2][:, :], PS[:, u % 2, 0:HN], m.act).then_inc(S["a_ready"], 1)
                    if u == 1:
                        router_exp(ROUTER[m.name][0], NG * m.experts, TP)
                    s = u // (2 * m.chunks)
                    part = u % (2 * m.chunks) - 2
                    if 0 <= part < 3 and s + 1 < m.slots:
                        split_high(m, s + 1, part)

            def router_exp(i, w, rows):
                act.wait_ge(S["r_shift"], i + 1)
                activation(rl[0:rows, 1, 0:w], rl[0:rows, 0, 0:w], ACT.Exp).then_inc(S["r_exp"], 1)

            def attention(a, stage):
                u0 = UNIT0[a.name]

                def keys(u):
                    U = u0 + u
                    act.wait_ge(S["qk_ready"], U + 1)
                    if U >= 2:
                        act.wait_ge(S["s_ready"], U - 1)
                    if a.tm:
                        o = KS[u % 2][0:a.fq, :].rearrange("f (p t) -> f t p", t=TAU)
                        i = PS[0:a.fq, 1, 0:HN].rearrange("f (t p) -> f t p", t=TAU)
                    else:
                        o, i = KS[u % 2][0:a.fq, :], PS[0:a.fq, 1, 0:HN]
                    if a.qk_norm:
                        activation(o, i, ACT.Identity, bias=qn[:, 3:4], scale=qn[:, 2:3]).then_inc(S["k_sb"], 1)
                    else:
                        activation(o, i, ACT.Copy).then_inc(S["k_sb"], 1)

                def vals(j, p):
                    act.wait_ge(S["v_ready"], V0[a.name] + j * a.vpieces + p + 1)
                    o = 384 * (p % a.vparts)
                    activation(VS[:, 4 * j + p // a.vparts, o:o + 384], PS[:, 4 + 2 * j + p % 2, 0:384],
                               ACT.Copy).then_inc(S["v_sb"], 1)

                def exps(u):
                    U = u0 + u
                    act.wait_ge(S["s_taken"], U + 1)
                    e = ES[u % 2][0:a.rows, :]
                    activation(e, e, ACT.Exp).then_inc(S["e_ready"], 1)

                def probs_turned(u):
                    U = u0 + u
                    act.wait_ge(S["pt_ready"], U + 1)
                    if U >= 2:
                        act.wait_ge(S["o_ready"], U - 1)
                    view = lambda x: x.rearrange("p (i r) -> p i r", i=4)[:, :, 0:a.rows]
                    activation(view(PT[u % 2][:, :]), view(PS[:, 4, :]), ACT.Copy).then_inc(S["pt_sb"], 1)

                def outs(u):
                    U = u0 + u
                    act.wait_ge(S["o_ready"], U + 1)
                    o = (u // 2) * B * N + HN * (u % 2)
                    activation(OT[0:a.fv, o:o + HN].rearrange("f (i r n) -> f r i n", i=4, r=2),
                               OB[0:a.fv, :, :].rearrange("f r (i n) -> f r i n", i=4), ACT.Copy).then_inc(S["o_sb"], 1)

                def square(u):
                    n = u + 1
                    act.wait_ge(S["tm_ready"], TM0[a.name] + n)
                    if u >= 1:
                        act.wait_ge(S["tm_sum"], u)
                    activation(T2[:, :], PSF[0:TP, 1024:1024 + TAU * 256], ACT.Square).then_inc(S["tm_square"], 1)

                lag = 1 if a.tm else 0
                for i in range(a.units + lag + 4):
                    if a.qk_norm and i < a.units:
                        square(i)
                    if i == 0:
                        for p in range(a.vpieces):
                            if p == 2:
                                evac_xt(stage, "attn", a, 1)
                            vals(0, p)
                    for p in pieces(a, i):
                        vals(1, p)
                    if 0 <= i - lag < a.units:
                        keys(i - lag)
                    if 0 <= i - lag - 1 < a.units:
                        exps(i - lag - 1)
                    if a.gated and i == lag + 2:
                        router_exp(1, HB * GRP, 128)
                    if 0 <= i - lag - 3 < a.units:
                        probs_turned(i - lag - 3)
                    if 0 <= i - lag - 4 < a.units:
                        outs(i - lag - 4)

            def grid_attention():
                for i in range(0, NG):
                    act.wait_ge(S["grid_ready"], i + 1)
                    activation(GQ[:, i * 576:(i + 1) * 576].rearrange("p (n w) -> p n w", n=2),
                               PS[0:TP, 2 * (i % 2):2 * (i % 2) + 2, 0:288], ACT.Copy).then_inc(S["grid_sb"], 1)
                for j in range(2):
                    act.wait_ge(S["grid_s"], j + 1)
                    e = sg1[:, 1, 0:108]
                    activation(e, e, ACT.Exp, scale=0.25).then_inc(S["grid_e"], 1)
                for g in range(NG):
                    act.wait_ge(S["grid_turned"], g + 1)
                    activation(GT[:, 3 * g * TP:3 * (g + 1) * TP], PS[0:64, 4 + g % 2, 0:3 * TP],
                               ACT.Copy).then_inc(S["grid_osb"], 1)

            for dst, src in consts:
                nc.scalar.dma_start(dst, src).then_inc(S["in_const"], 16)
            act.wait_ge(S["in_const"], 16 * len(consts))
            y = 0
            for i, (kind, arg) in enumerate(STAGES):
                if kind == "moe":
                    for part in range(3):
                        split_high(arg, 0, part)
                else:
                    y += 1
                evac_xt(i, kind, arg, 0)
                if kind == "attn":
                    attention(arg, i)
                    continue
                evac_xt(i, kind, arg, 1)
                if kind == "moe":
                    moe(arg)
                else:
                    grid_attention()

        @block.vector
        def _(dve):
            V = nc.vector
            count = [0]

            def link(ins):
                count[0] += 1
                ins.then_inc(S["dve_step"], 1)
                dve.wait_ge(S["dve_step"], count[0])

            def statistics(n, src, j):
                gs = range(TAU * j, TAU * (j + 1))
                for g in gs:
                    last = V.bn_stats(st[:, g, :], src[:, g, 0:C])
                link(last)
                for g in gs:
                    last = V.bn_aggr(mv[:, g, :], st[:, g, :])
                link(last)
                V.tensor_scalar(var[:, TAU * j:TAU * (j + 1)], mv[:, TAU * j:TAU * (j + 1), 1], EPS, None,
                                ALU.add).then_inc(S["ln_stats"], 1)

            def normalised(n, src, j, tiles, moe):
                dve.wait_ge(S["ln_rstd"], n + 1)
                for g in range(TAU * j, TAU * j + tiles):
                    last = V.tensor_scalar(XN[:, g, 0:C], src[:, g, 0:C], mv[:, g, 0:1], rstd[:, g:g + 1],
                                           ALU.subtract, ALU.mult)
                    if moe:
                        last = V.tensor_scalar(XN[:, g, C:], src[:, g, 128:C], mv[:, g, 0:1], rstd[:, g:g + 1],
                                               ALU.subtract, ALU.mult)
                return last

            def evac_xt(k, kind, a, j):
                def copy(o, i):
                    if kind == "attn" and a.double_ln:
                        return V.tensor_scalar(o, i, gb[0:64, 1:2], gb[0:64, 3:4], ALU.mult, ALU.add)
                    return V.tensor_copy(o, i)

                dve.wait_ge(S["ln_turned"], 2 * k + j + 1)
                xt_copy(copy, 1, j, kind == "grid").then_inc(S["xt1_ready"], 1)
                if kind == "attn":
                    dve.wait_ge(S["xt1_ready"], 2 * k + j + 1)
                    V.tensor_copy(xv_half(1, j, CB[1]), XT[0:CB[1], 1, HN * j:HN * (j + 1)].rearrange("k (b n) -> k b n", b=HB)
                                  ).then_inc(S["xv1_ready"], 1)

            def prepare(k, kind, a, first_pass, prev):
                passes = 2 if kind == "attn" and a.double_ln else 1
                for j in range(2):
                    n = first_pass + passes * j
                    stream(prev, j)
                    if passes == 2:
                        statistics(n, H, j)
                        link(normalised(n, H, j, TAU, False))
                        n += 1
                    src = XN if passes == 2 else H
                    statistics(n, src, j)
                    if j == 1:
                        finish(k, kind, a, 0)
                    normalised(n, src, j, TAU - 1, kind == "moe").then_inc(S["ln_normed"], 1)
                    if kind == "moe" and j == 0:
                        split_low1(a, 0)
                finish(k, kind, a, 1)

            def finish(k, kind, a, j):
                evac_xt(k, kind, a, j)
                if kind == "moe":
                    split_stream(k, MOES.index(a), j)

            def split_low1(m, s):
                n = MS0[m.name] + s
                r = n % RING
                dve.wait_ge(S["w_hi"], 3 * n + 2)
                V.tensor_tensor(WL[r][0:64, 1, 0:m.width], RG[r][0:64, 1, 0:m.width],
                                WH[r][0:64, 1, 0:m.width].bitcast(F32), ALU.subtract).then_inc(S["w_lo1"], 1)

            def split_stream(k, m, j):
                cols = slice(HN * j, HN * (j + 1))
                V.tensor_copy(by_token(X1[0:64, cols]), turned(j, 1, 0, 64))
                link(V.tensor_copy(by_token(X1T[64:128, cols]), turned(j, 1, 64, 128)))
                V.tensor_tensor(by_token(X1[64:128, cols]), turned(j, 1, 64, 128), by_token(X1T[64:128, cols].bitcast(F32)),
                                ALU.subtract)
                dve.wait_ge(S["xt0_ready"], XT0_N[k] + j + 1)
                dve.wait_ge(S["x_high"], 2 * m + j + 1)
                V.tensor_tensor(XL[:, cols], XT[:, 0, cols], XH[:, cols].bitcast(F32), ALU.subtract).then_inc(S["x_split"], 1)

            def softmax(rows, w, parts, logits, add=None):
                G = w[0]
                view = lambda k, o, n: rl[0:rows, k, 0:G * w[1]].rearrange("p (g e) -> p g e", g=G)[:, :, o:o + n]
                for n_, (o, n) in enumerate(parts):
                    link(V.tensor_reduce(rs[0:rows, n_, 0:G], logits[:, :, o:o + n], X, ALU.max))
                    last = V.tensor_tensor(view(0, o, n), logits[:, :, o:o + n],
                                           rs[0:rows, n_, 0:G].unsqueeze(2).to_broadcast([rows, G, n]), ALU.subtract)
                return last, view

            def normalise(rows, w, parts, view, r):
                dve.wait_ge(S["r_exp"], r + 1)
                G = w[0]
                for n_, (o, n) in enumerate(parts):
                    link(V.tensor_reduce(rs[0:rows, n_, 0:G], view(1, o, n), X, ALU.add))
                    link(V.reciprocal(rs[0:rows, n_, 0:G], rs[0:rows, n_, 0:G]))
                    link(V.tensor_tensor(view(2, o, n), view(1, o, n),
                                         rs[0:rows, n_, 0:G].unsqueeze(2).to_broadcast([rows, G, n]), ALU.mult))

            def top_mask(dst, sel, rows, G, E, k):
                cube = [rows, G, E, E]
                r1 = R1[0:rows, 0:G * E * E].rearrange("p (g e f) -> p g e f", g=G, e=E)
                r2 = R2[0:rows, 0:G * E * E].rearrange("p (g e f) -> p g e f", g=G, e=E)
                other = sel.unsqueeze(2).to_broadcast(cube)
                own = sel.unsqueeze(3).to_broadcast(cube)
                V.tensor_tensor(r1, other, own, ALU.is_gt)
                link(V.tensor_tensor(r2, other, own, ALU.is_equal))
                link(V.tensor_tensor(r2, r2, tri[0:rows, 0:E, 0:E].unsqueeze(1).to_broadcast(cube), ALU.mult))
                link(V.tensor_tensor(r1, r1, r2, ALU.add))
                link(V.tensor_reduce(dst, r1, X, ALU.add))
                link(V.tensor_scalar(dst, dst, float(k), None, ALU.is_lt))

            def router(m, i):
                r, e = ROUTER[m.name]
                w = (NG, e)
                dve.wait_ge(S["logits"], r + 1)
                logits = PS[0:TP, 7, 0:NG * e].rearrange("p (g e) -> p g e", g=NG)
                last, view = softmax(TP, w, [(0, e)], logits)
                last.then_inc(S["r_shift"], 1)
                normalise(TP, w, [(0, e)], view, r)
                probs = view(2, 0, e)
                mask = view(3, 0, e)
                sel = probs
                if m is M2:
                    sel = view(0, 0, e)
                    link(V.tensor_tensor(sel, probs, ebias[:, :].unsqueeze(1).to_broadcast([TP, NG, e]), ALU.add))
                if m is M3:
                    for g in range(NG):
                        last = V.max(top8[:, g, :], probs[:, g, :])
                    link(last)
                    for g in range(NG):
                        last = V.match_replace(mask[:, g, :], top8[:, g, :], probs[:, g, :], -1.0)
                    link(last)
                    link(V.tensor_scalar(mask, mask, 0.0, None, ALU.is_lt))
                else:
                    top_mask(mask, sel, TP, NG, e, m.topk)
                if m is M0:
                    V.tensor_reduce(maxp[:, :], probs, X, ALU.max)
                    link(V.tensor_copy(comb[0][:, :, :], mask))
                    return
                link(V.tensor_tensor(mask, mask, probs, ALU.mult))
                link(V.tensor_reduce(rs[0:TP, 0, 0:NG], mask, X, ALU.add))
                if m is M2:
                    link(V.tensor_scalar(rs[0:TP, 0, 0:NG], rs[0:TP, 0, 0:NG], 1e-9, None, ALU.add))
                link(V.reciprocal(rs[0:TP, 0, 0:NG], rs[0:TP, 0, 0:NG]))
                link(V.tensor_tensor(comb[i][:, :, 0:e], mask,
                                     rs[0:TP, 0, 0:NG].unsqueeze(2).to_broadcast([TP, NG, e]), ALU.mult))

            def centre(n):
                c, g = n // A1.ng, n % A1.ng
                if n == 0:
                    dve.wait_ge(in_att["l1f"], 48)
                w = wqkv["l1f"][:, c, g * 256:(g + 1) * 256].rearrange("k (h d) -> k h d", d=64)
                w = w[0:CB[c]]
                m = cw[0:CB[c], 4 * n:4 * (n + 1)]
                link(V.tensor_reduce(m, w, X, ALU.add))
                link(V.tensor_scalar(m, m, -1.0 / 64, None, ALU.mult))
                last = V.tensor_tensor(w, w, m.unsqueeze(2).to_broadcast([CB[c], 4, 64]), ALU.add)
                if n == NC_ * A1.ng - 1:
                    last.then_inc(S["setup_dve"], 1)

            def moe(m, i):
                for u in range(m.units):
                    if m is M0 and u >= 8 and u % 4 == 0 and u // 4 - 2 < NC_ * A1.ng:
                        centre(u // 4 - 2)
                    if True:
                        U = MU0[m.name] + u
                        if m.up:
                            dve.wait_ge(S["sg_ready"], SG0[m.name] + u + 1)
                            V.tensor_tensor(AF[U % 2][:, :], SG[u % 2][:, :], PS[:, 2 + u % 2, 0:HN],
                                            ALU.mult).then_inc(S["a_ready"], 1)
                        dve.wait_ge(S["a_ready"], U + 1)
                        if U >= 3:
                            dve.wait_ge(S["w3_done"], U - 2)
                        V.tensor_copy(AH[U % 3][:, :], AF[U % 2][:, :]).then_inc(S["ah_hi"], 1)
                        dve.wait_ge(S["ah_hi"], U + 1)
                        V.tensor_tensor(AL[U % 3][:, :], AF[U % 2][:, :], AH[U % 3][:, :].bitcast(F32),
                                        ALU.subtract).then_inc(S["ah_lo"], 1)
                        s = u // (2 * m.chunks)
                        if u % (2 * m.chunks) == 4 and s + 1 < m.slots:
                            split_low1(m, s + 1)
                    if u == 1:
                        router(m, i)
                    if u >= 2:
                        drain(m, i, u - 2)

            def drain(m, i, u):
                s, ch, j = u // (2 * m.chunks), u // 2 % m.chunks, u % 2
                if not m.last(s, ch):
                    return
                e = m.expert(s, ch)
                dve.wait_ge(S["w3_done"], MU0[m.name] + u + 1)
                d = MD0[m.name] + 2 * owner_index(m, s, ch) + j
                if d >= 2 and owner_index(m, s, ch):
                    dve.wait_ge(S["drained"], d - 1)
                for tau in range(TAU):
                    g = TAU * j + tau
                    y = YB(g)
                    into = ACC if m is M0 else H
                    coef = comb[i][:, g, e:e + 1]
                    if m is M0 and e == 0:
                        last = V.tensor_scalar(ACC[:, g, :], y, coef, None, ALU.mult)
                    else:
                        last = V.scalar_tensor_tensor(into[:, g, :], y, coef, into[:, g, :], ALU.mult, ALU.add)
                last.then_inc(S["drained"], 1)

            def stream(prev, j):
                kind, a, y = prev
                gs = slice(TAU * j, TAU * (j + 1))
                if kind == "patch":
                    dve.wait_ge(S["patch_summed"], j + 1)
                    for g in range(TAU * j, TAU * (j + 1)):
                        last = V.tensor_tensor(H[:, g, :], PB(g), bias[:, 0, :], ALU.add)
                    link(last)
                    link(V.tensor_tensor(H[:, gs, :], H[:, gs, :], posb[:, :, :], ALU.add))
                elif kind == "moe":
                    drain(a, MOES.index(a), a.units - 2 + j)
                    dve.wait_ge(S["drained"], MD0[a.name] + 2 * len(set(a.owner)) - 1 + j)
                    if a is M0:
                        link(V.tensor_copy(ACCB[:, gs, :], ACC[:, gs, :]))
                        for g in range(TAU * j, TAU * (j + 1)):
                            last = V.scalar_tensor_tensor(H[:, g, :], ACCB[:, g, :], maxp[:, g:g + 1], H[:, g, :],
                                                          ALU.mult, ALU.add)
                        link(last)
                else:
                    dve.wait_ge(S["y_ready"], 2 * y + j + 1)
                    dve.wait_ge(S["bias_added"], y + 1)
                    g = TAU * j
                    flat = H[:, g:g + 2, :].rearrange("p g f -> p (g f)")
                    V.tensor_tensor(flat, PS[0:TP, 2 * j, 0:2 * C], flat, ALU.add)
                    link(V.tensor_tensor(H[:, g + 2, :], PB(g + 2), H[:, g + 2, :], ALU.add))

            def gates(a):
                dve.wait_ge(S["logits"], 2)
                logits = PS[:, 4, 0:HB * GRP].rearrange("p (g e) -> p g e", g=HB)
                parts = [(0, 10), (10, 2), (12, 2)]
                last, view = softmax(128, (HB, GRP), parts, logits)
                last.then_inc(S["r_shift"], 1)
                normalise(128, (HB, GRP), parts, view, 1)
                p, m10 = view(2, 0, 10), view(3, 0, 10)
                top_mask(m10, p, 128, HB, 10, 2)
                link(V.tensor_tensor(m10, m10, p, ALU.mult))
                tot = rs[:, 0, 0:HB]
                link(V.tensor_reduce(tot, m10, X, ALU.add))
                link(V.tensor_scalar(tot, tot, FEPS, None, ALU.max))
                link(V.reciprocal(tot, tot))
                w0 = view(2, 10, 2)
                link(V.tensor_scalar(w0, w0, 4.0, None, ALU.mult))
                link(V.tensor_tensor(tot, tot, view(2, 10, 2)[:, :, 1], ALU.mult))
                link(V.tensor_tensor(m10, m10, tot.unsqueeze(2).to_broadcast([128, HB, 10]), ALU.mult))
                sh = view(2, 12, 2)
                link(V.tensor_tensor(sh, sh, w0[:, :, 0:1].to_broadcast([128, HB, 2]), ALU.mult))
                for par in range(2):
                    i = slice(64 * par, 64 * (par + 1))
                    for hh in range(2):
                        o = slice(64 * hh, 64 * (hh + 1))
                        V.tensor_copy(GH[o, 0, par:B:2], sh[i, :, hh])
                        last = V.tensor_copy(GH[o, 1:6, par:B:2].rearrange("p g b -> p b g"), m10[i, :, hh:10:2])
                link(last)

            def attention(a):
                u0 = UNIT0[a.name]

                def token_major(u):
                    n = TM0[a.name] + u
                    f2 = TAU * 2 * a.fq
                    src = PSF[0:TP, 1024:1024 + f2]
                    tx, t2 = TX[u % 2][:, 0:f2], T2[:, 0:f2]
                    if u0 + u >= 2:
                        dve.wait_ge(S["qk_ready"], u0 + u - 1)
                    if a.rope:
                        dve.wait_ge(S["tm_ready"], n + 1)
                        co = rope[:, 0, :, :].rearrange("p t f -> p (t f)")
                        si = rope[:, 1, :, :].rearrange("p t f -> p (t f)")
                        V.tensor_tensor(tx, src, co, ALU.mult)
                        V.tensor_tensor(t2[:, 0:f2:2], src[:, 1:f2:2], si[:, 0:f2:2], ALU.mult)
                        link(V.tensor_tensor(t2[:, 1:f2:2], src[:, 0:f2:2], si[:, 1:f2:2], ALU.mult))
                        V.tensor_tensor(tx, tx, t2, ALU.add).then_inc(S["tm_done"], 1)
                    else:
                        dve.wait_ge(S["tm_rstd"], u + 1)
                        V.tensor_tensor(tx.rearrange("p (h d) -> p h d", d=64), src.rearrange("p (h d) -> p h d", d=64),
                                        ssq[:, 2, :].unsqueeze(2).to_broadcast([TP, 12, 64]),
                                        ALU.mult).then_inc(S["tm_done"], 1)

                def mean_square(u):
                    dve.wait_ge(S["tm_square"], u + 1)
                    link(V.tensor_reduce(ssq[:, 0, :], T2[:, :].rearrange("p (h d) -> p h d", d=64), X, ALU.add))
                    V.tensor_scalar(ssq[:, 1, :], ssq[:, 0, :], 1.0 / 64, EPS, ALU.mult, ALU.add).then_inc(S["tm_sum"], 1)

                def queries(u):
                    U = u0 + u
                    dve.wait_ge(S["qk_ready"], U + 1)
                    if u == 0 and a in PADDED:
                        dve.wait_ge(S["pads"], PADDED.index(a) + 1)
                    if U >= 2:
                        dve.wait_ge(S["s_ready"], U - 1)
                    for h in range(a.hg):
                        q = QB[u % 2][0:a.fq, :, h * a.stride:h * a.stride + N]
                        if a.tm:
                            last = q_scale(q.rearrange("f b (n t) -> f b n t", t=TAU),
                                           PS[0:a.fq, 0, 0:HN].rearrange("f (t b n) -> f b n t", t=TAU, b=HB), h)
                        else:
                            last = q_scale(q, PS[0:a.fq, 0, 0:HN].rearrange("f (b n) -> f b n", b=HB), h)
                    last.then_inc(S["q_sb"], 1)

                def q_scale(o, i, h):
                    if a.qk_norm:
                        return V.tensor_scalar(o, i, qs[:, 2 * h:2 * h + 1], qs[:, 2 * h + 1:2 * h + 2], ALU.mult, ALU.add)
                    k = h if a.dim == 16 else 3 + h
                    return V.tensor_scalar(o, i, mh[0:a.fq, k:k + 1], None, ALU.mult)

                def shift(u):
                    U = u0 + u
                    dve.wait_ge(S["s_ready"], U + 1)
                    if U >= 2:
                        dve.wait_ge(S["p_sb"], U - 1)
                    s = PS[0:a.rows, 5, 0:HN].rearrange("p (b k) -> p b k", b=HB)
                    e = ES[u % 2][0:a.rows, :].rearrange("p (b k) -> p b k", b=HB)
                    mx = sm[0:a.rows, 0, :]
                    if a.mask:
                        mk = masks[:, 0 if a.mask == "causal" else 1, :]
                        link(V.tensor_tensor(e, s, mk.unsqueeze(1).to_broadcast([a.rows, HB, N]), ALU.add))
                        s = e
                    link(V.tensor_reduce(mx, s, X, ALU.max))
                    V.tensor_tensor(e, s, mx.unsqueeze(2).to_broadcast([a.rows, HB, N]),
                                    ALU.subtract).then_inc(S["s_taken"], 1)

                def norm(u):
                    U = u0 + u
                    dve.wait_ge(S["e_ready"], U + 1)
                    e = ES[u % 2][0:a.rows, :].rearrange("p (b k) -> p b k", b=HB)
                    tot, inv = sm[0:a.rows, 1, :], sm[0:a.rows, 2, :]
                    link(V.tensor_reduce(tot, e, X, ALU.add))
                    link(V.reciprocal(inv, tot))
                    if a.gated:
                        link(V.tensor_tensor(inv, inv, GH[:, u // 2, HB * (u % 2):HB * (u % 2 + 1)], ALU.mult))
                    if U >= 2:
                        dve.wait_ge(S["pt_ready"], U - 1)
                    V.tensor_tensor(PN[u % 2][0:a.rows, :, 0:N], e, inv.unsqueeze(2).to_broadcast([a.rows, HB, N]),
                                    ALU.mult).then_inc(S["p_sb"], 1)

                lag = 1 if a.tm else 0
                for i in range(a.units + lag + 4):
                    if a.qk_norm and i < a.units:
                        mean_square(i)
                    if a.rope and i < a.units:
                        token_major(i)
                    if 0 <= i - lag < a.units:
                        queries(i - lag)
                    if a.qk_norm and i < a.units:
                        token_major(i)
                    if 0 <= i - lag - 1 < a.units:
                        shift(i - lag - 1)
                    if a.gated and i == lag + 2:
                        gates(a)
                    if 0 <= i - lag - 2 < a.units:
                        norm(i - lag - 2)

            def grid_attention():
                qkv = GQ.rearrange("p (j k f) -> p j k f", j=2, k=3)
                for j in range(2):
                    dve.wait_ge(S["grid_sb"], 3 * j + 3)
                    prod = OT[0:TP, 0:9 * C].rearrange("p (q k f) -> p q k f", q=3, k=3)
                    q = qkv[:, j, :, 0:C].unsqueeze(2).to_broadcast([TP, 3, 3, C])
                    k = qkv[:, j, :, C:2 * C].unsqueeze(1).to_broadcast([TP, 3, 3, C])
                    link(V.tensor_tensor(prod, q, k, ALU.mult))
                    sc = sg1[:, 0, 0:108]
                    link(V.tensor_reduce(sc, OT[0:TP, 0:9 * C].rearrange("p (s d) -> p s d", d=16), X, ALU.add))
                    s3 = sc.rearrange("p (q k n) -> p q n k", q=3, k=3)
                    mx = sg1[:, 2, 0:36].rearrange("p (q n) -> p q n", q=3)
                    link(V.tensor_reduce(mx, s3, X, ALU.max))
                    e3 = sg1[:, 1, 0:108].rearrange("p (q k n) -> p q n k", q=3, k=3)
                    V.tensor_tensor(e3, s3, mx.unsqueeze(3).to_broadcast([TP, 3, 12, 3]),
                                    ALU.subtract).then_inc(S["grid_s"], 1)
                    dve.wait_ge(S["grid_e"], j + 1)
                    link(V.tensor_reduce(mx, e3, X, ALU.add))
                    link(V.reciprocal(mx, mx))
                    link(V.tensor_tensor(e3, e3, mx.unsqueeze(3).to_broadcast([TP, 3, 12, 3]), ALU.mult))
                    o = GO[:, 4 * C * j:4 * C * j + 3 * C].rearrange("p (n q d) -> p q n d", n=12, q=3)
                    p4 = sg1[:, 1, 0:108].rearrange("p (q k n) -> p q k n", q=3, k=3)
                    tmp = OT[0:TP, 0:576].rearrange("p (q n d) -> p q n d", q=3, n=12)
                    for ki in range(3):
                        v = qkv[:, j, ki, 2 * C:3 * C].rearrange("p (n d) -> p n d", n=12)
                        w = p4[:, :, ki, :].unsqueeze(3).to_broadcast([TP, 3, 12, 16])
                        vv = v.unsqueeze(1).to_broadcast([TP, 3, 12, 16])
                        link(V.tensor_tensor(o if ki == 0 else tmp, w, vv, ALU.mult))
                        if ki:
                            last = V.tensor_tensor(o, o, tmp, ALU.add)
                            if ki == 1:
                                link(last)
                    last.then_inc(S["grid_o"], 1)
                    dve.wait_ge(S["grid_o"], j + 1)

            V.memset(comb[1][:, :, 8:9], 1.0)
            V.memset(MIX[:, :], 0.0)
            link(V.memset(XT[64:65, 1, :], 1.0))
            dve.wait_ge(S["in_const"], 16 * len(consts))
            for h in range(2):
                V.tensor_scalar(qs[:, 2 * h:2 * h + 1], qn[:, 0:1], mh[:, 3 + h:4 + h], None, ALU.mult)
                last = V.tensor_scalar(qs[:, 2 * h + 1:2 * h + 2], qn[:, 1:2], mh[:, 3 + h:4 + h], None, ALU.mult)
            link(last)

            y = n = 0
            prev = ("patch", None, 0)
            for i, (kind, arg) in enumerate(STAGES):
                prepare(i, kind, arg, n, prev)
                n += 4 if kind == "attn" and arg.double_ln else 2
                prev = (kind, arg, y)
                if kind == "moe":
                    moe(arg, MOES.index(arg))
                elif kind == "attn":
                    attention(arg)
                    y += 1
                else:
                    grid_attention()
                    y += 1
            for j in range(2):
                stream(prev, j)

        @block.gpsimd
        def _(pool):
            G = nc.gpsimd
            count = [0]

            def link(ins):
                count[0] += 1
                ins.then_inc(S["pool_step"], 1)
                pool.wait_ge(S["pool_step"], count[0])

            link(G.memset(nhalf[:, :], -0.5))
            link(G.memset(tri[:, :, :], 1.0))
            link(G.affine_select(out=tri[:, :, :], in_=tri[:, :, :], compare_op=ALU.is_gt, fill=0.0, base=0,
                                 pattern=[[1, 16], [-1, 16]], channel_multiplier=0))
            G.memset(nhalf[:, 0:1], -0.5).then_inc(S["setup_pool"], 1)
            pool.wait_ge(S["setup_pool"], 1)
            pool.wait_ge(S["in_const"], 16 * len(consts))
            def split_low(m, s):
                n = MS0[m.name] + s
                r, w = n % RING, m.width
                pool.wait_ge(S["w_hi"], 3 * n + 1)
                G.tensor_tensor(WL[r][:, 0, 0:w], RG[r][:, 0, 0:w], WH[r][:, 0, 0:w].bitcast(F32),
                                ALU.subtract).then_inc(S["w_lo"], 1)

            def split_low_down(m, s):
                n = MS0[m.name] + s
                r, d = n % RING, m.chunks * C
                pool.wait_ge(S["w_hi"], 3 * n + 3)
                G.tensor_tensor(DL[r][:, 0:d], RD[r][:, 0:d], DH[r][:, 0:d].bitcast(F32),
                                ALU.subtract).then_inc(S["w_lo"], 1)

            def pads(a):
                for r in range(2):
                    last = G.memset(PN[r][:, :, N:], 0.0)
                    if a.stride != N:
                        last = G.memset(QB[r][:, :, :], 0.0)
                last.then_inc(S["pads"], 1)

            y = n = 0
            for i, (kind, arg) in enumerate(STAGES):
                double, moe = kind == "attn" and arg.double_ln, kind == "moe"
                if arg is A0 or arg is A1:
                    pads(arg)
                for j in range(2):
                    for second in range(2 if double else 1):
                        pool.wait_ge(S["ln_stats"], n + 1)
                        r = rstd[:, TAU * j:TAU * (j + 1)]
                        G.tensor_tensor(r, var[:, TAU * j:TAU * (j + 1)], nhalf[0:TP, 0:TAU], ALU.pow).then_inc(S["ln_rstd"], 1)
                        pool.wait_ge(S["ln_rstd"], n + 1)
                        n += 1
                    g = TAU * j + TAU - 1
                    src = XN if double else H
                    last = G.tensor_scalar(XN[:, g, 0:C], src[:, g, 0:C], mv[:, g, 0:1], rstd[:, g:g + 1],
                                           ALU.subtract, ALU.mult)
                    if moe:
                        last = G.tensor_scalar(XN[:, g, C:], src[:, g, 128:C], mv[:, g, 0:1], rstd[:, g:g + 1],
                                               ALU.subtract, ALU.mult)
                    last.then_inc(S["ln_third"], 1)
                    if moe and j == 0:
                        split_low(arg, 0)
                if arg is A3:
                    pads(arg)
                if kind != "moe":
                    pool.wait_ge(S["ln_normed"], 2 * i + 2)
                    pool.wait_ge(S["ln_third"], 2 * i + 2)
                    G.tensor_tensor(H[:, :, :], H[:, :, :], bias[:, 1 + y, :].unsqueeze(1).to_broadcast([TP, NG, C]),
                                    ALU.add).then_inc(S["bias_added"], 1)
                    y += 1
                else:
                    for s in range(arg.slots):
                        if s:
                            split_low(arg, s)
                        split_low_down(arg, s)
                if kind == "attn" and arg.qk_norm:
                    for u in range(arg.units):
                        pool.wait_ge(S["tm_sum"], u + 1)
                        G.tensor_tensor(ssq[:, 2, :], ssq[:, 1, :], nhalf[0:TP, 0:12], ALU.pow).then_inc(S["tm_rstd"], 1)


def layouts(a):
    f = np.float32
    z = lambda *shape: np.zeros(shape, f)
    t = {}
    t["patch"] = a["x"].reshape(B, 3, 6, 16, 6, 16).transpose(1, 3, 5, 0, 2, 4).reshape(TOKF, 128, B * N).transpose(1, 0, 2)
    t["wtok"] = a["L0_tok_W"].T.reshape(TOKF, 128, C).transpose(1, 0, 2)

    def chunks(w, b=None):
        o = z(128, NC_, w.shape[1])
        for c in range(NC_):
            o[0:CR[c], c] = w[128 * c:128 * c + CR[c]]
        if b is not None:
            o[CR[1], 1] = b
        return o

    def attn(at, wq, wk, wv, wo, bq, bk, bv):
        parts = []
        for w, b, slot in ((wq, bq, at.dim), (wk, bk, at.dim), (wv, bv, at.slot)):
            w = chunks(w, b).reshape(128, NC_, at.ng, at.hg, at.dim)
            o = z(128, NC_, at.ng, at.hg, slot)
            o[..., 0:at.dim] = w
            parts.append(o.reshape(128, NC_, at.ng, at.hg * slot))
        qk = np.concatenate(parts[0:2], axis=3).reshape(128, NC_, at.v0)
        w = np.concatenate([qk, parts[2].reshape(128, NC_, at.ng * at.fv)], axis=2)
        for c in range(NC_):
            t[f"wqkv_{at.name}_{c}"] = w[0:CB[c], c]
        o = z(at.ng, at.hg, at.slot, C)
        o[:, :, 0:at.dim] = wo.reshape(at.ng, at.hg, at.dim, C)
        t["wp_" + at.name] = o.reshape(at.ng, at.fv, C).transpose(1, 0, 2)

    def thirds(w):
        n = w.shape[-1] // 3
        return w[..., 0:n], w[..., n:2 * n], w[..., 2 * n:]

    q, k, v = thirds(a["L0_attn_W_attn"])
    bq, bk, bv = thirds(a["L0_attn_b_attn"])
    attn(A0, q, k, v, a["L0_attn_W_proj"], bq, bk, bv)
    q, k, v = thirds(a["L1_ffn_qkv_w"])
    bq, bk, bv = thirds(a["L1_ffn_qkv_b"])
    attn(A1, q, k, v, a["L1_ffn_proj_w"], bq, bk, bv)
    q, k, v = thirds(a["L2_attn_w_qkv"])
    attn(A2, q, k, v, a["L2_attn_w_out"], None, None, None)
    attn(A3, a["L3_attn_Wq"], a["L3_attn_Wk"], a["L3_attn_Wv"], a["L3_attn_Wo"],
         a["L3_attn_bq"], a["L3_attn_bk"], a["L3_attn_bv"])
    t["wg_0"], t["wg_1"] = a["L1_attn_qkv_w"].T[0:128], a["L1_attn_qkv_w"].T[128:]
    t["wgp"] = a["L1_attn_proj_w"].T.reshape(3, 64, C).transpose(1, 0, 2)

    def moe(m, gate, up, down):
        t["gu_" + m.name] = np.concatenate([w for w in (gate, up) if w is not None], axis=2)
        t["wd_" + m.name] = down.reshape(m.slots, m.chunks, 128, C).transpose(0, 2, 1, 3)

    moe(M0, a["L0_ffn_w1"], a["L0_ffn_w2"], a["L0_ffn_w3"])
    cat = lambda w, s: np.concatenate([w, s[None]]).transpose(0, 2, 1)
    moe(M2, cat(a["L2_ffn_Wg"], a["L2_ffn_sg"]), cat(a["L2_ffn_Wu"], a["L2_ffn_su"]), cat(a["L2_ffn_Wd"], a["L2_ffn_sd"]))
    moe(M3, a["L3_ffn_w1"].reshape(C, M3.slots, 512).transpose(1, 0, 2), None,
        a["L3_ffn_w2"].reshape(M3.slots, 512, C))

    t["wr0"] = chunks(a["L0_ffn_router_w"], a["L0_ffn_router_b"])
    t["wr1"] = chunks(np.concatenate([a["L1_ffn_wg_w"], a["L1_ffn_wg0_w"], a["L1_ffn_wg1_w"]], axis=1))
    t["wr2"] = chunks(a["L2_ffn_w_router"].T)
    t["wr3"] = chunks(a["L3_ffn_router_w"].T)
    t["bias"] = np.broadcast_to(np.stack([a[n] for n in (
        "L0_tok_b", "L0_attn_b_proj", "L1_attn_proj_b", "L1_ffn_proj_b", "L2_attn_b_out", "L3_attn_bo")]), (TP, 6, C))
    t["posb"] = np.broadcast_to(a["L0_tok_pos"].reshape(1, NB, TAU, C), (HB, NB, TAU, C)).reshape(TP, TAU, C)
    t["gb"] = np.concatenate([chunks(a[n][:, None])[:, :, 0] for n in ("L2_attn_gamma", "L2_attn_beta")], axis=1)
    t["qn"] = np.stack([np.concatenate([a["L1_ffn_" + n]] * 2) for n in
                        ("q_norm_w", "q_norm_b", "k_norm_w", "k_norm_b")], axis=1)
    t["ebias"] = np.broadcast_to(a["L2_ffn_expert_bias"], (TP, 8))

    t["ident"] = np.eye(128, dtype=f)
    mh = z(128, 6)
    for h in range(3):
        mh[16 * h:16 * (h + 1), h] = 16 ** -0.5
    for h in range(2):
        mh[64 * h:64 * (h + 1), 3 + h] = 64 ** -0.5
    t["mh"] = mh
    inv = (1.0 / 10000.0 ** (np.arange(0, 16, 2, dtype=f) / f(16))).astype(f)
    ang = (np.arange(N, dtype=f)[:, None] * inv[None]).astype(f)
    cos, sin = np.repeat(np.cos(ang), 2, axis=1).astype(f), np.repeat(np.sin(ang), 2, axis=1).astype(f)
    sin[:, 0::2] *= -1
    tok = (TAU * (np.arange(TP) % NB))[:, None] + np.arange(TAU)[None]
    t["rope"] = np.stack([np.tile(w[tok], (1, 1, 6)) for w in (cos, sin)], axis=1)
    i, j = np.arange(N)[:, None], np.arange(N)[None]
    causal = np.where(j <= i, 0, -1e30).astype(f)
    band = np.where(abs(i - j) <= 32, 0, -1e9).astype(f)
    t["masks"] = np.stack([np.tile(w, (3, 1)) for w in (causal, band)], axis=1)
    return {n: np.ascontiguousarray(w) for n, w in t.items()}


def kernel(**inputs):
    import concourse.bacc as _bacc
    from concourse.bass_utils import run_bass_kernel_spmd as _run

    nc = _bacc.Bacc("TRN2", target_bir_lowering=False, num_devices=1)
    arrays, aps = {}, {}
    for name, w in layouts({n: np.asarray(v) for n, v in inputs.items()}).items():
        arrays[f"in_{name}_dram"] = w
        aps[name] = nc.dram_tensor(f"in_{name}_dram", w.shape, mybir.dt.from_np(w.dtype), kind="ExternalInput").ap()
    out = nc.dram_tensor("out_0_dram", (B, N, C), F32, kind="ExternalOutput").ap()
    bass_vit_tower(nc, aps, out)
    r = _run(nc, [arrays], core_ids=[0])
    return r.results[0]["out_0_dram"]
```

```python
from contextlib import ExitStack

import numpy as np
import concourse.bass as bass
from concourse import mybir

ALU = mybir.AluOpType
ACT = mybir.ActivationFunctionType
F32 = mybir.dt.float32
BF16 = mybir.dt.bfloat16
X = mybir.AxisListType.X

B, N, C = 16, 36, 192
NC_ = 2
CR = (128, C - 128)
CB = (CR[0], CR[1] + 1)
TP = 96
NG = B * N // TP
TAU = 3
HB = 8
HN = HB * N
NB = N // TAU
TOKF = 768 // 128
VW = 64
EPS = 1e-5
FEPS = float(np.finfo(np.float32).eps)


class Attn:

    def __init__(self, name, heads_of_group, dim, slot, stride, token_major, rope=False, qk_norm=False,
                 mask=None, gated=False, double_ln=False):
        self.name, self.hg, self.dim, self.slot, self.stride = name, heads_of_group, dim, slot, stride
        self.ng = 12 // heads_of_group
        self.fq = heads_of_group * dim
        self.fv = heads_of_group * slot
        self.rows = heads_of_group * stride
        self.tm, self.rope, self.qk_norm = token_major, rope, qk_norm
        self.mask, self.gated, self.double_ln = mask, gated, double_ln
        self.v0 = self.ng * 2 * self.fq
        self.width = self.v0 + self.ng * self.fv
        self.vparts = self.ng * self.fv // 384
        self.vpieces = 4 * self.vparts
        self.units = 2 * self.ng
        self.paired = dim == 16 and not token_major


class Moe:

    def __init__(self, name, slots, chunks, up, act, experts, topk, owner):
        self.name, self.slots, self.chunks, self.up, self.act = name, slots, chunks, up, act
        self.experts, self.topk, self.owner = experts, topk, owner
        self.units = slots * chunks * 2
        self.width = chunks * 128 * (2 if up else 1)

    def expert(self, s, m):
        return self.owner[s * self.chunks + m]

    def first(self, s, m):
        n = s * self.chunks + m
        return n == 0 or self.owner[n - 1] != self.owner[n]

    def last(self, s, m):
        n = s * self.chunks + m
        return n == len(self.owner) - 1 or self.owner[n + 1] != self.owner[n]


A0 = Attn("l0a", 3, 16, 32, N, True, rope=True, mask="causal")
A1 = Attn("l1f", 2, 64, 64, N, True, qk_norm=True, gated=True)
A2 = Attn("l2a", 2, 64, 64, N, False, double_ln=True)
A3 = Attn("l3a", 3, 16, 32, N, False, mask="band")
ATTNS = [A0, A1, A2, A3]
M0 = Moe("l0f", 8, 4, True, ACT.Silu, 8, 1, [s for s in range(8) for _ in range(4)])
M2 = Moe("l2f", 9, 3, True, ACT.Silu, 8, 2, [s for s in range(9) for _ in range(3)])
M3 = Moe("l3f", 6, 4, False, ACT.Gelu_apprx_tanh, 16, 8,
         list(range(8)) + [8 + e for e in range(8) for _ in range(2)])
MOES = [M0, M2, M3]
UNIT0 = {a.name: sum(x.units for x in ATTNS[:i]) for i, a in enumerate(ATTNS)}
TM0 = {A0.name: 0, A1.name: A0.units}
V0 = {a.name: sum(2 * x.vpieces for x in ATTNS[:i]) for i, a in enumerate(ATTNS)}
MU0 = {m.name: sum(x.units for x in MOES[:i]) for i, m in enumerate(MOES)}
MS0 = {m.name: sum(x.slots for x in MOES[:i]) for i, m in enumerate(MOES)}
SG0 = {M0.name: 0, M2.name: M0.units}
MD0 = {}
_d = 0
for _m in MOES:
    MD0[_m.name] = _d
    _d += 2 * len(set(_m.owner))
RING = 2
WG_ = 1024
GRP = 14
STAGES = [("attn", A0), ("moe", M0), ("grid", None), ("attn", A1), ("attn", A2), ("moe", M2), ("attn", A3), ("moe", M3)]
XT0_N = [2 * sum(1 for k, a in STAGES[:i] if k != "attn" or a.tm) for i in range(len(STAGES))]
PADDED = [A0, A1, A3]
ROUTER = {"l0f": (0, 8), "l2f": (2, 8), "l3f": (3, 16)}
XV_N = {"l0a": 0, "l1f": 1, "l2a": 2, "l3a": 3}
CONSTS = ["ident", "posb", "bias0", "mh", "rope", "masks", "bias", "gb", "qn", "ebias", "wr0", "wr1", "wr2", "wr3"]


def pieces(a, i):
    n = 4 if a.tm else 3
    return range(a.vpieces * (i - 1) // n, a.vpieces * i // n) if 1 <= i <= n else ()


def owner_index(m, s, ch):
    return m.owner[s * m.chunks + ch]


def units_before(slot):
    n = 0
    for m in MOES:
        k = min(slot, m.slots)
        n += k * m.chunks * 2
        slot -= k
    return n


def bass_vit_tower(nc, t, out):
    with ExitStack() as ctx:
        def sb(name, shape, dt=F32):
            return ctx.enter_context(nc.sbuf_tensor(name, shape, dt))

        def sem(name):
            return ctx.enter_context(nc.semaphore(name))

        PS = ctx.enter_context(nc.psum_tensor("PS", [128, 8, 512], F32))
        PSF = PS[:, :, :].rearrange("p b n -> p (b n)")

        OB = PS[:, 6:8, 0:HN // 2]

        def YB(g):
            return PS[0:TP, (4, 4, 5, 6, 6, 7)[g], (g % TAU % 2) * C:(g % TAU % 2 + 1) * C]

        def PB(g):
            return PS[0:TP, (0, 0, 1, 2, 2, 3)[g], (g % TAU % 2) * C:(g % TAU % 2 + 1) * C]

        H = sb("H", [TP, NG, C])
        XN = sb("XN", [TP, NG, 256])
        XT = sb("XT", [128, NC_, B * N])
        ACC = sb("ACC", [TP, NG, C])
        BIG = sb("BIG", [128, TOKF * B * N])
        OT = sb("OT", [128, 6 * B * N])
        WTOK = OT[:, 0:TOKF * C].rearrange("p (k f) -> p k f", k=TOKF)
        MIX = sb("MIX", [128, NC_ * B * VW])
        XV = MIX[:, :].rearrange("k (c n) -> k c n", c=NC_)
        st = sb("st", [TP, NG, 6])
        mv = sb("mv", [TP, NG, 2])
        var = sb("var", [TP, NG])
        rstd = sb("rstd", [TP, NG])
        cst = sb("cst", [128, 128])
        mh = sb("mh", [128, 6])
        nhalf = sb("nhalf", [128, 16])
        tri = sb("tri", [128, 16, 16])
        rope = sb("rope", [TP, 2, TAU, 96])
        masks = sb("masks", [108, 2, N])
        posb = sb("posb", [TP, TAU, C])
        bias = sb("bias", [TP, 6, C])
        gb = sb("gb", [128, 4])
        qn = sb("qn", [128, 4])
        qs = sb("qs", [128, 4])
        ebias = sb("ebias", [TP, 8])
        wr = [sb(f"wr{i}", [128, NC_, e]) for i, e in enumerate((8, GRP, 8, 16))]
        wqkv = {a.name: sb("wqkv_" + a.name, [128, NC_, a.width]) for a in (A0, A1)}
        wp = {a.name: sb("wp_" + a.name, [a.fv, a.ng, C]) for a in (A0, A1, A2)}
        wqkv["l3a"], wp["l3a"] = wqkv["l0a"], wp["l0a"]
        wqkv["l2a"] = wqkv["l1f"]
        wg = sb("wg", [128, NC_, 3 * C])
        wgp = sb("wgp", [64, 3, C])
        RG = [sb(f"RG{r}", [128, NC_, WG_]) for r in range(RING)]
        RD = [sb(f"RD{r}", [128, 4 * C]) for r in range(RING)]
        ACCB = MIX[0:TP, 4 * HN:4 * HN + NG * C // 2].bitcast(BF16).rearrange("p (g f) -> p g f", g=NG)
        SG = [MIX[:, r * HN:(r + 1) * HN] for r in range(2)]
        AF = [MIX[:, r * HN:(r + 1) * HN] for r in range(2, 4)]
        T2 = ACC[:, 0:4, :].rearrange("p g f -> p (g f)")
        sm = sb("sm", [128, 4, HB])
        ssq = sb("ssq", [TP, 3, 12])
        cw = sb("cw", [128, NC_ * 24])
        R1, R2 = BIG[:, 0:1600], BIG[:, 1600:3200]
        rl = sb("rl", [128, 4, 16 * 16])
        rs = sb("rs", [128, 8, 16])
        GP = sb("GP", [128, 2, 6, HB])
        GH = sb("GH", [2 * N, 2, 6, HB])
        comb = [sb(f"comb{i}", [TP, NG, e]) for i, e in enumerate((8, 9, 16))]
        maxp = sb("maxp", [TP, NG])
        top8 = sb("top8", [TP, NG, 8])
        sg1 = sb("sg1", [TP, 3, 216])

        with ExitStack() as place:
            def sb1(name, shape, dt=F32):
                return place.enter_context(nc.sbuf_tensor(name, shape, dt))
            QB = [sb1(f"QB{r}", [128, HB, 128]) for r in range(2)]
            KS = [sb1(f"KS{r}", [128, HN]) for r in range(2)]
            VS = sb1("VS", [128, HB, 768])
            ES = [sb1(f"ES{r}", [128, HN]) for r in range(2)]
            PN = [sb1(f"PN{r}", [128, HB, VW]) for r in range(2)]
            PT = [sb1(f"PT{r}", [128, 512]) for r in range(2)]
            TX = [sb1(f"TX{r}", [TP, TAU * 256]) for r in range(2)]
        F32R = mybir.dt.float32r
        XH = sb("XH", [128, B * N], F32R)
        XL = sb("XL", [128, B * N], F32R)
        X1 = sb("X1", [128, B * N], F32R)
        X1T = sb("X1T", [128, B * N], F32R)
        WH = [sb(f"WH{r}", [128, NC_, WG_], F32R) for r in range(RING)]
        WL = [sb(f"WL{r}", [128, NC_, WG_], F32R) for r in range(RING)]
        DH = [sb(f"DH{r}", [128, 4 * C], F32R) for r in range(RING)]
        DL = [sb(f"DL{r}", [128, 4 * C], F32R) for r in range(RING)]
        AH = [sb(f"AH{r}", [128, HN], F32R) for r in range(3)]
        AL = [sb(f"AL{r}", [128, HN], F32R) for r in range(3)]

        S = {n: sem(n) for n in (
            "in_first", "in_const", "wslot0", "wslot1", "out_written",
            "centred", "patch_summed", "pads",
            "ln_stats", "ln_rstd", "ln_normed", "ln_turned", "xt0_ready", "xt1_ready", "xv0_ready", "xv1_ready",
            "x_high", "x1_high", "x1_low", "x_split",
            "tm_ready", "tm_square", "tm_taken", "tm_sum", "tm_rstd", "tm_done", "qk_ready", "q_sb", "q1_sb", "k_sb", "v_ready", "v_sb",
            "s_ready", "s_taken", "e_ready", "p_sb", "pt_ready", "pt_sb", "o_ready", "o_sb", "y_ready",
            "bias_added",
            "logits", "gates_made", "gates_in", "r_shift", "r_exp",
            "g_ready", "sg_ready", "a_ready", "ah_hi", "ah_lo", "w3_done", "drained", "w_hi", "w_lo", "w_lo1",
            "grid_ready", "grid_sb", "grid_product", "grid_s", "grid_e", "grid_o", "grid_turned", "grid_osb",
            "dve_step", "pool_step",
        )}
        in_att = {n: sem("in_att_" + n) for n in ("l0a", "grid", "l1f", "l2a", "l3a")}
        in_patch = [sem(f"in_patch{k}") for k in range(TOKF)]
        wslot = [S["wslot0"], S["wslot1"]]

        GQ = BIG[0:TP, :]
        GO = XN[:, :, :].rearrange("p g f -> p (g f)")
        GT = OT[0:64, 9 * C:18 * C]
        FIRST = CONSTS.index("bias0") + 1
        consts = [(dst[tuple(slice(None) for _ in dst.shape)], t[n]) for dst, n in zip(
            [cst, posb, bias[:, 0, :], mh, rope, masks, bias[:, 1:, :], gb, qn, ebias, *wr], CONSTS)]

        def xt_copy(copy, c, j, grid):
            k, cols = CR[c], slice(HN * j, HN * (j + 1))
            if grid:
                for tau in range(TAU):
                    o = XT[0:k, c, cols].rearrange("k (s b m t) -> k t b s m", s=3, b=HB, t=TAU)[:, tau]
                    i = PS[0:k, 4 + 2 * j + c, tau * TP:(tau + 1) * TP].rearrange("k (b s m) -> k b s m", b=HB, s=3)
                    last = copy(o, i)
                return last
            return copy(by_token(XT[0:k, c, cols]), turned(j, c, 0, k))

        def by_token(ap):
            return ap.rearrange("k (p t) -> k t p", t=TAU)

        def turned(j, c, lo, hi):
            return PS[lo:hi, 4 + 2 * j + c, 0:HN].rearrange("k (t p) -> k t p", t=TAU)

        def xv_half(c, j, rows):
            return XV[0:rows, c, :].rearrange("k (b n) -> k b n", b=B)[:, HB * j:HB * (j + 1), 0:N]

        def grid_product(j):
            qkv = GQ.rearrange("p (j k f) -> p j k f", j=2, k=3)
            prod = OT[0:TP, 0:9 * C] if j == 0 else VS[0:TP, :, :].rearrange("p i f -> p (i f)")[:, 0:9 * C]
            return (prod, qkv[:, j, :, 0:C].unsqueeze(2).to_broadcast([TP, 3, 3, C]),
                    qkv[:, j, :, C:2 * C].unsqueeze(1).to_broadcast([TP, 3, 3, C]))

        def q_views(a, u, h):
            q = QB[u % 2][0:a.fq, :, h * a.stride:h * a.stride + N]
            if a.tm:
                return (q.rearrange("f b (n t) -> f b n t", t=TAU),
                        PS[0:a.fq, 0, 0:HN].rearrange("f (t b n) -> f b n t", t=TAU, b=HB))
            return q, PS[0:a.fq, 0, 0:HN].rearrange("f (b n) -> f b n", b=HB)

        block = ctx.enter_context(nc.Block())

        def tile(ap2, j, tau, width=TP):
            return ap2[:, HN * j + tau:HN * (j + 1):TAU]

        @block.sync
        def _(sp):
            for k in range(TOKF):
                sp.dma_start(WTOK[:, k, :], t["wtok"][:, k, :]).then_inc(in_patch[k], 16)
                sp.dma_start(BIG[:, k * B * N:(k + 1) * B * N], t["patch"][:, k, :]).then_inc(in_patch[k], 16)

            def qkv(a):
                for c in range(NC_):
                    sp.dma_start(wqkv[a.name][0:CB[c], c, :], t[f"wqkv_{a.name}_{c}"]).then_inc(in_att[a.name], 16)

            def proj(a):
                sp.dma_start(wp[a.name][:, :, :], t["wp_" + a.name]).then_inc(in_att[a.name], 16)

            def slots(m, lo, hi):
                w = m.width
                for s in range(lo, hi):
                    n = MS0[m.name] + s
                    if n >= RING:
                        sp.wait_ge(S["w_hi"], 3 * (n - 1))
                        sp.wait_ge(S["w_lo"], 2 * (n - 1))
                        sp.wait_ge(S["w_lo1"], n - 1)
                    r, arrived = n % RING, wslot[n % RING]
                    sp.dma_start(RG[r][:, 0, 0:w], t["gu_" + m.name][s, 0:128]).then_inc(arrived, 16)
                    for half in (0, 64):
                        sp.dma_start(RG[r][half:half + 64, 1, 0:w], t["gu_" + m.name][s, 128:C]).then_inc(arrived, 16)
                    sp.dma_start(RD[r][:, 0:m.chunks * C], t["wd_" + m.name][s]).then_inc(arrived, 16)

            qkv(A0)
            proj(A0)
            slots(M0, 0, RING)
            for c in range(NC_):
                sp.dma_start(wg[0:CR[c], c, :], t[f"wg_{c}"]).then_inc(in_att["grid"], 16)
            sp.dma_start(wgp[:, :, :], t["wgp"]).then_inc(in_att["grid"], 16)
            qkv(A1)
            proj(A1)
            proj(A2)
            slots(M0, RING, M0.slots)
            slots(M2, 0, RING)
            sp.wait_ge(S["y_ready"], 2)
            qkv(A3)
            proj(A3)
            sp.wait_ge(S["gates_made"], 1)
            for hh in range(2):
                for par in range(2):
                    sp.dma_start(GH[N * hh:N * (hh + 1), par], GP[VW * par:VW * par + N, hh]).then_inc(S["gates_in"], 16)
            sp.wait_ge(S["v_ready"], V0["l2a"])
            sp.wait_ge(S["tm_ready"], TM0["l1f"] + A1.units)
            qkv(A2)
            slots(M2, RING, M2.slots)
            slots(M3, 0, M3.slots)
            for j in range(2):
                sp.wait_ge(S["drained"], MD0[M3.name] + 2 * M3.experts - 1 + j)
                sp.dma_start(out.rearrange("b n f -> (b n) f").rearrange("(j p t) f -> j p (t f)", j=2, t=TAU)[j],
                             H[:, TAU * j:TAU * (j + 1), :].rearrange("p t f -> p (t f)")).then_inc(S["out_written"], 16)
            sp.wait_ge(S["out_written"], 32)



        @block.tensor
        def _(pe):
            mm, tr = nc.tensor.matmul, nc.tensor.transpose

            def turn(k, j, moe=False):
                for tau in range(TAU):
                    if tau == 0:
                        pe.wait_ge(S["ln_normed"], 2 * k + j + 1)
                    for c in range(NC_):
                        k_ = 128 if moe else CR[c]
                        last = tr(PS[0:k_, 4 + 2 * j + c, tau * TP:(tau + 1) * TP],
                                  XN[:, TAU * j + tau, c * 128:c * 128 + k_], cst[0:TP, 0:TP])
                last.then_inc(S["ln_turned"], 1)

            def wait_xt(k, j):
                pe.wait_ge(S["xt0_ready"], XT0_N[k] + j + 1)
                pe.wait_ge(S["xt1_ready"], 2 * k + j + 1)

            def wait_xv(a, j):
                pe.wait_ge(S["xv0_ready"], 2 * XV_N[a.name] + j + 1)
                pe.wait_ge(S["xv1_ready"], 2 * XV_N[a.name] + j + 1)

            def router(i, e, stage, j):
                wait_xt(stage, j)
                for g in range(TAU * j, TAU * (j + 1)):
                    for c in range(NC_):
                        last = mm(PS[0:TP, 5, g * e:(g + 1) * e], tile(XT[0:CB[c], c, 0:B * N], g // TAU, g % TAU),
                                  wr[i][0:CB[c], c, :], start=(c == 0), stop=(c == NC_ - 1))
                if j == 1:
                    last.then_inc(S["logits"], 1)

            def moe(m, stage):
                u0 = MU0[m.name]

                def hidden(u):
                    s, ch, j = u // (2 * m.chunks), u // 2 % m.chunks, u % 2
                    n, U = MS0[m.name] + s, u0 + u
                    r, cols = n % RING, slice(HN * j, HN * (j + 1))
                    if ch == 0 and j == 0:
                        pe.wait_ge(S["w_lo"], 2 * n + 1)
                        pe.wait_ge(S["w_lo1"], n + 1)
                    if u < 2:
                        pe.wait_ge(S["x_split"], 2 * MOES.index(m) + j + 1)
                    if U >= 2:
                        pe.wait_ge(S["a_ready"], U - 1)
                    for k in range(2 if m.up else 1):
                        o = PS[:, 2 * k + u % 2, 0:HN]
                        w = slice((k * m.chunks + ch) * 128, (k * m.chunks + ch + 1) * 128)
                        mm(o, WH[r][:, 0, w], XH[:, cols], start=True, stop=False)
                        mm(o, WH[r][:, 0, w], XL[:, cols], start=False, stop=False)
                        mm(o, WL[r][:, 0, w], XH[:, cols], start=False, stop=False)
                        mm(o, WH[r][:, 1, w], X1[:, cols], start=False, stop=False)
                        last = mm(o, WL[r][0:64, 1, w], X1[0:64, cols], start=False, stop=True)
                    last.then_inc(S["g_ready"], 1)

                def down(u):
                    s, ch, j = u // (2 * m.chunks), u // 2 % m.chunks, u % 2
                    n, U = MS0[m.name] + s, u0 + u
                    pe.wait_ge(S["ah_lo"], U + 1)
                    if ch == 0 and j == 0:
                        pe.wait_ge(S["w_lo"], 2 * n + 2)
                    if u == 0:
                        pe.wait_ge(S["r_shift"], ROUTER[m.name][0] + 1)
                    if m.first(s, ch):
                        d = MD0[m.name] + 2 * owner_index(m, s, ch) - 2 + j
                        if d >= 0:
                            pe.wait_ge(S["drained"], d + 1)
                    for tau in range(TAU):
                        g = TAU * j + tau
                        w = slice(ch * C, (ch + 1) * C)
                        first = m.first(s, ch) and tau != 1
                        hi, lo = AH[U % 3][:, tau:HN:TAU], AL[U % 3][:, tau:HN:TAU]
                        mm(YB(g), hi, DH[n % RING][:, w], start=first, stop=False, skip_group_check=True)
                        mm(YB(g), hi, DL[n % RING][:, w], start=False, stop=False, skip_group_check=True)
                        last = mm(YB(g), lo, DH[n % RING][:, w], start=False, stop=m.last(s, ch), skip_group_check=True)
                    last.then_inc(S["w3_done"], 1)

                turn(stage, 0, True)
                for u in range(m.units + 2):
                    if u == 1:
                        turn(stage, 1, True)
                        router(*ROUTER[m.name], stage, 0)
                    if u < m.units:
                        hidden(u)
                    if u == 1:
                        router(*ROUTER[m.name], stage, 1)
                    if u >= 2:
                        down(u - 2)

            def attention(a, stage):
                u0 = UNIT0[a.name]
                W, P2 = wqkv[a.name], wp[a.name]
                def gate_logits():
                    wait_xv(a, 1)
                    for i in range(HB):
                        for c in range(NC_):
                            last = mm(PS[:, 0, i * GRP:(i + 1) * GRP], XV[0:CB[c], c, 2 * i * VW:2 * (i + 1) * VW],
                                      wr[1][0:CB[c], c, :], start=(c == 0), stop=(c == NC_ - 1))
                    last.then_inc(S["logits"], 1)

                def token_major(u):
                    g, j = u // 2, u % 2
                    if u >= 1:
                        if a.qk_norm:
                            pe.wait_ge(S["tm_taken"], u)
                        else:
                            pe.wait_ge(S["tm_done"], TM0[a.name] + u)
                    if g == 0:
                        wait_xt(stage, j)
                    for tau in range(TAU):
                        for c in range(NC_):
                            last = mm(PSF[0:TP, 1024 + tau * 2 * a.fq:1024 + (tau + 1) * 2 * a.fq],
                                      tile(XT[0:CB[c], c, 0:B * N], j, tau),
                                      W[0:CB[c], c, g * 2 * a.fq:(g + 1) * 2 * a.fq],
                                      start=(c == 0), stop=(c == NC_ - 1))
                    last.then_inc(S["tm_ready"], 1)

                def qk(u):
                    g, j = u // 2, u % 2
                    U = u0 + u
                    if a.tm:
                        pe.wait_ge(S["tm_done"], TM0[a.name] + u + 1)
                    if a.gated and u == 0:
                        pe.wait_ge(S["r_shift"], 2)
                    if u >= 1:
                        pe.wait_ge(S["q_sb"], U)
                        pe.wait_ge(S["k_sb"], U)
                        if a.paired:
                            pe.wait_ge(S["q1_sb"], u)
                    for k in range(2):
                        if a.paired:
                            for r in range(2):
                                for c in range(NC_):
                                    off = (2 * g + k) * a.fq
                                    last = mm(PS[VW * r:VW * r + a.fq, k, 0:HN // 2].rearrange("f (b n) -> f b n", n=N),
                                              W[0:CB[c], c, off:off + a.fq], xv_half(c, j, CB[c])[:, r:HB:2, :],
                                              start=(c == 0), stop=(c == NC_ - 1))
                        elif a.tm:
                            for tau in range(TAU):
                                last = tr(PS[0:a.fq, k, tau * TP:(tau + 1) * TP],
                                          TX[u % 2][:, (2 * tau + k) * a.fq:(2 * tau + k + 1) * a.fq],
                                          cst[0:TP, 0:TP])
                        else:
                            for c in range(NC_):
                                off = (2 * g + k) * a.fq
                                last = mm(PS[0:a.fq, k, 0:HN].rearrange("f (b n) -> f b n", b=HB), W[0:CB[c], c, off:off + a.fq],
                                          xv_half(c, j, CB[c]), start=(c == 0), stop=(c == NC_ - 1))
                    last.then_inc(S["qk_ready"], 1)

                def values(j, p):
                    pair, part = 4 * j + p // a.vparts, p % a.vparts
                    wait_xv(a, j)
                    if p >= 2:
                        pe.wait_ge(S["v_sb"], V0[a.name] + j * a.vpieces + p - 1)
                    for c in range(NC_):
                        last = mm(PS[:, 4 + 2 * j + p % 2, 0:384], XV[0:CB[c], c, 2 * pair * VW:2 * (pair + 1) * VW],
                                  W[0:CB[c], c, a.v0 + 384 * part:a.v0 + 384 * (part + 1)],
                                  start=(c == 0), stop=(c == NC_ - 1))
                    last.then_inc(S["v_ready"], 1)

                def scores(u):
                    U = u0 + u
                    pe.wait_ge(S["q_sb"], U + 1)
                    pe.wait_ge(S["k_sb"], U + 1)
                    if a.paired:
                        pe.wait_ge(S["q1_sb"], u + 1)
                    if u == 0:
                        pe.wait_ge(S["v_sb"], V0[a.name] + a.vpieces)
                    if u >= 1:
                        pe.wait_ge(S["s_taken"], U)
                    for i in range(HB // 2 if a.paired else 0):
                        last = mm(PS[0:a.rows, 5, 2 * i * N:2 * (i + 1) * N], QB[u % 2][0:VW + a.fq, i, 0:a.rows],
                                  KS[u % 2][0:VW + a.fq, 2 * i * N:2 * (i + 1) * N], start=True, stop=True)
                    for b in range(0 if a.paired else HB):
                        last = mm(PS[0:a.rows, 5, b * N:(b + 1) * N], QB[u % 2][0:a.fq, b, 0:a.rows],
                                  KS[u % 2][0:a.fq, b * N:(b + 1) * N], start=True, stop=True)
                    last.then_inc(S["s_ready"], 1)

                def turn_probs(u):
                    U = u0 + u
                    pe.wait_ge(S["p_sb"], U + 1)
                    if u >= 1:
                        pe.wait_ge(S["pt_sb"], U)
                    for i in range(HB // 2):
                        last = tr(PS[:, 4, i * 128:i * 128 + a.rows], PN[u % 2][0:a.rows, 2 * i:2 * i + 2, :],
                                  cst[0:a.rows, 0:a.rows])
                    last.then_inc(S["pt_ready"], 1)

                def mix(u):
                    U = u0 + u
                    pe.wait_ge(S["pt_sb"], U + 1)
                    if u == 0:
                        pe.wait_ge(S["v_sb"], V0[a.name] + 2 * a.vpieces)
                    if u >= 1:
                        pe.wait_ge(S["o_sb"], U)
                    for b in range(HB):
                        i, r = b // 2, VW * (b % 2)
                        for h in range(a.hg):
                            last = mm(OB[a.slot * h:a.slot * (h + 1), b % 2, i * N:(i + 1) * N],
                                      VS[r:r + N, 4 * (u % 2) + i, (u // 2) * a.fv + h * a.slot:(u // 2) * a.fv + (h + 1) * a.slot],
                                      PT[u % 2][r:r + N, i * 128 + h * a.stride:i * 128 + h * a.stride + N],
                                      start=True, stop=True)
                    last.then_inc(S["o_ready"], 1)

                def output(tiles, groups):
                    for t6 in tiles:
                        for g in groups:
                            last = mm(PB(t6), tile(OT[0:a.fv, g * B * N:(g + 1) * B * N], t6 // TAU, t6 % TAU), P2[:, g, :],
                                      start=(g == 0 and t6 % TAU != 1), stop=(g == a.ng - 1), skip_group_check=True)
                    return last

                lag = 1 if a.tm else 0
                turn(stage, 0)
                pe.wait_ge(in_att[a.name], 48)
                pe.wait_ge(S["in_const"], 16 * (len(consts) - FIRST))
                if a.gated:
                    pe.wait_ge(S["centred"], 1)
                for i in range(a.units + lag + 4):
                    if a.tm and i < a.units:
                        token_major(i)
                    if i == 0:
                        for p in range(a.vpieces):
                            if p == 2:
                                turn(stage, 1)
                            if a.gated and p == 5:
                                gate_logits()
                            values(0, p)
                    for p in pieces(a, i):
                        values(1, p)
                    if 0 <= i - lag < a.units:
                        qk(i - lag)
                    if 0 <= i - lag - 1 < a.units:
                        scores(i - lag - 1)
                    if 0 <= i - lag - 3 < a.units:
                        turn_probs(i - lag - 3)
                    late = i - lag - a.units
                    if 0 <= late < 3:
                        pe.wait_ge(S["o_sb"], u0 + a.units - 4)
                        output(range(2 * late, 2 * late + 2), range(a.ng - 2))
                    if late == 3:
                        pe.wait_ge(S["o_sb"], u0 + a.units - 1)
                        output(range(TAU), range(a.ng - 2, a.ng)).then_inc(S["y_ready"], 1)
                    if 0 <= i - lag - 4 < a.units:
                        mix(i - lag - 4)
                pe.wait_ge(S["o_sb"], u0 + a.units)
                output(range(TAU, NG), range(a.ng - 2, a.ng)).then_inc(S["y_ready"], 1)

            def grid_attention(stage):
                turn(stage, 0)
                pe.wait_ge(in_att["grid"], 48)
                for i in range(NG):
                    j, ks = i // TAU, i % TAU
                    if i == 1:
                        turn(stage, 1)
                    if ks == 0:
                        wait_xt(stage, j)
                    if i >= 2:
                        pe.wait_ge(S["grid_sb"], i - 1)
                    for n in range(2):
                        for c in range(NC_):
                            last = mm(PS[0:TP, 2 * (i % 2) + n, 0:288], XT[0:CR[c], c, i * TP:(i + 1) * TP], wg[0:CR[c], c, 288 * n:288 * (n + 1)],
                                      start=(c == 0), stop=(c == NC_ - 1))
                    last.then_inc(S["grid_ready"], 1)
                pe.wait_ge(S["grid_sb"], NG)
                for j in range(2):
                    pe.wait_ge(S["grid_o"], j + 1)
                    for g in range(TAU * j, TAU * (j + 1)):
                        if g >= 2:
                            pe.wait_ge(S["grid_osb"], g - 1)
                        for nd in range(3):
                            o = 4 * C * j + nd * C + 64 * (g % TAU)
                            last = tr(PS[0:64, 4 + g % 2, nd * TP:(nd + 1) * TP], GO[:, o:o + 64], cst[0:TP, 0:TP])
                        last.then_inc(S["grid_turned"], 1)
                    for g in range(TAU * j, TAU * (j + 1)):
                        pe.wait_ge(S["grid_osb"], g + 1)
                        for nd in range(3):
                            last = mm(PB(g), GT[:, (3 * g + nd) * TP:(3 * g + nd + 1) * TP], wgp[:, nd, :],
                                      start=(nd == 0), stop=(nd == 2))
                    last.then_inc(S["y_ready"], 1)

            for k in range(TOKF):
                pe.wait_ge(in_patch[k], 32)
                for g in range(NG):
                    last = mm(PB(g), tile(BIG[:, k * B * N:(k + 1) * B * N], g // TAU, g % TAU), WTOK[:, k, :],
                              start=(k == 0 and g % TAU != 1), stop=(k == TOKF - 1), skip_group_check=True)
                    if k == TOKF - 1 and g % TAU == TAU - 1:
                        last.then_inc(S["patch_summed"], 1)
            pe.wait_ge(S["in_first"], 16 * FIRST)
            for i, (kind, arg) in enumerate(STAGES):
                if kind == "moe":
                    moe(arg, i)
                elif kind == "attn":
                    attention(arg, i)
                else:
                    grid_attention(i)

        @block.scalar
        def _(act):
            activation = nc.scalar.activation

            def evac_xt(k, kind, a, j):
                def copy(o, i):
                    if kind == "attn" and a.double_ln:
                        return activation(o, i, ACT.Identity, bias=gb[:, 2:3], scale=gb[:, 0:1])
                    return activation(o, i, ACT.Copy)

                act.wait_ge(S["ln_turned"], 2 * k + j + 1)
                if kind != "attn" or a.tm:
                    xt_copy(copy, 0, j, kind == "grid").then_inc(S["xt0_ready"], 1)
                if kind == "attn":
                    copy(xv_half(0, j, 128).rearrange("k b (m t) -> k t b m", t=TAU),
                         PS[:, 4 + 2 * j, 0:HN].rearrange("k (t b m) -> k t b m", t=TAU, b=HB)).then_inc(S["xv0_ready"], 1)
                if kind == "moe":
                    cols = slice(HN * j, HN * (j + 1))
                    copy(by_token(X1T[64:128, cols]), turned(j, 1, 64, 128)).then_inc(S["x1_high"], 1)
                    copy(by_token(XH[:, cols]), turned(j, 0, 0, 128))
                    act.wait_ge(S["x1_low"], 2 * MOES.index(a) + j + 1)
                    copy(by_token(X1[0:64, cols]), turned(j, 1, 0, 64)).then_inc(S["x_high"], 1)
                    xt_copy(copy, 1, j, False).then_inc(S["xt1_ready"], 1)

            def split_high(m, s, part):
                n = MS0[m.name] + s
                r = n % RING
                if part == 0:
                    act.wait_ge(wslot[r], 64 * (n // RING + 1))
                    if s >= RING:
                        act.wait_ge(S["w3_done"], units_before(n - RING + 1))
                if part < 2:
                    o, i = WH[r][:, part, 0:m.width], RG[r][:, part, 0:m.width]
                else:
                    o, i = DH[r][:, 0:m.chunks * C], RD[r][:, 0:m.chunks * C]
                activation(o, i, ACT.Copy).then_inc(S["w_hi"], 1)

            def moe(m):
                for u in range(m.units):
                    U = MU0[m.name] + u
                    act.wait_ge(S["g_ready"], U + 1)
                    if m.up:
                        if SG0[m.name] + u >= 2:
                            act.wait_ge(S["a_ready"], U - 1)
                        activation(SG[u % 2][:, :], PS[:, u % 2, 0:HN], m.act).then_inc(S["sg_ready"], 1)
                    else:
                        act.wait_ge(S["ah_lo"], U - 1)
                        activation(AF[U % 2][:, :], PS[:, u % 2, 0:HN], m.act)
                        act.wait_ge(S["w3_done"], U - 2)
                        activation(AH[U % 3][:, :], PS[:, u % 2, 0:HN], m.act).then_inc(S["a_ready"], 1)
                    if u == 1:
                        router_exp(ROUTER[m.name][0], NG * m.experts, TP)
                    s = u // (2 * m.chunks)
                    part = u % (2 * m.chunks) - 2
                    if 0 <= part < 3 and s + 1 < m.slots:
                        split_high(m, s + 1, part)

            def router_exp(i, w, rows):
                act.wait_ge(S["r_shift"], i + 1)
                activation(rl[0:rows, 1, 0:w], rl[0:rows, 0, 0:w], ACT.Exp).then_inc(S["r_exp"], 1)

            def attention(a, stage):
                u0 = UNIT0[a.name]

                def keys(u):
                    U = u0 + u
                    act.wait_ge(S["qk_ready"], U + 1)
                    if U >= 2:
                        act.wait_ge(S["s_ready"], U - 1)
                    if a.tm:
                        o = KS[u % 2][0:a.fq, :].rearrange("f (p t) -> f t p", t=TAU)
                        i = PS[0:a.fq, 1, 0:HN].rearrange("f (t p) -> f t p", t=TAU)
                    else:
                        o, i = KS[u % 2][0:a.fq, :], PS[0:a.fq, 1, 0:HN]
                    if a.paired:
                        if u == 0:
                            act.wait_ge(S["pads"], PADDED.index(a) + 1)
                        for r in range(2):
                            rows = slice(VW * r, VW * r + a.fq)
                            last = activation(KS[u % 2][rows, :].rearrange("f (i r n) -> f i r n", r=2, n=N)[:, :, r],
                                              PS[rows, 1, 0:HN // 2].rearrange("f (i n) -> f i n", n=N), ACT.Copy)
                        last.then_inc(S["k_sb"], 1)
                        for h in range(a.hg):
                            last = activation(QB[u % 2][rows, 0:HB // 2, h * N:(h + 1) * N],
                                              PS[rows, 0, 0:HN // 2].rearrange("f (i n) -> f i n", n=N), ACT.Copy,
                                              scale=mh[rows, h:h + 1])
                        last.then_inc(S["q1_sb"], 1)
                    elif a.qk_norm:
                        activation(o, i, ACT.Identity, bias=qn[:, 3:4], scale=qn[:, 2:3]).then_inc(S["k_sb"], 1)
                    else:
                        activation(o, i, ACT.Copy).then_inc(S["k_sb"], 1)

                def queries(u):
                    U = u0 + u
                    if u == 0:
                        act.wait_ge(S["pads"], PADDED.index(a) + 1)
                    if U >= 2:
                        act.wait_ge(S["s_ready"], U - 1)
                    for h in range(a.hg):
                        o, i = q_views(a, u, h)
                        if a.qk_norm:
                            last = activation(o, i, ACT.Identity, bias=qs[:, 2 * h + 1:2 * h + 2], scale=qs[:, 2 * h:2 * h + 1])
                        else:
                            last = activation(o, i, ACT.Copy, scale=mh[0:a.fq, h:h + 1])
                    last.then_inc(S["q_sb"], 1)

                def vals(j, p):
                    act.wait_ge(S["v_ready"], V0[a.name] + j * a.vpieces + p + 1)
                    o = 384 * (p % a.vparts)
                    activation(VS[:, 4 * j + p // a.vparts, o:o + 384], PS[:, 4 + 2 * j + p % 2, 0:384],
                               ACT.Copy).then_inc(S["v_sb"], 1)

                def exps(u):
                    U = u0 + u
                    act.wait_ge(S["s_taken"], U + 1)
                    e = ES[u % 2][0:a.rows, :]
                    activation(e, e, ACT.Exp).then_inc(S["e_ready"], 1)

                def probs_turned(u):
                    U = u0 + u
                    act.wait_ge(S["pt_ready"], U + 1)
                    if U >= 2:
                        act.wait_ge(S["o_ready"], U - 1)
                    view = lambda x: x.rearrange("p (i r) -> p i r", i=4)[:, :, 0:a.rows]
                    activation(view(PT[u % 2][:, :]), view(PS[:, 4, :]), ACT.Copy).then_inc(S["pt_sb"], 1)

                def outs(u):
                    U = u0 + u
                    act.wait_ge(S["o_ready"], U + 1)
                    o = (u // 2) * B * N + HN * (u % 2)
                    activation(OT[0:a.fv, o:o + HN].rearrange("f (i r n) -> f r i n", i=4, r=2),
                               OB[0:a.fv, :, :].rearrange("f r (i n) -> f r i n", i=4), ACT.Copy).then_inc(S["o_sb"], 1)

                def square(u):
                    n = u + 1
                    act.wait_ge(S["tm_ready"], TM0[a.name] + n)
                    if u >= 1:
                        act.wait_ge(S["tm_sum"], u)
                    activation(T2[:, :], PSF[0:TP, 1024:1024 + TAU * 256], ACT.Square).then_inc(S["tm_square"], 1)
                    act.wait_ge(S["qk_ready"], u0 + u - 1)
                    activation(TX[u % 2][:, :], PSF[0:TP, 1024:1024 + TAU * 256], ACT.Copy).then_inc(S["tm_taken"], 1)

                lag = 1 if a.tm else 0
                for i in range(a.units + lag + 4):
                    if a.qk_norm and i < a.units:
                        square(i)
                    if i == 0:
                        for p in range(a.vpieces):
                            if p == 2:
                                evac_xt(stage, "attn", a, 1)
                            vals(0, p)
                            if a.gated and p == 6:
                                router_exp(1, HB * GRP, 128)
                    for p in pieces(a, i):
                        vals(1, p)
                    if 0 <= i - lag < a.units:
                        keys(i - lag)
                        if a.tm:
                            queries(i - lag)
                    if 0 <= i - lag - 1 < a.units:
                        exps(i - lag - 1)
                    if 0 <= i - lag - 3 < a.units:
                        probs_turned(i - lag - 3)
                    if 0 <= i - lag - 4 < a.units:
                        outs(i - lag - 4)

            def grid_attention():
                for i in range(0, NG):
                    act.wait_ge(S["grid_ready"], i + 1)
                    activation(GQ[:, i * 576:(i + 1) * 576].rearrange("p (n w) -> p n w", n=2),
                               PS[0:TP, 2 * (i % 2):2 * (i % 2) + 2, 0:288], ACT.Copy).then_inc(S["grid_sb"], 1)
                for j in range(2):
                    act.wait_ge(S["grid_s"], j + 1)
                    e = sg1[:, 1, 0:108]
                    activation(e, e, ACT.Exp, scale=0.25).then_inc(S["grid_e"], 1)
                for g in range(NG):
                    act.wait_ge(S["grid_turned"], g + 1)
                    activation(GT[:, 3 * g * TP:3 * (g + 1) * TP], PS[0:64, 4 + g % 2, 0:3 * TP],
                               ACT.Copy).then_inc(S["grid_osb"], 1)

            for n, (dst, src) in enumerate(consts):
                nc.scalar.dma_start(dst, src).then_inc(S["in_first" if n < FIRST else "in_const"], 16)
            y = 0
            for i, (kind, arg) in enumerate(STAGES):
                if kind == "moe":
                    for part in range(3):
                        split_high(arg, 0, part)
                else:
                    y += 1
                evac_xt(i, kind, arg, 0)
                if kind == "attn":
                    act.wait_ge(S["in_const"], 16 * (len(consts) - FIRST))
                    attention(arg, i)
                    continue
                evac_xt(i, kind, arg, 1)
                if kind == "moe":
                    moe(arg)
                else:
                    grid_attention()

        @block.vector
        def _(dve):
            V = nc.vector
            count = [0]

            def link(ins):
                count[0] += 1
                ins.then_inc(S["dve_step"], 1)
                dve.wait_ge(S["dve_step"], count[0])

            def statistics(n, src, j):
                gs = range(TAU * j, TAU * (j + 1))
                for g in gs:
                    last = V.bn_stats(st[:, g, :], src[:, g, 0:C])
                link(last)
                for g in gs:
                    last = V.bn_aggr(mv[:, g, :], st[:, g, :])
                link(last)
                V.tensor_scalar(var[:, TAU * j:TAU * (j + 1)], mv[:, TAU * j:TAU * (j + 1), 1], EPS, None,
                                ALU.add).then_inc(S["ln_stats"], 1)

            def normalised(n, src, j, moe):
                dve.wait_ge(S["ln_rstd"], n + 1)
                for g in range(TAU * j, TAU * (j + 1)):
                    last = V.tensor_scalar(XN[:, g, 0:C], src[:, g, 0:C], mv[:, g, 0:1], rstd[:, g:g + 1],
                                           ALU.subtract, ALU.mult)
                if moe:
                    link(last)
                    gs = slice(TAU * j, TAU * (j + 1))
                    last = V.tensor_copy(XN[:, gs, C:], XN[:, gs, 128:C])
                return last

            def evac_xt(k, kind, a, j):
                def copy(o, i):
                    if kind == "attn" and a.double_ln:
                        return V.tensor_scalar(o, i, gb[0:64, 1:2], gb[0:64, 3:4], ALU.mult, ALU.add)
                    return V.tensor_copy(o, i)

                dve.wait_ge(S["ln_turned"], 2 * k + j + 1)
                xt_copy(copy, 1, j, kind == "grid").then_inc(S["xt1_ready"], 1)
                if kind == "attn":
                    dve.wait_ge(S["xt1_ready"], 2 * k + j + 1)
                    V.tensor_copy(xv_half(1, j, CB[1]), XT[0:CB[1], 1, HN * j:HN * (j + 1)].rearrange("k (b n) -> k b n", b=HB)
                                  ).then_inc(S["xv1_ready"], 1)

            def prepare(k, kind, a, first_pass, prev):
                passes = 2 if kind == "attn" and a.double_ln else 1
                for j in range(2):
                    n = first_pass + passes * j
                    stream(prev, j)
                    if j == 1 and kind == "moe":
                        split_second(MOES.index(a), 0)
                    elif j == 1:
                        evac_xt(k, kind, a, 0)
                    if passes == 2:
                        statistics(n, H, j)
                        link(normalised(n, H, j, False))
                        n += 1
                    src = XN if passes == 2 else H
                    statistics(n, src, j)
                    if j == 1 and kind == "moe":
                        split_first(k, MOES.index(a), 0)
                    normalised(n, src, j, kind == "moe").then_inc(S["ln_normed"], 1)
                    if kind == "moe" and j == 0:
                        split_low1(a, 0)
                if kind == "moe":
                    split_second(MOES.index(a), 1)
                    split_first(k, MOES.index(a), 1)
                else:
                    evac_xt(k, kind, a, 1)

            def split_low1(m, s):
                n = MS0[m.name] + s
                r = n % RING
                dve.wait_ge(S["w_hi"], 3 * n + 2)
                V.tensor_tensor(WL[r][0:64, 1, 0:m.width], RG[r][0:64, 1, 0:m.width],
                                WH[r][0:64, 1, 0:m.width].bitcast(F32), ALU.subtract).then_inc(S["w_lo1"], 1)

            def split_second(m, j):
                cols = slice(HN * j, HN * (j + 1))
                dve.wait_ge(S["x1_high"], 2 * m + j + 1)
                V.tensor_tensor(by_token(X1[64:128, cols]), turned(j, 1, 64, 128), by_token(X1T[64:128, cols].bitcast(F32)),
                                ALU.subtract).then_inc(S["x1_low"], 1)

            def split_first(k, m, j):
                cols = slice(HN * j, HN * (j + 1))
                dve.wait_ge(S["xt0_ready"], XT0_N[k] + j + 1)
                dve.wait_ge(S["x_high"], 2 * m + j + 1)
                V.tensor_tensor(XL[:, cols], XT[:, 0, cols], XH[:, cols].bitcast(F32), ALU.subtract).then_inc(S["x_split"], 1)

            def softmax(rows, w, parts, logits, add=None):
                G = w[0]
                view = lambda k, o, n: rl[0:rows, k, 0:G * w[1]].rearrange("p (g e) -> p g e", g=G)[:, :, o:o + n]
                for n_, (o, n) in enumerate(parts):
                    link(V.tensor_reduce(rs[0:rows, n_, 0:G], logits[:, :, o:o + n], X, ALU.max))
                    last = V.tensor_tensor(view(0, o, n), logits[:, :, o:o + n],
                                           rs[0:rows, n_, 0:G].unsqueeze(2).to_broadcast([rows, G, n]), ALU.subtract)
                return last, view

            def normalise(rows, w, parts, view, r):
                dve.wait_ge(S["r_exp"], r + 1)
                G = w[0]
                for n_, (o, n) in enumerate(parts):
                    link(V.tensor_reduce(rs[0:rows, n_, 0:G], view(1, o, n), X, ALU.add))
                    link(V.reciprocal(rs[0:rows, n_, 0:G], rs[0:rows, n_, 0:G]))
                    link(V.tensor_tensor(view(2, o, n), view(1, o, n),
                                         rs[0:rows, n_, 0:G].unsqueeze(2).to_broadcast([rows, G, n]), ALU.mult))

            def top_mask(dst, sel, rows, G, E, k):
                cube = [rows, G, E, E]
                r1 = R1[0:rows, 0:G * E * E].rearrange("p (g e f) -> p g e f", g=G, e=E)
                r2 = R2[0:rows, 0:G * E * E].rearrange("p (g e f) -> p g e f", g=G, e=E)
                other = sel.unsqueeze(2).to_broadcast(cube)
                own = sel.unsqueeze(3).to_broadcast(cube)
                V.tensor_tensor(r1, other, own, ALU.is_gt)
                link(V.tensor_tensor(r2, other, own, ALU.is_equal))
                link(V.tensor_tensor(r2, r2, tri[0:rows, 0:E, 0:E].unsqueeze(1).to_broadcast(cube), ALU.mult))
                link(V.tensor_tensor(r1, r1, r2, ALU.add))
                link(V.tensor_reduce(dst, r1, X, ALU.add))
                link(V.tensor_scalar(dst, dst, float(k), None, ALU.is_lt))

            def router(m, i):
                r, e = ROUTER[m.name]
                w = (NG, e)
                dve.wait_ge(S["logits"], r + 1)
                logits = PS[0:TP, 5, 0:NG * e].rearrange("p (g e) -> p g e", g=NG)
                last, view = softmax(TP, w, [(0, e)], logits)
                last.then_inc(S["r_shift"], 1)
                normalise(TP, w, [(0, e)], view, r)
                probs = view(2, 0, e)
                mask = view(3, 0, e)
                sel = probs
                if m is M2:
                    sel = view(0, 0, e)
                    link(V.tensor_tensor(sel, probs, ebias[:, :].unsqueeze(1).to_broadcast([TP, NG, e]), ALU.add))
                if m is M3:
                    for g in range(NG):
                        last = V.max(top8[:, g, :], probs[:, g, :])
                    link(last)
                    for g in range(NG):
                        last = V.match_replace(mask[:, g, :], top8[:, g, :], probs[:, g, :], -1.0)
                    link(last)
                    link(V.tensor_scalar(mask, mask, 0.0, None, ALU.is_lt))
                else:
                    top_mask(mask, sel, TP, NG, e, m.topk)
                if m is M0:
                    V.tensor_reduce(maxp[:, :], probs, X, ALU.max)
                    link(V.tensor_copy(comb[0][:, :, :], mask))
                    return
                link(V.tensor_tensor(mask, mask, probs, ALU.mult))
                link(V.tensor_reduce(rs[0:TP, 0, 0:NG], mask, X, ALU.add))
                if m is M2:
                    link(V.tensor_scalar(rs[0:TP, 0, 0:NG], rs[0:TP, 0, 0:NG], 1e-9, None, ALU.add))
                link(V.reciprocal(rs[0:TP, 0, 0:NG], rs[0:TP, 0, 0:NG]))
                link(V.tensor_tensor(comb[i][:, :, 0:e], mask,
                                     rs[0:TP, 0, 0:NG].unsqueeze(2).to_broadcast([TP, NG, e]), ALU.mult))

            def centre(n):
                c, g = n // A1.ng, n % A1.ng
                if n == 0:
                    dve.wait_ge(in_att["l1f"], 48)
                w = wqkv["l1f"][:, c, g * 256:(g + 1) * 256].rearrange("k (h d) -> k h d", d=64)
                w = w[0:CB[c]]
                m = cw[0:CB[c], 4 * n:4 * (n + 1)]
                link(V.tensor_reduce(m, w, X, ALU.add))
                link(V.tensor_scalar(m, m, -1.0 / 64, None, ALU.mult))
                last = V.tensor_tensor(w, w, m.unsqueeze(2).to_broadcast([CB[c], 4, 64]), ALU.add)
                if n == NC_ * A1.ng - 1:
                    last.then_inc(S["centred"], 1)

            def moe(m, i):
                for u in range(m.units):
                    if m is M0 and u >= 8 and u % 4 == 0 and u // 4 - 2 < NC_ * A1.ng:
                        centre(u // 4 - 2)
                    U = MU0[m.name] + u
                    if m.up:
                        dve.wait_ge(S["sg_ready"], SG0[m.name] + u + 1)
                        V.tensor_tensor(AF[U % 2][:, :], SG[u % 2][:, :], PS[:, 2 + u % 2, 0:HN],
                                        ALU.mult).then_inc(S["a_ready"], 1)
                    dve.wait_ge(S["a_ready"], U + 1)
                    if U >= 3:
                        dve.wait_ge(S["w3_done"], U - 2)
                    if m.up:
                        V.tensor_copy(AH[U % 3][:, :], AF[U % 2][:, :]).then_inc(S["ah_hi"], 1)
                        dve.wait_ge(S["ah_hi"], U + 1)
                    V.tensor_tensor(AL[U % 3][:, :], AF[U % 2][:, :], AH[U % 3][:, :].bitcast(F32),
                                    ALU.subtract).then_inc(S["ah_lo"], 1)
                    s = u // (2 * m.chunks)
                    if u % (2 * m.chunks) == 4 and s + 1 < m.slots:
                        split_low1(m, s + 1)
                    if u == 1:
                        router(m, i)
                    if u >= 2:
                        drain(m, i, u - 2)

            def drain(m, i, u):
                s, ch, j = u // (2 * m.chunks), u // 2 % m.chunks, u % 2
                if not m.last(s, ch):
                    return
                e = m.expert(s, ch)
                dve.wait_ge(S["w3_done"], MU0[m.name] + u + 1)
                d = MD0[m.name] + 2 * owner_index(m, s, ch) + j
                if d >= 2 and owner_index(m, s, ch):
                    dve.wait_ge(S["drained"], d - 1)
                for tau in range(TAU):
                    g = TAU * j + tau
                    y = YB(g)
                    into = ACC if m is M0 else H
                    coef = comb[i][:, g, e:e + 1]
                    if m is M0 and e == 0:
                        last = V.tensor_scalar(ACC[:, g, :], y, coef, None, ALU.mult)
                    else:
                        last = V.scalar_tensor_tensor(into[:, g, :], y, coef, into[:, g, :], ALU.mult, ALU.add)
                last.then_inc(S["drained"], 1)

            def stream(prev, j):
                kind, a, y = prev
                gs = slice(TAU * j, TAU * (j + 1))
                if kind == "patch":
                    dve.wait_ge(S["patch_summed"], j + 1)
                    for g in range(TAU * j, TAU * (j + 1)):
                        last = V.tensor_tensor(H[:, g, :], PB(g), bias[:, 0, :], ALU.add)
                    link(last)
                    link(V.tensor_tensor(H[:, gs, :], H[:, gs, :], posb[:, :, :], ALU.add))
                elif kind == "moe":
                    drain(a, MOES.index(a), a.units - 2 + j)
                    dve.wait_ge(S["drained"], MD0[a.name] + 2 * len(set(a.owner)) - 1 + j)
                    if a is M0:
                        link(V.tensor_copy(ACCB[:, gs, :], ACC[:, gs, :]))
                        for g in range(TAU * j, TAU * (j + 1)):
                            last = V.scalar_tensor_tensor(H[:, g, :], ACCB[:, g, :], maxp[:, g:g + 1], H[:, g, :],
                                                          ALU.mult, ALU.add)
                        link(last)
                else:
                    dve.wait_ge(S["y_ready"], 2 * y + j + 1)
                    dve.wait_ge(S["bias_added"], y + 1)
                    g = TAU * j
                    flat = H[:, g:g + 2, :].rearrange("p g f -> p (g f)")
                    V.tensor_tensor(flat, PS[0:TP, 2 * j, 0:2 * C], flat, ALU.add)
                    link(V.tensor_tensor(H[:, g + 2, :], PB(g + 2), H[:, g + 2, :], ALU.add))

            def gates(a):
                dve.wait_ge(S["logits"], 2)
                logits = PS[:, 0, 0:HB * GRP].rearrange("p (g e) -> p g e", g=HB)
                parts = [(0, 10), (10, 2), (12, 2)]
                last, view = softmax(128, (HB, GRP), parts, logits)
                last.then_inc(S["r_shift"], 1)
                normalise(128, (HB, GRP), parts, view, 1)
                p, m10 = view(2, 0, 10), view(3, 0, 10)
                top_mask(m10, p, 128, HB, 10, 2)
                link(V.tensor_tensor(m10, m10, p, ALU.mult))
                tot = rs[:, 0, 0:HB]
                link(V.tensor_reduce(tot, m10, X, ALU.add))
                link(V.tensor_scalar(tot, tot, FEPS, None, ALU.max))
                link(V.reciprocal(tot, tot))
                w0 = view(2, 10, 2)
                link(V.tensor_scalar(w0, w0, 4.0, None, ALU.mult))
                link(V.tensor_tensor(tot, tot, view(2, 10, 2)[:, :, 1], ALU.mult))
                link(V.tensor_tensor(m10, m10, tot.unsqueeze(2).to_broadcast([128, HB, 10]), ALU.mult))
                sh = view(2, 12, 2)
                link(V.tensor_tensor(sh, sh, w0[:, :, 0:1].to_broadcast([128, HB, 2]), ALU.mult))
                for hh in range(2):
                    V.tensor_copy(GP[:, hh, 0, :], sh[:, :, hh])
                    last = V.tensor_copy(GP[:, hh, 1:6, :].rearrange("p g b -> p b g"), m10[:, :, hh:10:2])
                last.then_inc(S["gates_made"], 1)

            def attention(a):
                u0 = UNIT0[a.name]

                def token_major(u):
                    n = TM0[a.name] + u
                    f2 = TAU * 2 * a.fq
                    src = PSF[0:TP, 1024:1024 + f2]
                    tx, t2 = TX[u % 2][:, 0:f2], T2[:, 0:f2]
                    if a.rope:
                        if u >= 2:
                            dve.wait_ge(S["qk_ready"], u0 + u - 1)
                        dve.wait_ge(S["tm_ready"], n + 1)
                        co = rope[:, 0, :, :].rearrange("p t f -> p (t f)")
                        si = rope[:, 1, :, :].rearrange("p t f -> p (t f)")
                        V.tensor_tensor(tx, src, co, ALU.mult)
                        V.tensor_tensor(t2[:, 0:f2:2], src[:, 1:f2:2], si[:, 0:f2:2], ALU.mult)
                        link(V.tensor_tensor(t2[:, 1:f2:2], src[:, 0:f2:2], si[:, 1:f2:2], ALU.mult))
                        V.tensor_tensor(tx, tx, t2, ALU.add).then_inc(S["tm_done"], 1)
                    else:
                        dve.wait_ge(S["tm_rstd"], u + 1)
                        dve.wait_ge(S["tm_taken"], u + 1)
                        V.tensor_tensor(tx.rearrange("p (h d) -> p h d", d=64), tx.rearrange("p (h d) -> p h d", d=64),
                                        ssq[:, 2, :].unsqueeze(2).to_broadcast([TP, 12, 64]),
                                        ALU.mult).then_inc(S["tm_done"], 1)

                def mean_square(u):
                    dve.wait_ge(S["tm_square"], u + 1)
                    link(V.tensor_reduce(ssq[:, 0, :], T2[:, :].rearrange("p (h d) -> p h d", d=64), X, ALU.add))
                    V.tensor_scalar(ssq[:, 1, :], ssq[:, 0, :], 1.0 / 64, EPS, ALU.mult, ALU.add).then_inc(S["tm_sum"], 1)

                def queries(u):
                    U = u0 + u
                    dve.wait_ge(S["qk_ready"], U + 1)
                    if u == 0 and a in PADDED:
                        dve.wait_ge(S["pads"], PADDED.index(a) + 1)
                    if U >= 2:
                        dve.wait_ge(S["s_ready"], U - 1)
                    for h in range(a.hg if a.paired else 0):
                        last = V.tensor_scalar(QB[u % 2][0:a.fq, 0:HB // 2, h * N:(h + 1) * N],
                                               PS[0:a.fq, 0, 0:HN // 2].rearrange("f (i n) -> f i n", n=N),
                                               mh[0:a.fq, h:h + 1], None, ALU.mult)
                    for h in range(0 if a.paired else a.hg):
                        o, i = q_views(a, u, h)
                        last = V.tensor_scalar(o, i, mh[0:a.fq, 3 + h:4 + h], None, ALU.mult)
                    last.then_inc(S["q_sb"], 1)

                def shift(u):
                    U = u0 + u
                    dve.wait_ge(S["s_ready"], U + 1)
                    if U >= 2:
                        dve.wait_ge(S["p_sb"], U - 1)
                    s = PS[0:a.rows, 5, 0:HN].rearrange("p (b k) -> p b k", b=HB)
                    e = ES[u % 2][0:a.rows, :].rearrange("p (b k) -> p b k", b=HB)
                    mx = sm[0:a.rows, 0, :]
                    if a.mask:
                        mk = masks[:, 0 if a.mask == "causal" else 1, :]
                        link(V.tensor_tensor(e, s, mk.unsqueeze(1).to_broadcast([a.rows, HB, N]), ALU.add))
                        s = e
                    link(V.tensor_reduce(mx, s, X, ALU.max))
                    V.tensor_tensor(e, s, mx.unsqueeze(2).to_broadcast([a.rows, HB, N]),
                                    ALU.subtract).then_inc(S["s_taken"], 1)

                def norm(u):
                    U = u0 + u
                    dve.wait_ge(S["e_ready"], U + 1)
                    e = ES[u % 2][0:a.rows, :].rearrange("p (b k) -> p b k", b=HB)
                    tot, inv = sm[0:a.rows, 1, :], sm[0:a.rows, 2, :]
                    link(V.tensor_reduce(tot, e, X, ALU.add))
                    link(V.reciprocal(inv, tot))
                    if a.gated:
                        if u == 0:
                            dve.wait_ge(S["gates_in"], 64)
                        pairs = inv.rearrange("p (i r) -> p r i", r=2)
                        link(V.tensor_tensor(pairs, pairs, GH[:, :, u // 2, 4 * (u % 2):4 * (u % 2 + 1)], ALU.mult))
                    if u == 0 and a in PADDED:
                        dve.wait_ge(S["pads"], PADDED.index(a) + 1)
                    if U >= 2:
                        dve.wait_ge(S["pt_ready"], U - 1)
                    V.tensor_tensor(PN[u % 2][0:a.rows, :, 0:N], e, inv.unsqueeze(2).to_broadcast([a.rows, HB, N]),
                                    ALU.mult).then_inc(S["p_sb"], 1)

                lag = 1 if a.tm else 0
                for i in range(a.units + lag + 4):
                    if a.qk_norm and i < a.units:
                        mean_square(i)
                    if a.rope and i < a.units:
                        token_major(i)
                    if not a.tm and 0 <= i - lag < a.units:
                        queries(i - lag)
                    if 0 <= i - lag - 1 < a.units:
                        shift(i - lag - 1)
                    if a.qk_norm and i < a.units:
                        token_major(i)
                    if a.gated and i == 0:
                        gates(a)
                    if 0 <= i - lag - 2 < a.units:
                        norm(i - lag - 2)

            def grid_attention():
                qkv = GQ.rearrange("p (j k f) -> p j k f", j=2, k=3)
                for j in range(2):
                    dve.wait_ge(S["grid_sb"], 3 * j + 3)
                    prod, q, k = grid_product(j)
                    if j == 0:
                        link(V.tensor_tensor(prod.rearrange("p (q k f) -> p q k f", q=3, k=3), q, k, ALU.mult))
                    else:
                        dve.wait_ge(S["grid_product"], 1)
                    sc = sg1[:, 0, 0:108]
                    link(V.tensor_reduce(sc, prod.rearrange("p (s d) -> p s d", d=16), X, ALU.add))
                    s3 = sc.rearrange("p (q k n) -> p q n k", q=3, k=3)
                    mx = sg1[:, 2, 0:36].rearrange("p (q n) -> p q n", q=3)
                    link(V.tensor_reduce(mx, s3, X, ALU.max))
                    e3 = sg1[:, 1, 0:108].rearrange("p (q k n) -> p q n k", q=3, k=3)
                    V.tensor_tensor(e3, s3, mx.unsqueeze(3).to_broadcast([TP, 3, 12, 3]),
                                    ALU.subtract).then_inc(S["grid_s"], 1)
                    dve.wait_ge(S["grid_e"], j + 1)
                    link(V.tensor_reduce(mx, e3, X, ALU.add))
                    link(V.reciprocal(mx, mx))
                    link(V.tensor_tensor(e3, e3, mx.unsqueeze(3).to_broadcast([TP, 3, 12, 3]), ALU.mult))
                    o = GO[:, 4 * C * j:4 * C * j + 3 * C].rearrange("p (n q d) -> p q n d", n=12, q=3)
                    p4 = sg1[:, 1, 0:108].rearrange("p (q k n) -> p q k n", q=3, k=3)
                    tmp = OT[0:TP, 0:576].rearrange("p (q n d) -> p q n d", q=3, n=12)
                    for ki in range(3):
                        v = qkv[:, j, ki, 2 * C:3 * C].rearrange("p (n d) -> p n d", n=12)
                        w = p4[:, :, ki, :].unsqueeze(3).to_broadcast([TP, 3, 12, 16])
                        vv = v.unsqueeze(1).to_broadcast([TP, 3, 12, 16])
                        link(V.tensor_tensor(o if ki == 0 else tmp, w, vv, ALU.mult))
                        if ki:
                            last = V.tensor_tensor(o, o, tmp, ALU.add)
                            if ki == 1:
                                link(last)
                    last.then_inc(S["grid_o"], 1)
                    dve.wait_ge(S["grid_o"], j + 1)

            V.memset(comb[1][:, :, 8:9], 1.0)
            V.memset(MIX[:, :], 0.0)
            link(V.memset(XT[64:65, 1, :], 1.0))
            dve.wait_ge(S["in_first"], 16 * FIRST)

            y = n = 0
            prev = ("patch", None, 0)
            for i, (kind, arg) in enumerate(STAGES):
                prepare(i, kind, arg, n, prev)
                n += 4 if kind == "attn" and arg.double_ln else 2
                prev = (kind, arg, y)
                if kind == "moe":
                    moe(arg, MOES.index(arg))
                elif kind == "attn":
                    if arg is A0:
                        dve.wait_ge(S["in_const"], 16 * (len(consts) - FIRST))
                        for h in range(2):
                            V.tensor_scalar(qs[:, 2 * h:2 * h + 1], qn[:, 0:1], mh[:, 3 + h:4 + h], None, ALU.mult)
                            last = V.tensor_scalar(qs[:, 2 * h + 1:2 * h + 2], qn[:, 1:2], mh[:, 3 + h:4 + h], None, ALU.mult)
                        link(last)
                    attention(arg)
                    y += 1
                else:
                    grid_attention()
                    y += 1
            for j in range(2):
                stream(prev, j)

        @block.gpsimd
        def _(pool):
            G = nc.gpsimd
            count = [0]

            def link(ins):
                count[0] += 1
                ins.then_inc(S["pool_step"], 1)
                pool.wait_ge(S["pool_step"], count[0])

            G.memset(nhalf[:, :], -0.5)
            link(G.memset(tri[:, :, :], 1.0))
            link(G.affine_select(out=tri[:, :, :], in_=tri[:, :, :], compare_op=ALU.is_gt, fill=0.0, base=0,
                                 pattern=[[1, 16], [-1, 16]], channel_multiplier=0))
            def split_low(m, s):
                n = MS0[m.name] + s
                r, w = n % RING, m.width
                pool.wait_ge(S["w_hi"], 3 * n + 1)
                G.tensor_tensor(WL[r][:, 0, 0:w], RG[r][:, 0, 0:w], WH[r][:, 0, 0:w].bitcast(F32),
                                ALU.subtract).then_inc(S["w_lo"], 1)

            def split_low_down(m, s):
                n = MS0[m.name] + s
                r, d = n % RING, m.chunks * C
                pool.wait_ge(S["w_hi"], 3 * n + 3)
                G.tensor_tensor(DL[r][:, 0:d], RD[r][:, 0:d], DH[r][:, 0:d].bitcast(F32),
                                ALU.subtract).then_inc(S["w_lo"], 1)

            def pads(a):
                for r in range(2):
                    last = G.memset(PN[r][:, :, N:], 0.0)
                    if a.paired:
                        G.memset(QB[r][:, :, :], 0.0)
                        last = G.memset(KS[r][:, :], 0.0)
                last.then_inc(S["pads"], 1)

            y = n = 0
            for i, (kind, arg) in enumerate(STAGES):
                double, moe = kind == "attn" and arg.double_ln, kind == "moe"
                if arg is A0 or arg is A1:
                    pads(arg)
                for j in range(2):
                    for second in range(2 if double else 1):
                        pool.wait_ge(S["ln_stats"], n + 1)
                        r = rstd[:, TAU * j:TAU * (j + 1)]
                        G.tensor_tensor(r, var[:, TAU * j:TAU * (j + 1)], nhalf[0:TP, 0:TAU], ALU.pow).then_inc(S["ln_rstd"], 1)
                        n += 1
                    if moe and j == 0:
                        split_low(arg, 0)
                if arg is A3:
                    pads(arg)
                if arg is A0:
                    pool.wait_ge(S["in_const"], 16 * (len(consts) - FIRST))
                if kind != "moe":
                    pool.wait_ge(S["ln_normed"], 2 * i + 2)
                    G.tensor_tensor(H[:, :, :], H[:, :, :], bias[:, 1 + y, :].unsqueeze(1).to_broadcast([TP, NG, C]),
                                    ALU.add).then_inc(S["bias_added"], 1)
                    y += 1
                    if kind == "grid":
                        pool.wait_ge(S["grid_sb"], NG)
                        prod, q, k = grid_product(1)
                        G.tensor_tensor(prod.rearrange("p (q k f) -> p q k f", q=3, k=3), q, k,
                                        ALU.mult).then_inc(S["grid_product"], 1)
                else:
                    for s in range(arg.slots):
                        if s:
                            split_low(arg, s)
                        split_low_down(arg, s)
                if kind == "attn" and arg.qk_norm:
                    for u in range(arg.units):
                        pool.wait_ge(S["tm_sum"], u + 1)
                        G.tensor_tensor(ssq[:, 2, :], ssq[:, 1, :], nhalf[0:TP, 0:12], ALU.pow).then_inc(S["tm_rstd"], 1)


def layouts(a):
    f = np.float32
    z = lambda *shape: np.zeros(shape, f)
    t = {}
    t["patch"] = a["x"].reshape(B, 3, 6, 16, 6, 16).transpose(1, 3, 5, 0, 2, 4).reshape(TOKF, 128, B * N).transpose(1, 0, 2)
    t["wtok"] = a["L0_tok_W"].T.reshape(TOKF, 128, C).transpose(1, 0, 2)

    def chunks(w, b=None):
        o = z(128, NC_, w.shape[1])
        for c in range(NC_):
            o[0:CR[c], c] = w[128 * c:128 * c + CR[c]]
        if b is not None:
            o[CR[1], 1] = b
        return o

    def attn(at, wq, wk, wv, wo, bq, bk, bv):
        parts = []
        for w, b, slot in ((wq, bq, at.dim), (wk, bk, at.dim), (wv, bv, at.slot)):
            w = chunks(w, b).reshape(128, NC_, at.ng, at.hg, at.dim)
            o = z(128, NC_, at.ng, at.hg, slot)
            o[..., 0:at.dim] = w
            parts.append(o.reshape(128, NC_, at.ng, at.hg * slot))
        qk = np.concatenate(parts[0:2], axis=3).reshape(128, NC_, at.v0)
        w = np.concatenate([qk, parts[2].reshape(128, NC_, at.ng * at.fv)], axis=2)
        for c in range(NC_):
            t[f"wqkv_{at.name}_{c}"] = w[0:CB[c], c]
        o = z(at.ng, at.hg, at.slot, C)
        o[:, :, 0:at.dim] = wo.reshape(at.ng, at.hg, at.dim, C)
        t["wp_" + at.name] = o.reshape(at.ng, at.fv, C).transpose(1, 0, 2)

    def thirds(w):
        n = w.shape[-1] // 3
        return w[..., 0:n], w[..., n:2 * n], w[..., 2 * n:]

    q, k, v = thirds(a["L0_attn_W_attn"])
    bq, bk, bv = thirds(a["L0_attn_b_attn"])
    attn(A0, q, k, v, a["L0_attn_W_proj"], bq, bk, bv)
    q, k, v = thirds(a["L1_ffn_qkv_w"])
    bq, bk, bv = thirds(a["L1_ffn_qkv_b"])
    attn(A1, q, k, v, a["L1_ffn_proj_w"], bq, bk, bv)
    q, k, v = thirds(a["L2_attn_w_qkv"])
    attn(A2, q, k, v, a["L2_attn_w_out"], None, None, None)
    attn(A3, a["L3_attn_Wq"], a["L3_attn_Wk"], a["L3_attn_Wv"], a["L3_attn_Wo"],
         a["L3_attn_bq"], a["L3_attn_bk"], a["L3_attn_bv"])
    t["wg_0"], t["wg_1"] = a["L1_attn_qkv_w"].T[0:128], a["L1_attn_qkv_w"].T[128:]
    t["wgp"] = a["L1_attn_proj_w"].T.reshape(3, 64, C).transpose(1, 0, 2)

    def moe(m, gate, up, down):
        t["gu_" + m.name] = np.concatenate([w for w in (gate, up) if w is not None], axis=2)
        t["wd_" + m.name] = down.reshape(m.slots, m.chunks, 128, C).transpose(0, 2, 1, 3)

    moe(M0, a["L0_ffn_w1"], a["L0_ffn_w2"], a["L0_ffn_w3"])
    cat = lambda w, s: np.concatenate([w, s[None]]).transpose(0, 2, 1)
    moe(M2, cat(a["L2_ffn_Wg"], a["L2_ffn_sg"]), cat(a["L2_ffn_Wu"], a["L2_ffn_su"]), cat(a["L2_ffn_Wd"], a["L2_ffn_sd"]))
    moe(M3, a["L3_ffn_w1"].reshape(C, M3.slots, 512).transpose(1, 0, 2), None,
        a["L3_ffn_w2"].reshape(M3.slots, 512, C))

    t["wr0"] = chunks(a["L0_ffn_router_w"], a["L0_ffn_router_b"])
    t["wr1"] = chunks(np.concatenate([a["L1_ffn_wg_w"], a["L1_ffn_wg0_w"], a["L1_ffn_wg1_w"]], axis=1))
    t["wr2"] = chunks(a["L2_ffn_w_router"].T)
    t["wr3"] = chunks(a["L3_ffn_router_w"].T)
    t["bias0"] = np.broadcast_to(a["L0_tok_b"], (TP, C))
    t["bias"] = np.broadcast_to(np.stack([a[n] for n in (
        "L0_attn_b_proj", "L1_attn_proj_b", "L1_ffn_proj_b", "L2_attn_b_out", "L3_attn_bo")]), (TP, 5, C))
    t["posb"] = np.broadcast_to(a["L0_tok_pos"].reshape(1, NB, TAU, C), (HB, NB, TAU, C)).reshape(TP, TAU, C)
    t["gb"] = np.concatenate([chunks(a[n][:, None])[:, :, 0] for n in ("L2_attn_gamma", "L2_attn_beta")], axis=1)
    t["qn"] = np.stack([np.concatenate([a["L1_ffn_" + n]] * 2) for n in
                        ("q_norm_w", "q_norm_b", "k_norm_w", "k_norm_b")], axis=1)
    t["ebias"] = np.broadcast_to(a["L2_ffn_expert_bias"], (TP, 8))

    t["ident"] = np.eye(128, dtype=f)
    mh = z(128, 6)
    for h in range(3):
        for r in (0, VW):
            mh[r + 16 * h:r + 16 * (h + 1), h] = 16 ** -0.5
    for h in range(2):
        mh[64 * h:64 * (h + 1), 3 + h] = 64 ** -0.5
    t["mh"] = mh
    inv = (1.0 / 10000.0 ** (np.arange(0, 16, 2, dtype=f) / f(16))).astype(f)
    ang = (np.arange(N, dtype=f)[:, None] * inv[None]).astype(f)
    cos, sin = np.repeat(np.cos(ang), 2, axis=1).astype(f), np.repeat(np.sin(ang), 2, axis=1).astype(f)
    sin[:, 0::2] *= -1
    tok = (TAU * (np.arange(TP) % NB))[:, None] + np.arange(TAU)[None]
    t["rope"] = np.stack([np.tile(w[tok], (1, 1, 6)) for w in (cos, sin)], axis=1)
    i, j = np.arange(N)[:, None], np.arange(N)[None]
    causal = np.where(j <= i, 0, -1e30).astype(f)
    band = np.where(abs(i - j) <= 32, 0, -1e9).astype(f)
    t["masks"] = np.stack([np.tile(w, (3, 1)) for w in (causal, band)], axis=1)
    return {n: np.ascontiguousarray(w) for n, w in t.items()}


def kernel(**inputs):
    import concourse.bacc as _bacc
    from concourse.bass_utils import run_bass_kernel_spmd as _run

    nc = _bacc.Bacc("TRN2", target_bir_lowering=False, num_devices=1)
    arrays, aps = {}, {}
    for name, w in layouts({n: np.asarray(v) for n, v in inputs.items()}).items():
        arrays[f"in_{name}_dram"] = w
        aps[name] = nc.dram_tensor(f"in_{name}_dram", w.shape, mybir.dt.from_np(w.dtype), kind="ExternalInput").ap()
    out = nc.dram_tensor("out_0_dram", (B, N, C), F32, kind="ExternalOutput").ap()
    bass_vit_tower(nc, aps, out)
    r = _run(nc, [arrays], core_ids=[0])
    return r.results[0]["out_0_dram"]
```
